# Optimizing a Trainium2 kernel written in Bass

```python
import numpy as np
import jax
import jax.numpy as jnp

def _softmax(x, axis=-1):
    return jax.nn.softmax(x, axis=axis)

def _gelu(x):
    return jax.nn.gelu(x, approximate=True)

def _silu(x):
    return jax.nn.silu(x)

def _sigmoid(x):
    return jax.nn.sigmoid(x)

def _layernorm(x, axis=-1, eps=1e-05):
    m = jnp.mean(x, axis=axis, keepdims=True)
    v = jnp.var(x, axis=axis, keepdims=True)
    return (x - m) / jnp.sqrt(v + eps)

def _scatter_add(tgt, idx, src, axis=0):
    return tgt.at[idx].add(src)

def _segment_sum(src, seg, n):
    return jax.ops.segment_sum(src, seg, n)
kernel_name = 'mk_gps_d2_gnn_r32_340c74'

def setup_inputs(seed: int=0):
    np.random.seed(seed)
    _w = jnp.asarray

    def _rec_inputs():
        import jax
        import jax.numpy as jnp
        _gk = jax.random.key(seed)
        x = -0.0002117 + 1 * jax.random.normal(jax.random.fold_in(_gk, 1), (3125, 256), jnp.float32)
        src = jax.random.randint(jax.random.fold_in(_gk, 2), (50000,), 0, 3125, jnp.int32)
        dst = jax.random.randint(jax.random.fold_in(_gk, 3), (50000,), 0, 3125, jnp.int32)
        _o = jnp.argsort(dst, stable=True)
        src = src[_o]
        dst = dst[_o]
        edge_attr_2 = jax.random.uniform(jax.random.fold_in(_gk, 11), (50000, 2), jnp.float32, 0.0, 1)
        edge_weight = jax.random.uniform(jax.random.fold_in(_gk, 13), (50000,), jnp.float32, 0.0, 1)
        return (x, src, dst, edge_attr_2, edge_weight)
    x, src, dst, edge_attr_2, edge_weight = _rec_inputs()

    def _L0_gnn_setup():
        import jax, jax.numpy as jnp
        import numpy as np
        N = 3125
        E = 100000
        DIN = 256
        DOUT = 256
        key = jax.random.key(seed)
        k1, k2, k3, k4, k5 = jax.random.split(key, 5)
        stdv = 1.0 / np.sqrt(DOUT)
        inputs = {'input': jax.random.normal(k1, (N, DIN), dtype=jnp.float32), 'edge_index': jax.random.randint(k2, (2, E), 0, N, dtype=jnp.int64), 'edge_weight': jax.random.uniform(k3, (E,), dtype=jnp.float32), 'weight': jax.random.uniform(k4, (DIN, DOUT), minval=-stdv, maxval=stdv, dtype=jnp.float32), 'bias': jax.random.uniform(k5, (DOUT,), minval=-stdv, maxval=stdv, dtype=jnp.float32)}
        return inputs
    _L0_gnn_all = _L0_gnn_setup()
    _L0_gnn_in = {k: v for k, v in _L0_gnn_all.items() if k in ('weight', 'bias')}
    del _L0_gnn_all

    def _L0_mix_setup():
        import jax, jax.numpy as jnp
        import numpy as np
        DIM = 256
        HEADS = 4
        DIM_HEAD = 32
        NUM_MEM = 4
        HIDDEN = HEADS * DIM_HEAD
        SCALE = DIM_HEAD ** (-0.5)

        def rmsnorm(x, g):
            n = jnp.linalg.norm(x, axis=-1, keepdims=True)
            return x / jnp.maximum(n, 1e-12) * g * x.shape[-1] ** 0.5
        key = jax.random.key(seed)
        ks = jax.random.split(key, 8)
        B, N = (4, 512)
        return {'x': jax.random.normal(ks[0], (B, N, DIM), jnp.float32), 't': jax.random.normal(ks[1], (B,), jnp.float32), 'w_qkv': jax.random.normal(ks[2], (DIM, 3 * HIDDEN), jnp.float32) * 0.02, 'mem_kv': jax.random.normal(ks[3], (2, HEADS, DIM_HEAD, NUM_MEM), jnp.float32), 'w_out': jax.random.normal(ks[4], (HIDDEN, DIM), jnp.float32) * 0.02, 'b_out': jnp.zeros((DIM,), jnp.float32), 'g_out': jnp.ones((DIM,), jnp.float32), 'g_pre': jnp.ones((DIM,), jnp.float32)}
    _L0_mix_all = _L0_mix_setup()
    _L0_mix_in = {k: v for k, v in _L0_mix_all.items() if k in ('t', 'w_qkv', 'mem_kv', 'w_out', 'b_out', 'g_out', 'g_pre')}
    del _L0_mix_all

    def _L0_ffn_setup():
        import jax, jax.numpy as jnp
        import numpy as np
        B, S, D, F, E, K = (8, 64, 256, 1024, 8, 2)
        key = jax.random.key(seed)
        ks = jax.random.split(key, 10)
        s = 0.02
        return {'x': jax.random.normal(ks[0], (B, S, D), dtype=jnp.float32), 'Wr': jax.random.normal(ks[1], (D, E), dtype=jnp.float32) * s, 'W1s': jax.random.normal(ks[2], (D, F), dtype=jnp.float32) * s, 'b1s': jnp.zeros((F,), dtype=jnp.float32), 'W2s': jax.random.normal(ks[3], (F, D), dtype=jnp.float32) * s, 'b2s': jnp.zeros((D,), dtype=jnp.float32), 'W1p': jax.random.normal(ks[4], (E, D, F), dtype=jnp.float32) * s, 'b1p': jnp.zeros((E, F), dtype=jnp.float32), 'W2p': jax.random.normal(ks[5], (E, F, D), dtype=jnp.float32) * s, 'b2p': jnp.zeros((E, D), dtype=jnp.float32)}
    _L0_ffn_all = _L0_ffn_setup()
    _L0_ffn_in = {k: v for k, v in _L0_ffn_all.items() if k in ('Wr', 'W1s', 'b1s', 'W2s', 'b2s', 'W1p', 'b1p', 'W2p', 'b2p')}
    del _L0_ffn_all

    def _L1_gnn_setup():
        import jax, jax.numpy as jnp
        import numpy as np
        N_NODES = 3125
        N_EDGES = 50000
        IN_FEATS = 256
        OUT_FEATS = 64
        NUM_HEADS = 4
        key = jax.random.key(seed)
        k_h, k_adj, k_dir, k_wf, k_wr, k_af = jax.random.split(key, 6)
        h = jax.random.normal(k_h, (N_NODES, IN_FEATS), dtype=jnp.float32)
        adj = jax.random.randint(k_adj, (2, N_EDGES), 0, N_NODES, dtype=jnp.int64)
        bit = jax.random.randint(k_dir, (N_EDGES,), 0, 2).astype(jnp.float32)
        direction = jnp.stack([bit, 1.0 - bit], axis=1)
        s_w = float(np.sqrt(6.0 / (IN_FEATS + OUT_FEATS)))
        s_a = float(np.sqrt(6.0 / (NUM_HEADS + OUT_FEATS)))
        W_forward = jax.random.uniform(k_wf, (OUT_FEATS, IN_FEATS), jnp.float32, -s_w, s_w)
        W_reverse = jax.random.uniform(k_wr, (OUT_FEATS, IN_FEATS), jnp.float32, -s_w, s_w)
        attn_forward = jax.random.uniform(k_af, (1, NUM_HEADS, OUT_FEATS), jnp.float32, -s_a, s_a)
        return {'h': h, 'adj': adj, 'direction': direction, 'W_forward': W_forward, 'W_reverse': W_reverse, 'attn_forward': attn_forward}
    _L1_gnn_all = _L1_gnn_setup()
    _L1_gnn_in = {k: v for k, v in _L1_gnn_all.items() if k in ('W_forward', 'W_reverse', 'attn_forward')}
    del _L1_gnn_all

    def _L1_mix_setup():
        import jax, jax.numpy as jnp
        import numpy as np
        HEADS = 8
        DIM_HEAD = 64
        EPS = 1e-05

        def _inst_norm_lastdim(t):
            mu = jnp.mean(t, axis=-1, keepdims=True)
            var = jnp.mean(jnp.square(t - mu), axis=-1, keepdims=True)
            return (t - mu) * jax.lax.rsqrt(var + EPS)
        key = jax.random.key(seed)
        k1, k2, k3, k4 = jax.random.split(key, 4)
        b, n, dim = (4, 256, 256)
        inner = HEADS * DIM_HEAD
        x = jax.random.normal(k1, (b, n, dim), dtype=jnp.float32)
        Wqkv = jax.random.normal(k2, (3 * inner, dim), dtype=jnp.float32) * (1.0 / np.sqrt(dim))
        Wout = jax.random.normal(k3, (dim, inner), dtype=jnp.float32) * (1.0 / np.sqrt(inner))
        bout = jax.random.normal(k4, (dim,), dtype=jnp.float32) * 0.01
        return {'x': x, 'Wqkv': Wqkv, 'Wout': Wout, 'bout': bout}
    _L1_mix_all = _L1_mix_setup()
    _L1_mix_in = {k: v for k, v in _L1_mix_all.items() if k in ('Wqkv', 'Wout', 'bout')}
    del _L1_mix_all

    def _L1_ffn_setup():
        import jax, jax.numpy as jnp
        import numpy as np
        B, N, D = (16, 128, 256)
        NUM_EXPERTS, TOP_K, HEADS = (4, 2, 4)
        N_EDGES = 32768
        LN_EPS = 1e-05

        def _layernorm(x, g, b):
            mu = x.mean(-1, keepdims=True)
            var = ((x - mu) ** 2).mean(-1, keepdims=True)
            return (x - mu) * jax.lax.rsqrt(var + LN_EPS) * g + b

        def _forward(x, edge_index, W_gat, att_src, att_dst, b_gat, ln_gamma, ln_beta, W1, b1, W2, b2):
            Bc, Nc, Dc = x.shape
            M = Bc * Nc
            x_flat = x.reshape(M, Dc)
            h = (x_flat @ W_gat).reshape(M, HEADS, NUM_EXPERTS)
            loops = jnp.arange(M, dtype=edge_index.dtype)
            src = jnp.concatenate([edge_index[0], loops])
            dst = jnp.concatenate([edge_index[1], loops])
            a_src = (h * att_src).sum(-1)
            a_dst = (h * att_dst).sum(-1)
            e = jax.nn.leaky_relu(a_src[src] + a_dst[dst], negative_slope=0.2)
            e_max = jax.ops.segment_max(e, dst, num_segments=M)
            ee = jnp.exp(e - e_max[dst])
            denom = jax.ops.segment_sum(ee, dst, num_segments=M)
            alpha = ee / (denom[dst] + 1e-16)
            msg = h[src] * alpha[:, :, None]
            agg = jax.ops.segment_sum(msg, dst, num_segments=M).reshape(M, HEADS * NUM_EXPERTS) + b_gat
            scores = _layernorm(agg, ln_gamma, ln_beta).reshape(M, HEADS, NUM_EXPERTS).mean(1)
            scores = scores.reshape(Bc, Nc, NUM_EXPERTS)
            topk_s, topk_i = jax.lax.top_k(scores, TOP_K)
            w = jax.nn.softmax(topk_s, axis=-1)
            out = jnp.zeros_like(x)
            for ei in range(NUM_EXPERTS):
                g = jnp.where(topk_i == ei, w, 0.0).sum(-1)
                hh = jax.nn.gelu(x @ W1[ei] + b1[ei], approximate=False)
                out = out + g[..., None] * (hh @ W2[ei] + b2[ei])
            return out
        key = jax.random.key(seed)
        ks = jax.random.split(key, 8)
        s = 0.05
        return {'x': jax.random.normal(ks[0], (B, N, D), jnp.float32), 'W_gat': jax.random.normal(ks[1], (D, HEADS * NUM_EXPERTS), jnp.float32) * s, 'att_src': jax.random.normal(ks[2], (HEADS, NUM_EXPERTS), jnp.float32) * s, 'att_dst': jax.random.normal(ks[3], (HEADS, NUM_EXPERTS), jnp.float32) * s, 'b_gat': jnp.zeros((HEADS * NUM_EXPERTS,), jnp.float32), 'ln_gamma': jnp.ones((HEADS * NUM_EXPERTS,), jnp.float32), 'ln_beta': jnp.zeros((HEADS * NUM_EXPERTS,), jnp.float32), 'W1': jax.random.normal(ks[4], (NUM_EXPERTS, D, 2 * D), jnp.float32) * s, 'b1': jnp.zeros((NUM_EXPERTS, 2 * D), jnp.float32), 'W2': jax.random.normal(ks[5], (NUM_EXPERTS, 2 * D, D), jnp.float32) * s, 'b2': jnp.zeros((NUM_EXPERTS, D), jnp.float32), 'edge_index': jax.random.randint(ks[6], (2, N_EDGES), 0, B * N, jnp.int32)}
    _L1_ffn_all = _L1_ffn_setup()
    _L1_ffn_in = {k: v for k, v in _L1_ffn_all.items() if k in ('W_gat', 'att_src', 'att_dst', 'b_gat', 'ln_gamma', 'ln_beta', 'W1', 'b1', 'W2', 'b2', 'edge_index')}
    del _L1_ffn_all
    return {'x': x, 'src': src, 'dst': dst, 'edge_attr_2': edge_attr_2, 'edge_weight': edge_weight, 'L0_gnn_weight': _L0_gnn_in['weight'], 'L0_gnn_bias': _L0_gnn_in['bias'], 'L0_mix_t': _L0_mix_in['t'], 'L0_mix_w_qkv': _L0_mix_in['w_qkv'], 'L0_mix_mem_kv': _L0_mix_in['mem_kv'], 'L0_mix_w_out': _L0_mix_in['w_out'], 'L0_mix_b_out': _L0_mix_in['b_out'], 'L0_mix_g_out': _L0_mix_in['g_out'], 'L0_mix_g_pre': _L0_mix_in['g_pre'], 'L0_ffn_Wr': _L0_ffn_in['Wr'], 'L0_ffn_W1s': _L0_ffn_in['W1s'], 'L0_ffn_b1s': _L0_ffn_in['b1s'], 'L0_ffn_W2s': _L0_ffn_in['W2s'], 'L0_ffn_b2s': _L0_ffn_in['b2s'], 'L0_ffn_W1p': _L0_ffn_in['W1p'], 'L0_ffn_b1p': _L0_ffn_in['b1p'], 'L0_ffn_W2p': _L0_ffn_in['W2p'], 'L0_ffn_b2p': _L0_ffn_in['b2p'], 'L1_gnn_W_forward': _L1_gnn_in['W_forward'], 'L1_gnn_W_reverse': _L1_gnn_in['W_reverse'], 'L1_gnn_attn_forward': _L1_gnn_in['attn_forward'], 'L1_mix_Wqkv': _L1_mix_in['Wqkv'], 'L1_mix_Wout': _L1_mix_in['Wout'], 'L1_mix_bout': _L1_mix_in['bout'], 'L1_ffn_W_gat': _L1_ffn_in['W_gat'], 'L1_ffn_att_src': _L1_ffn_in['att_src'], 'L1_ffn_att_dst': _L1_ffn_in['att_dst'], 'L1_ffn_b_gat': _L1_ffn_in['b_gat'], 'L1_ffn_ln_gamma': _L1_ffn_in['ln_gamma'], 'L1_ffn_ln_beta': _L1_ffn_in['ln_beta'], 'L1_ffn_W1': _L1_ffn_in['W1'], 'L1_ffn_b1': _L1_ffn_in['b1'], 'L1_ffn_W2': _L1_ffn_in['W2'], 'L1_ffn_b2': _L1_ffn_in['b2'], 'L1_ffn_edge_index': _L1_ffn_in['edge_index']}

def reference(x, src, dst, edge_attr_2, edge_weight, L0_gnn_weight, L0_gnn_bias, L0_mix_t, L0_mix_w_qkv, L0_mix_mem_kv, L0_mix_w_out, L0_mix_b_out, L0_mix_g_out, L0_mix_g_pre, L0_ffn_Wr, L0_ffn_W1s, L0_ffn_b1s, L0_ffn_W2s, L0_ffn_b2s, L0_ffn_W1p, L0_ffn_b1p, L0_ffn_W2p, L0_ffn_b2p, L1_gnn_W_forward, L1_gnn_W_reverse, L1_gnn_attn_forward, L1_mix_Wqkv, L1_mix_Wout, L1_mix_bout, L1_ffn_W_gat, L1_ffn_att_src, L1_ffn_att_dst, L1_ffn_b_gat, L1_ffn_ln_gamma, L1_ffn_ln_beta, L1_ffn_W1, L1_ffn_b1, L1_ffn_W2, L1_ffn_b2, L1_ffn_edge_index):
    import jax
    import jax.numpy as jnp

    def _L0_gnn_ref(input, edge_index, edge_weight, weight, bias):
        import jax, jax.numpy as jnp
        import numpy as np
        N = 3125
        E = 100000
        DIN = 256
        DOUT = 256
        support = jnp.matmul(input, weight)
        row, col = (edge_index[0], edge_index[1])
        msgs = support[col] * edge_weight[:, None]
        output = jax.ops.segment_sum(msgs, row, num_segments=input.shape[0])
        return output + bias

    def _L0_mix_ref(x, t, w_qkv, mem_kv, w_out, b_out, g_out, g_pre):
        import jax, jax.numpy as jnp
        import numpy as np
        DIM = 256
        HEADS = 4
        DIM_HEAD = 32
        NUM_MEM = 4
        HIDDEN = HEADS * DIM_HEAD
        SCALE = DIM_HEAD ** (-0.5)

        def rmsnorm(x, g):
            n = jnp.linalg.norm(x, axis=-1, keepdims=True)
            return x / jnp.maximum(n, 1e-12) * g * x.shape[-1] ** 0.5
        b, n, c = x.shape
        xn = rmsnorm(x, g_pre)
        qkv = xn @ w_qkv
        q, k, v = jnp.split(qkv, 3, axis=-1)

        def to_heads(z):
            return z.reshape(b, n, HEADS, DIM_HEAD).transpose(0, 2, 3, 1)
        q, k, v = map(to_heads, (q, k, v))
        mk = jnp.broadcast_to(mem_kv[0], (b, HEADS, DIM_HEAD, NUM_MEM))
        mv = jnp.broadcast_to(mem_kv[1], (b, HEADS, DIM_HEAD, NUM_MEM))
        k = jnp.concatenate([mk, k], axis=-1)
        v = jnp.concatenate([mv, v], axis=-1)
        q = jax.nn.softmax(q, axis=-2) * SCALE
        k = jax.nn.softmax(k, axis=-1)
        context = jnp.einsum('bhdn,bhen->bhde', k, v)
        out = jnp.einsum('bhde,bhdn->bhen', context, q)
        out = out.transpose(0, 3, 1, 2).reshape(b, n, HIDDEN)
        out = rmsnorm(out @ w_out + b_out, g_out)
        return out + x

    def _L0_ffn_ref(x, Wr, W1s, b1s, W2s, b2s, W1p, b1p, W2p, b2p):
        import jax, jax.numpy as jnp
        import numpy as np
        B, S, D, F, E, K = (8, 64, 256, 1024, 8, 2)
        gelu = lambda t: jax.nn.gelu(t, approximate=False)
        shared = gelu(x @ W1s + b1s) @ W2s + b2s
        rw = jax.nn.softmax(x @ Wr, axis=-1)
        topw, topi = jax.lax.top_k(rw, K)
        topw = topw / jnp.sum(topw, axis=-1, keepdims=True)
        mask = jnp.sum(jax.nn.one_hot(topi, E, dtype=topw.dtype) * topw[..., None], axis=-2)
        h = gelu(jnp.einsum('bsd,edf->bsef', x, W1p) + b1p)
        priv = jnp.einsum('bsef,efd->bsed', h, W2p) + b2p
        routed = jnp.einsum('bsed,bse->bsd', priv, mask)
        return shared + routed

    def _L1_gnn_ref(h, adj, direction, W_forward, W_reverse, attn_forward):
        import jax, jax.numpy as jnp
        import numpy as np
        N_NODES = 3125
        N_EDGES = 50000
        IN_FEATS = 256
        OUT_FEATS = 64
        NUM_HEADS = 4
        N = h.shape[0]
        H = attn_forward.shape[1]
        h_fwd = h @ W_forward.T
        h_rev = h @ W_reverse.T
        src, dst = (adj[0], adj[1])
        messages = h_fwd[src] * direction[:, 0:1] + h_rev[src] * direction[:, 1:2]
        scores = jnp.einsum('ef,hf->eh', messages, attn_forward[0])
        scores = jax.nn.leaky_relu(scores, negative_slope=0.2)
        exp_scores = jnp.exp(scores - scores.max(axis=0, keepdims=True))
        sum_exp = jax.ops.segment_sum(exp_scores, dst, num_segments=N)
        norm = exp_scores / (sum_exp[dst] + 1e-10)
        outs = [jax.ops.segment_sum(messages * norm[:, hd:hd + 1], dst, num_segments=N) for hd in range(H)]
        out = jnp.stack(outs, axis=1)
        return out.reshape(N, -1)

    def _L1_mix_ref(x, Wqkv, Wout, bout):
        import jax, jax.numpy as jnp
        import numpy as np
        HEADS = 8
        DIM_HEAD = 64
        EPS = 1e-05

        def _inst_norm_lastdim(t):
            mu = jnp.mean(t, axis=-1, keepdims=True)
            var = jnp.mean(jnp.square(t - mu), axis=-1, keepdims=True)
            return (t - mu) * jax.lax.rsqrt(var + EPS)
        b, n, dim = x.shape
        qkv = jnp.einsum('bnc,fc->bnf', x, Wqkv)
        q, k, v = jnp.split(qkv, 3, axis=-1)

        def to_heads(t):
            return t.reshape(b, n, HEADS, DIM_HEAD).transpose(0, 2, 1, 3)
        q, k, v = (to_heads(q), to_heads(k), to_heads(v))
        k = _inst_norm_lastdim(k)
        v = _inst_norm_lastdim(v)
        dots = jnp.einsum('bhnd,bhne->bhde', k, v)
        out = jnp.einsum('bhnd,bhde->bhne', q, dots) / n
        out = out.transpose(0, 2, 1, 3).reshape(b, n, HEADS * DIM_HEAD)
        return jnp.einsum('bnf,cf->bnc', out, Wout) + bout

    def _L1_ffn_ref(x, W_gat, att_src, att_dst, b_gat, ln_gamma, ln_beta, W1, b1, W2, b2, edge_index):
        import jax, jax.numpy as jnp
        import numpy as np
        B, N, D = (16, 128, 256)
        NUM_EXPERTS, TOP_K, HEADS = (4, 2, 4)
        N_EDGES = 32768
        LN_EPS = 1e-05

        def _layernorm(x, g, b):
            mu = x.mean(-1, keepdims=True)
            var = ((x - mu) ** 2).mean(-1, keepdims=True)
            return (x - mu) * jax.lax.rsqrt(var + LN_EPS) * g + b

        def _forward(x, edge_index, W_gat, att_src, att_dst, b_gat, ln_gamma, ln_beta, W1, b1, W2, b2):
            Bc, Nc, Dc = x.shape
            M = Bc * Nc
            x_flat = x.reshape(M, Dc)
            h = (x_flat @ W_gat).reshape(M, HEADS, NUM_EXPERTS)
            loops = jnp.arange(M, dtype=edge_index.dtype)
            src = jnp.concatenate([edge_index[0], loops])
            dst = jnp.concatenate([edge_index[1], loops])
            a_src = (h * att_src).sum(-1)
            a_dst = (h * att_dst).sum(-1)
            e = jax.nn.leaky_relu(a_src[src] + a_dst[dst], negative_slope=0.2)
            e_max = jax.ops.segment_max(e, dst, num_segments=M)
            ee = jnp.exp(e - e_max[dst])
            denom = jax.ops.segment_sum(ee, dst, num_segments=M)
            alpha = ee / (denom[dst] + 1e-16)
            msg = h[src] * alpha[:, :, None]
            agg = jax.ops.segment_sum(msg, dst, num_segments=M).reshape(M, HEADS * NUM_EXPERTS) + b_gat
            scores = _layernorm(agg, ln_gamma, ln_beta).reshape(M, HEADS, NUM_EXPERTS).mean(1)
            scores = scores.reshape(Bc, Nc, NUM_EXPERTS)
            topk_s, topk_i = jax.lax.top_k(scores, TOP_K)
            w = jax.nn.softmax(topk_s, axis=-1)
            out = jnp.zeros_like(x)
            for ei in range(NUM_EXPERTS):
                g = jnp.where(topk_i == ei, w, 0.0).sum(-1)
                hh = jax.nn.gelu(x @ W1[ei] + b1[ei], approximate=False)
                out = out + g[..., None] * (hh @ W2[ei] + b2[ei])
            return out
        return _forward(x, edge_index, W_gat, att_src, att_dst, b_gat, ln_gamma, ln_beta, W1, b1, W2, b2)
    edge_index = jnp.stack([src, dst])
    xn = _layernorm(x, axis=-1)
    x = x + _L0_gnn_ref(xn, edge_index, edge_weight, L0_gnn_weight, L0_gnn_bias) + _L0_mix_ref(xn[None], L0_mix_t, L0_mix_w_qkv, L0_mix_mem_kv, L0_mix_w_out, L0_mix_b_out, L0_mix_g_out, L0_mix_g_pre)[0]
    x = x + _L0_ffn_ref(_layernorm(x, axis=-1)[None], L0_ffn_Wr, L0_ffn_W1s, L0_ffn_b1s, L0_ffn_W2s, L0_ffn_b2s, L0_ffn_W1p, L0_ffn_b1p, L0_ffn_W2p, L0_ffn_b2p)[0]
    xn = _layernorm(x, axis=-1)
    x = x + _L1_gnn_ref(xn, edge_index, edge_attr_2, L1_gnn_W_forward, L1_gnn_W_reverse, L1_gnn_attn_forward) + _L1_mix_ref(xn[None], L1_mix_Wqkv, L1_mix_Wout, L1_mix_bout)[0]
    x = x + _L1_ffn_ref(_layernorm(x, axis=-1)[None], L1_ffn_W_gat, L1_ffn_att_src, L1_ffn_att_dst, L1_ffn_b_gat, L1_ffn_ln_gamma, L1_ffn_ln_beta, L1_ffn_W1, L1_ffn_b1, L1_ffn_W2, L1_ffn_b2, L1_ffn_edge_index)[0]
    return x

_drawn_inputs = setup_inputs


def setup_inputs(seed=0):
    import zlib

    import numpy as np

    out = dict(_drawn_inputs(seed))
    spreads = {'L0_mix_b_out': (0.0, 0.1),
     'L0_mix_g_out': (1.0, 0.2),
     'L0_mix_g_pre': (1.0, 0.6),
     'L0_ffn_b1s': (0.0, 0.346),
     'L0_ffn_b2s': (0.0, 0.1),
     'L0_ffn_b1p': (0.0, 0.625),
     'L0_ffn_b2p': (0.0, 0.1),
     'L1_ffn_b_gat': (0.0, 0.1),
     'L1_ffn_ln_gamma': (1.0, 0.2),
     'L1_ffn_ln_beta': (0.0, 0.379),
     'L1_ffn_b1': (0.0, 0.423),
     'L1_ffn_b2': (0.0, 0.319)}
    factors = {'L0_mix_w_qkv': 8.0,
     'L0_mix_mem_kv': 8.0,
     'L0_mix_w_out': 8.0,
     'L1_mix_bout': 8.0,
     'L1_ffn_att_src': 8.0,
     'L1_ffn_att_dst': 26.981,
     'L0_gnn_bias': 2.67}
    for name, (base, spread) in spreads.items():
        noise = np.random.default_rng([zlib.crc32(name.encode()), seed]).standard_normal(out[name].shape)
        drawn = base * np.exp(spread * noise) if base else spread * noise
        out[name] = jnp.asarray(drawn.astype(out[name].dtype))
    for name, factor in factors.items():
        out[name] = (out[name] * factor).astype(out[name].dtype)
    return out
```

```python
from contextlib import ExitStack

import concourse.bass as bass
from concourse import mybir

F32 = mybir.dt.float32
I32 = mybir.dt.int32
ALU = mybir.AluOpType
ACT = mybir.ActivationFunctionType
AX = mybir.AxisListType
ds = bass.ds

P = 128
D = 256
N = 3125
T = -(-N // P)
LAST = N - (T - 1) * P
NP = T * P
KD = D // P
GROUP = 256
RING = 8
HALF = RING // 2
BODY_GROUPS = RING * P // GROUP
NEG = -1.0e30


def up(a, b):
    return -(-a // b) * b


def slot_tiles(edges):
    return up((edges + T * (GROUP - 1)) // GROUP * (GROUP // P), RING)


class Chain:

    def __init__(self, eng, sem):
        self.eng, self.sem, self.n = eng, sem, 0

    def then(self, ins, extra=0):
        ins.then_inc(self.sem, 1)
        self.n += 1
        self.eng.wait_ge(self.sem, self.n + extra)


class Core:

    def __init__(self, nc, inputs, out):
        self.nc, self.a, self.out = nc, inputs, out
        self.kept = []
        self.spent = []

    def sb(self, ctx, name, shape, dt=F32):
        return ctx.enter_context(self.nc.sbuf_tensor(name, shape, dt))

    def sem(self, ctx, name):
        if any(ctx is k for k in self.kept):
            return ctx.enter_context(self.nc.semaphore(name))
        self.spent.append(self.nc.alloc_semaphore(name=name))
        return self.spent[-1]

    def clear_spent(self):
        self.nc.all_engine_barrier()
        self.nc.clear_and_free_semaphores(self.spent)
        self.nc.all_engine_barrier()
        self.spent = []


def meet(eng, met, n):
    eng.drain().then_inc(met, 1)
    eng.wait_ge(met, 4 * n)


def everyone_meets(block, met, n):
    block.sync(lambda e: meet(e, met, n))
    block.scalar(lambda e: meet(e, met, n))
    block.vector(lambda e: meet(e, met, n))
    block.tensor(lambda e: meet(e, met, n))




def stage_setup(c, ctx):
    nc = c.nc
    c.bank = ctx.enter_context(nc.psum_tensor("banks", [P, 8, 512], F32))
    c.met = c.sem(ctx, "met")
    c.row_norm = c.sb(ctx, "row_norm", [P, T])
    c.X = c.sb(ctx, "x", [P, T, D])
    c.XT = c.sb(ctx, "xT", [P, T * 260])
    c.xT = c.XT[:, 0:KD * NP].rearrange("p (k n) -> p k n", k=KD)
    c.ident = c.sb(ctx, "ident", [P, P])
    c.before = c.sb(ctx, "before", [P, P])
    c.ones = c.sb(ctx, "ones", [P, 512])
    c.iota_i = c.sb(ctx, "iota_i", [P, 512], I32)
    c.iota = c.sb(ctx, "iota", [P, 512])
    c.part_i = c.sb(ctx, "part_i", [P, 1], I32)
    c.part = c.sb(ctx, "part", [P, 1])
    c.head32 = c.sb(ctx, "head32", [P, P])
    c.head64 = c.sb(ctx, "head64", [P, P])
    load_sem = c.sem(ctx, "setup_loaded")
    const_sem = c.sem(ctx, "constants_made")
    zero_sem = c.sem(ctx, "tail_zeroed")
    with nc.Block() as block:
        @block.sync
        def _(sp):
            sp.dma_start(c.X[:, 0:T - 1, :], c.a["x"][0:(T - 1) * P, :].rearrange("(t p) d -> p t d", p=P))\
              .then_inc(load_sem, 16)
            sp.wait_ge(zero_sem, 1)
            sp.dma_start(c.X[0:LAST, T - 1, :], c.a["x"][(T - 1) * P:N, :]).then_inc(load_sem, 16)
            sp.wait_ge(load_sem, 32)

        @block.vector
        def _(dve):
            dve.memset(c.X[:, T - 1, :], 0.0).then_inc(zero_sem, 1)

        @block.gpsimd
        def _(pool):
            ch = Chain(pool, const_sem)
            ch.then(pool.memset(c.ones[:], 1.0))
            ch.then(pool.memset(c.ident[:], 0.0))
            ch.then(pool.affine_select(out=c.ident[:], in_=c.ident[:], compare_op=ALU.not_equal, fill=1.0,
                                       base=0, pattern=[[-1, P]], channel_multiplier=1))
            ch.then(pool.affine_select(out=c.before[:], in_=c.ones[:, 0:P], compare_op=ALU.is_gt, fill=0.0,
                                       base=0, pattern=[[1, P]], channel_multiplier=-1))
            ch.then(pool.iota(c.iota_i[:], pattern=[[1, 512]], base=0, channel_multiplier=0))
            ch.then(pool.tensor_copy(c.iota[:], c.iota_i[:]))
            ch.then(pool.iota(c.part_i[:], pattern=[[1, 1]], base=0, channel_multiplier=1))
            ch.then(pool.tensor_copy(c.part[:], c.part_i[:]))
            for mask, d in ((c.head32, DH0), (c.head64, FEAT)):
                heads = mask[:].rearrange("p (h d) -> p h d", d=d)
                ch.then(pool.affine_select(out=heads, in_=c.ones[:, 0:P].rearrange("p (h d) -> p h d", d=d),
                                           compare_op=ALU.is_ge, fill=0.0, base=0,
                                           pattern=[[-d, P // d], [0, d]], channel_multiplier=1))
                ch.then(pool.affine_select(out=heads, in_=heads, compare_op=ALU.is_ge, fill=0.0, base=d - 1,
                                           pattern=[[d, P // d], [0, d]], channel_multiplier=-1))




class Edges:

    def __init__(self, c, name, key, val, payload, parts, ctx):
        self.name, self.key, self.val, self.payload = name, key, val, payload
        self.parts, self.slot = parts, None
        self.count = key.shape[0]
        self.per = self.count // parts
        assert self.per * parts == self.count and self.per % RING == 0
        self.tiles = slot_tiles(self.count)
        self.groups = self.tiles * P // GROUP
        self.slots = c.nc.dram_tensor(f"slots_{name}", [P * self.tiles, 4], F32, kind="Internal").ap()
        self.group_tile = c.sb(ctx, f"group_tile_{name}", [1, self.groups], I32)
        self.filled = c.sem(ctx, f"slots_filled_{name}")
        self.ranked = c.sem(ctx, f"ranked_{name}")

    def hold_records(self, c, ctx):
        self.rows = c.sb(ctx, f"slot_row_{self.name}", [P, self.per], I32)
        self.rec = c.sb(ctx, f"rec_{self.name}", [P, self.per, 4])


def rank_stage(c, block, ctx, e, met_n):
    nc, J, n = c.nc, e.per, e.parts
    key = c.sb(ctx, f"key_{e.name}", [P, J], I32)
    val = c.sb(ctx, f"val_{e.name}", [P, J], I32)
    hi_i = c.sb(ctx, f"hi_i_{e.name}", [P, J], I32)
    hi = c.sb(ctx, f"hi_{e.name}", [P, J])
    pay = c.sb(ctx, f"pay_{e.name}", [P, J, 2])
    one_hot = c.sb(ctx, f"in_tile_{e.name}", [P, 2, J])
    seen = c.sb(ctx, f"seen_{e.name}", [P, 2, J])
    pos = c.sb(ctx, f"pos_{e.name}", [P, J])
    posf = c.sb(ctx, f"posf_{e.name}", [P, J])
    cnt = c.sb(ctx, f"cnt_{e.name}", [P, T])
    num_i = c.sb(ctx, f"num_i_{e.name}", [P, T], I32)
    num = c.sb(ctx, f"num_{e.name}", [P, T])
    upto = c.sb(ctx, f"upto_{e.name}", [P, T])
    first = c.sb(ctx, f"first_{e.name}", [P, T])
    gt = c.sb(ctx, f"gt_{e.name}", [1, e.groups])
    fill = c.sb(ctx, f"fill_{e.name}", [P, e.tiles, 4])
    ps = c.bank[:, 0:2, :]
    loaded = c.sem(ctx, f"edges_loaded_{e.name}")
    step = c.sem(ctx, f"rank_step_{e.name}")
    counted = c.sem(ctx, f"counted_{e.name}")
    summed = c.sem(ctx, f"count_summed_{e.name}")
    empty = c.sem(ctx, f"empty_slots_{e.name}")
    met = c.met

    @block.sync
    def _(sp):
        sp.dma_start(key[0:n, :], e.key.rearrange("(p j) -> p j", p=n)).then_inc(loaded, 16)
        sp.dma_start(val[0:n, :], e.val.rearrange("(p j) -> p j", p=n)).then_inc(loaded, 16)
        if e.payload is not None:
            w = e.payload.shape[1] if len(e.payload.shape) == 2 else 1
            src = e.payload.rearrange("(p j) w -> p j w", p=n) if w > 1 else \
                e.payload.rearrange("(p j w) -> p j w", p=n, w=1)
            sp.dma_start(pay[0:n, :, 0:w] if w > 1 else pay[0:n, :, 0:1], src).then_inc(loaded, 16)
        sp.wait_ge(empty, 1)
        sp.dma_start(e.slots.rearrange("(p t) w -> p (t w)", p=P), fill[:].rearrange("p t w -> p (t w)"))\
          .then_inc(e.filled, 16)
        sp.wait_ge(e.filled, 16)
        meet(sp, met, met_n)

    @block.scalar
    def _(act):
        meet(act, met, met_n)

    @block.tensor
    def _(pe):
        pe.wait_ge(counted, 1)
        pe.matmul(ps[:, 0, 0:T], c.ones[0:n, 0:P], cnt[0:n, :], start=True, stop=True)
        pe.matmul(ps[0:n, 1, 0:T], c.before[0:n, 0:n], cnt[0:n, :], start=True, stop=True).then_inc(summed, 1)
        meet(pe, met, met_n)

    @block.vector
    def _(dve):
        ch = Chain(dve, step)
        ch.then(dve.memset(fill[:], 0.0))
        ch.then(dve.memset(fill[:, :, 1:2], -1.0))
        dve.sem_inc(empty, 1)
        payload_dmas = 0 if e.payload is None else 1
        dve.wait_ge(loaded, 32 + 16 * payload_dmas)
        ch.then(dve.tensor_copy(e.rec[0:n, :, 0:1].bitcast(I32).rearrange("p j o -> p (j o)"), val[0:n, :]))
        ch.then(dve.memset(e.rec[0:n, :, 2:4], 0.0))
        if e.payload is not None:
            w = e.payload.shape[1] if len(e.payload.shape) == 2 else 1
            ch.then(dve.tensor_copy(e.rec[0:n, :, 2:2 + w], pay[0:n, :, 0:w]))
        ch.then(dve.tensor_scalar(hi_i[0:n, :], key[0:n, :], 7, None, ALU.logical_shift_right))
        ch.then(dve.tensor_copy(hi[0:n, :], hi_i[0:n, :]))
        ch.then(dve.tensor_scalar(hi_i[0:n, :], key[0:n, :], P - 1, None, ALU.bitwise_and))
        ch.then(dve.tensor_copy(e.rec[0:n, :, 1:2].rearrange("p j o -> p (j o)"), hi_i[0:n, :]))
        with dve.Fori(0, T) as b:
            ch.then(dve.tensor_scalar(one_hot[0:n, 0, :], hi[0:n, :], c.iota[0:n, ds(b, 1)], 0.0, ALU.is_equal,
                                      ALU.add, accum_out=cnt[0:n, ds(b, 1)]), b)
        ch.n += T - 1
        dve.sem_inc(counted, 1)
        dve.wait_ge(summed, 1)
        ch.then(dve.tensor_scalar(num_i[:], ps[:, 0, 0:T], float(GROUP - 1), None, ALU.add))
        ch.then(dve.tensor_scalar(num_i[:], num_i[:], GROUP.bit_length() - 1, None, ALU.logical_shift_right))
        ch.then(dve.tensor_copy(num[:], num_i[:]))
        ch.then(dve.tensor_tensor_scan(upto[:], c.ones[:, 0:T], num[:], 0.0, ALU.mult, ALU.add))
        ch.then(dve.tensor_tensor(first[:], upto[:], num[:], ALU.subtract))
        ch.then(dve.tensor_scalar(first[:], first[:], float(GROUP), -1.0, ALU.mult, ALU.add))
        ch.then(dve.tensor_tensor(first[0:n, :], first[0:n, :], ps[0:n, 1, 0:T], ALU.add))
        ch.then(dve.memset(gt[:], 0.0))
        with dve.Fori(0, T) as b:
            ch.then(dve.scalar_tensor_tensor(gt[:], c.iota[0:1, 0:e.groups], upto[0:1, ds(b, 1)], gt[:],
                                             ALU.is_ge, ALU.add), b)
        ch.n += T - 1
        ch.then(dve.tensor_scalar(e.group_tile[:], gt[:], float(T - 1), None, ALU.min))
        ch.then(dve.memset(pos[0:n, :], 0.0))
        with dve.Fori(0, T) as b:
            ch.then(dve.tensor_scalar(one_hot[0:n, 0, :], hi[0:n, :], c.iota[0:n, ds(b, 1)], None,
                                      ALU.is_equal), 4 * b)
            ch.then(dve.tensor_tensor_scan(seen[0:n, 0, :], c.ones[0:n, 0:J], one_hot[0:n, 0, :],
                                           first[0:n, ds(b, 1)], ALU.mult, ALU.add), 4 * b)
            ch.then(dve.tensor_tensor(seen[0:n, 0, :], seen[0:n, 0, :], one_hot[0:n, 0, :], ALU.mult), 4 * b)
            ch.then(dve.tensor_tensor(pos[0:n, :], pos[0:n, :], seen[0:n, 0, :], ALU.add), 4 * b)
        ch.n += 4 * (T - 1)
        ch.then(dve.tensor_copy(e.rows[0:n, :], pos[0:n, :]))
        ch.then(dve.tensor_scalar(hi_i[0:n, :], e.rows[0:n, :], P - 1, None, ALU.bitwise_and))
        ch.then(dve.tensor_scalar(e.rows[0:n, :], e.rows[0:n, :], 7, None, ALU.logical_shift_right))
        ch.then(dve.tensor_copy(posf[0:n, :], e.rows[0:n, :]))
        ch.then(dve.scalar_tensor_tensor(e.rows[0:n, :], hi_i[0:n, :], float(e.tiles), posf[0:n, :],
                                         ALU.mult, ALU.add))
        dve.sem_inc(e.ranked, 1)
        meet(dve, met, met_n)


def scatter_records(c, block, ctx, e):
    n = e.parts
    idx = c.sb(ctx, f"scatter_idx_{e.name}", [P, RING], I32)
    rec = c.sb(ctx, f"scatter_rec_{e.name}", [P, RING, 4])
    staged = c.sem(ctx, f"record_staged_{e.name}")
    turns = c.sem(ctx, f"scatter_turns_{e.name}")
    moved = [c.sem(ctx, f"records_moved_{e.name}_{k}") for k in range(RING)]

    @block.gpsimd
    def _(pool):
        pool.wait_ge(e.ranked, 1)
        pool.wait_ge(e.filled, 16)
        with pool.Fori(0, e.per // RING) as i:
            for h in range(2):
                for k in range(HALF * h, HALF * h + HALF):
                    pool.wait_ge(moved[k], i * 16)
                at = HALF * h
                pool.tensor_copy(idx[0:n, at:at + HALF], e.rows[0:n, ds(i * RING + at, HALF)]).then_inc(staged, 1)
                pool.tensor_copy(rec[0:n, at:at + HALF, :], e.rec[0:n, ds(i * RING + at, HALF), :])\
                    .then_inc(staged, 1)
                pool.wait_ge(staged, i * 4 + 2 * h + 2)
                pool.sem_inc(turns, 1)
                for k in range(at, at + HALF):
                    pool.indirect_dma_start(e.slots, bass.IndirectOffsetOnAxis(idx[0:n, k:k + 1], 0),
                                            rec[0:n, k, :], None).then_inc(moved[k], 16)
        for k in range(RING):
            pool.wait_ge(moved[k], 16 * (e.per // RING))




def norm_stage(c, block, ctx, name, met_n, first, rows=None):
    X = c.X
    stats = c.sb(ctx, f"stats_{name}", [P, T, 6])
    mv = c.sb(ctx, f"mean_var_{name}", [P, T, 2])
    var = c.sb(ctx, f"var_{name}", [P, T])
    rstd = c.sb(ctx, f"rstd_{name}", [P, T])
    scale = c.sb(ctx, f"scale_{name}", [P, T])
    gain = c.sb(ctx, f"gain_{name}", [P, T])
    shift = c.sb(ctx, f"shift_{name}", [P, T])
    sd = c.sb(ctx, f"sd_{name}", [P, T])
    xn = c.sb(ctx, f"xn_{name}", [P, 1, D])
    xn2 = c.sb(ctx, f"xn2_{name}", [P, 1, D])
    bufs = [xn, xn2]
    ps = [c.bank[:, k, 0:KD * P].rearrange("p (h n) -> p h n", h=KD) for k in range(2)]
    step = c.sem(ctx, f"norm_step_{name}")
    var_ready = c.sem(ctx, f"var_ready_{name}")
    root_ready = c.sem(ctx, f"root_ready_{name}")
    normed = c.sem(ctx, f"normed_{name}")
    turned = c.sem(ctx, f"turned_{name}")
    copied = c.sem(ctx, f"turned_copied_{name}")
    kept = c.sem(ctx, f"residual_kept_{name}")
    met = c.met
    pairs = T // 2

    @block.vector
    def _(dve):
        ch = Chain(dve, step)
        with dve.Fori(0, T) as t:
            dve.bn_stats(stats[:, ds(t, 1), :].rearrange("p a d -> p (a d)"),
                         X[:, ds(t, 1), :].rearrange("p a d -> p (a d)")).then_inc(step, 1)
        ch.n += T
        dve.wait_ge(step, ch.n)
        for t in range(T):
            dve.bn_aggr(mv[:, t, :], stats[:, t, :]).then_inc(step, 1)
        ch.n += T
        dve.wait_ge(step, ch.n)
        ch.then(dve.tensor_scalar(var[:], mv[:, :, 1], 1e-5, None, ALU.add))
        dve.sem_inc(var_ready, 1)
        dve.wait_ge(root_ready, 1)
        ch.then(dve.reciprocal(rstd[:], sd[:]))
        if first:
            ch.then(dve.tensor_tensor(scale[:], rstd[:], rstd[:], ALU.mult))
            ch.then(dve.tensor_tensor(scale[:], scale[:], mv[:, :, 1], ALU.mult))
            ch.then(dve.tensor_scalar(var[:], scale[:], float(D), None, ALU.mult))
            dve.sem_inc(var_ready, 1)
            dve.wait_ge(root_ready, 2)
            ch.then(dve.tensor_scalar(sd[:], sd[:], 1e-12, 1.0 / D ** 0.5, ALU.max, ALU.mult))
            ch.then(dve.tensor_copy(c.row_norm[:], sd[:]))
            ch.then(dve.reciprocal(scale[:], sd[:]))
            ch.then(dve.tensor_tensor(scale[:], scale[:], rstd[:], ALU.mult))
            ch.then(dve.tensor_scalar(gain[:], rstd[:], 1.0, None, ALU.add))
            ch.then(dve.tensor_tensor(shift[:], rstd[:], mv[:, :, 0], ALU.mult))
        else:
            ch.then(dve.tensor_copy(scale[:], rstd[:]))

        def tile(t, k, order):
            dve.wait_ge(turned, order)
            dve.tensor_scalar(bufs[k][:, 0, :], X[:, ds(t, 1), :].rearrange("p a d -> p (a d)"),
                              mv[:, ds(t, 1), 0:1].rearrange("p a b -> p (a b)"), scale[:, ds(t, 1)],
                              ALU.subtract, ALU.mult).then_inc(normed, 1)
            if rows is not None:
                dve.tensor_scalar(rows[:, ds(t, 1), :].rearrange("p a d -> p (a d)"),
                                  X[:, ds(t, 1), :].rearrange("p a d -> p (a d)"),
                                  mv[:, ds(t, 1), 0:1].rearrange("p a b -> p (a b)"), scale[:, ds(t, 1)],
                                  ALU.subtract, ALU.mult)
            if first:
                dve.wait_ge(normed, order)
                dve.tensor_scalar(X[:, ds(t, 1), :].rearrange("p a d -> p (a d)"),
                                  X[:, ds(t, 1), :].rearrange("p a d -> p (a d)"),
                                  gain[:, ds(t, 1)], shift[:, ds(t, 1)], ALU.mult, ALU.subtract)\
                    .then_inc(kept, 1)

        with dve.Fori(0, pairs) as i:
            for k in range(2):
                tile(i * 2 + k, k, i * 2 + k + 1)
        tile(T - 1, 0, T)
        meet(dve, met, met_n)

    @block.tensor
    def _(pe):
        pe.sem_inc(turned, 2)

        def tile(k, order):
            pe.wait_ge(normed, order)
            pe.wait_ge(copied, order)
            for h in range(KD):
                mm = pe.transpose(ps[k][:, h, :], bufs[k][:, 0, h * P:(h + 1) * P], c.ident[:])
            mm.then_inc(turned, 1)

        with pe.Fori(0, pairs) as i:
            for k in range(2):
                tile(k, i * 2 + k + 1)
        tile(0, T)
        meet(pe, met, met_n)

    @block.scalar
    def _(act):
        act.wait_ge(var_ready, 1)
        act.activation(sd[:], var[:], ACT.Sqrt).then_inc(root_ready, 1)
        if first:
            act.wait_ge(var_ready, 2)
            act.activation(sd[:], var[:], ACT.Sqrt).then_inc(root_ready, 1)
        act.sem_inc(copied, 2)

        def tile(t, k, order):
            act.wait_ge(turned, order + 2)
            act.copy(c.xT[:, :, ds(t * P, P)], ps[k][:, :, :]).then_inc(copied, 1)

        with act.Fori(0, pairs) as i:
            for k in range(2):
                tile(i * 2 + k, k, i * 2 + k + 1)
        tile(T - 1, 0, T)
        meet(act, met, met_n)

    @block.sync
    def _(sp):
        meet(sp, met, met_n)




HEADS0, DH0, MEM = 4, 32, 4
HID0 = HEADS0 * DH0


def mix0_stage(c, block, ctx, met_n):
    nc, a = c.nc, c.a
    TM = T + 1
    wg = c.sb(ctx, "w_gnn0", [P, KD, D])
    wq = c.sb(ctx, "w_qkv0", [P, KD, 3 * HID0])
    wo = c.sb(ctx, "w_out0", [P, D])
    g_pre = c.sb(ctx, "g_pre0", [P, KD])
    row = c.sb(ctx, "rows0", [P, 3, D])
    qkv = c.sb(ctx, "qkv0", [P, TM, 3 * HID0])
    sup = c.sb(ctx, "support_ring", [P, 2, D])
    y = c.sb(ctx, "y0", [P, T, D])
    scr = c.sb(ctx, "square0", [P, D])
    k_top = c.sb(ctx, "k_top", [P, HID0])
    k_max = c.sb(ctx, "k_max", [P, 1])
    k_diag = c.sb(ctx, "k_diag", [P, HID0])
    off = c.sb(ctx, "k_off", [P, 2])
    q_max = c.sb(ctx, "q_max", [P, T * HEADS0])
    q_sum = c.sb(ctx, "q_sum", [P, T * HEADS0])
    inv_k = c.sb(ctx, "inv_k", [P, 1])
    ctx_t = c.sb(ctx, "context_t", [P, HID0])
    mat = c.sb(ctx, "context_out", [P, D])
    q_t = c.sb(ctx, "q_t", [P, 2, P])
    ss = c.sb(ctx, "y_square", [P, T])
    rn = c.sb(ctx, "y_norm", [P, T])
    in_w = c.sem(ctx, "mix0_loaded")
    mem_zero = c.sem(ctx, "mem_zeroed")
    step = c.sem(ctx, "mix0_step")
    sup_ready = c.sem(ctx, "support_ready")
    sup_out = c.sem(ctx, "support_evacuated")
    sup_stored = [c.sem(ctx, f"support_stored_{k}") for k in range(2)]
    qkv_ready = c.sem(ctx, "qkv_ready")
    qkv_out = c.sem(ctx, "qkv_evacuated")
    scaled = c.sem(ctx, "g_pre_applied")
    top_ready, top_t, diag_ready, top_bc = (c.sem(ctx, f"k_top_{s}") for s in ("ready", "t", "diag", "bc"))
    k_shift, k_exp, q_shift, q_exp = (c.sem(ctx, s) for s in ("k_shifted", "k_exped", "q_shifted", "q_exped"))
    ctx_ready, ctx_out, mat_ready, mat_out = (c.sem(ctx, s) for s in ("ctx_ready", "ctx_out", "mat_ready", "mat_out"))
    q_ready, q_turned, q_copied, y_ready, y_out = \
        (c.sem(ctx, s) for s in ("q_ready", "q_turned", "q_copied", "y0_ready", "y0_out"))
    ss_ready, ss_root = c.sem(ctx, "ss_ready"), c.sem(ctx, "ss_root")
    met = c.met
    q, k, v = (qkv[:, :, i * HID0:(i + 1) * HID0] for i in range(3))

    @block.sync
    def _(sp):
        sp.dma_start(wg[:], a["gnn0_w"].rearrange("(k p) n -> p k n", p=P)).then_inc(in_w, 16)
        sp.dma_start(wq[:], a["qkv0_w"].rearrange("(k p) n -> p k n", p=P)).then_inc(in_w, 16)
        sp.dma_start(wo[:], a["out0_w"]).then_inc(in_w, 16)
        sp.dma_start(g_pre[:], a["g_pre0"]).then_inc(in_w, 16)
        for i, name in enumerate(("b_out0", "g_out0", "gnn0_b")):
            sp.dma_start(row[:, i, :], a[name].partition_broadcast(P)).then_inc(in_w, 16)
        sp.wait_ge(mem_zero, 1)
        for i in range(2):
            sp.dma_start(qkv[0:MEM, T, (1 + i) * HID0:(2 + i) * HID0], a["mem0"][i]).then_inc(in_w, 16)
        for t in range(T):
            sp.wait_ge(sup_out, t + 1)
            sp.dma_start(c.support[t * P:(t + 1) * P, :], sup[:, t % 2, :]).then_inc(sup_stored[t % 2], 16)
        sp.wait_ge(sup_stored[0], 16 * (-(-T // 2)))
        sp.wait_ge(sup_stored[1], 16 * (T // 2))
        meet(sp, met, met_n)

    @block.tensor
    def _(pe):
        pe.wait_ge(in_w, 16 * 9)
        pe.wait_ge(scaled, 1)
        for t in range(T):
            if t >= 2:
                pe.wait_ge(sup_out, t - 1)
                pe.wait_ge(qkv_out, t - 1)
            for kk in range(KD):
                mm = pe.matmul(c.bank[:, t % 2, 0:D], c.xT[:, kk, t * P:(t + 1) * P], wg[:, kk, :],
                               start=kk == 0, stop=kk == KD - 1)
            mm.then_inc(sup_ready, 1)
            for kk in range(KD):
                mm = pe.matmul(c.bank[:, 2 + t % 2, 0:3 * HID0], c.xT[:, kk, t * P:(t + 1) * P], wq[:, kk, :],
                               start=kk == 0, stop=kk == KD - 1)
            mm.then_inc(qkv_ready, 1)
        pe.wait_ge(top_ready, 1)
        pe.transpose(c.bank[:, 4, 0:P], k_top[:], c.ident[:]).then_inc(top_t, 1)
        pe.wait_ge(diag_ready, 1)
        pe.matmul(c.bank[:, 5, 0:HID0], c.ones[:, 0:P], k_diag[:], start=True, stop=True).then_inc(top_bc, 1)
        pe.wait_ge(k_exp, 1)
        for t in range(TM):
            pe.matmul(c.bank[:, 6, 0:HID0], v[:, t, :], k[:, t, :], start=t == 0, stop=t == TM - 1)
            mm = pe.matmul(c.bank[:, 7, 0:1], k[:, t, :], c.ones[:, 0:1], start=t == 0, stop=t == TM - 1)
        mm.then_inc(ctx_ready, 1)
        pe.wait_ge(ctx_out, 1)
        pe.matmul(c.bank[:, 4, 0:D], ctx_t[:], wo[:], start=True, stop=True).then_inc(mat_ready, 1)
        pe.wait_ge(q_ready, 1)
        pe.wait_ge(mat_out, 1)
        for t in range(T + 1):
            if t < T:
                if t >= 2:
                    pe.wait_ge(q_copied, t - 1)
                pe.transpose(c.bank[:, t % 2, 0:P], q[:, t, :], c.ident[:]).then_inc(q_turned, 1)
            if t >= 1:
                pe.wait_ge(q_copied, t)
                if t >= 3:
                    pe.wait_ge(y_out, t - 2)
                pe.matmul(c.bank[:, 2 + (t - 1) % 2, 0:D], q_t[:, (t - 1) % 2, :], mat[:],
                          start=True, stop=True).then_inc(y_ready, 1)
        meet(pe, met, met_n)

    @block.scalar
    def _(act):
        for t in range(T):
            act.wait_ge(qkv_ready, t + 1)
            act.copy(qkv[:, t, :], c.bank[:, 2 + t % 2, 0:3 * HID0]).then_inc(qkv_out, 1)
        act.wait_ge(k_shift, 1)
        act.activation(k, k, ACT.Exp).then_inc(k_exp, 1)
        act.wait_ge(q_shift, 1)
        act.activation(q[:, 0:T, :], q[:, 0:T, :], ACT.Exp).then_inc(q_exp, 1)
        for t in range(T):
            act.wait_ge(q_turned, t + 1)
            if t >= 2:
                act.wait_ge(y_ready, t - 1)
            act.copy(q_t[:, t % 2, :], c.bank[:, t % 2, 0:P]).then_inc(q_copied, 1)
        act.wait_ge(ss_ready, 1)
        act.activation(rn[:], ss[:], ACT.Sqrt).then_inc(ss_root, 1)
        meet(act, met, met_n)

    @block.vector
    def _(dve):
        ch = Chain(dve, step)
        dve.memset(qkv[:, T, :], 0.0).then_inc(mem_zero, 1)
        ch.then(dve.tensor_scalar(off[:, 0:1], c.part[:], float(LAST), NEG, ALU.is_ge, ALU.mult))
        ch.then(dve.tensor_scalar(off[:, 1:2], c.part[:], float(MEM), NEG, ALU.is_ge, ALU.mult))
        dve.wait_ge(in_w, 16 * 9)
        for kk in range(KD):
            ch.then(dve.tensor_scalar(wq[:, kk, :], wq[:, kk, :], g_pre[:, kk:kk + 1], None, ALU.mult))
        dve.sem_inc(scaled, 1)
        for t in range(T):
            dve.wait_ge(sup_ready, t + 1)
            if t >= 2:
                dve.wait_ge(sup_stored[t % 2], 16 * (t // 2))
            dve.tensor_scalar(sup[:, t % 2, :], c.bank[:, t % 2, 0:D], c.row_norm[:, t:t + 1], None, ALU.mult)\
                .then_inc(sup_out, 1)
        dve.wait_ge(qkv_out, T)
        ch.then(dve.tensor_scalar(k[:, T - 1, :], k[:, T - 1, :], off[:, 0:1], None, ALU.add))
        ch.then(dve.tensor_scalar(k[:, T, :], k[:, T, :], off[:, 1:2], None, ALU.add))
        dve.tensor_reduce(k_top[:], k.rearrange("p t c -> p c t"), AX.X, ALU.max).then_inc(top_ready, 1)
        dve.wait_ge(top_t, 1)
        ch.then(dve.tensor_reduce(k_max[:], c.bank[:, 4, 0:P], AX.X, ALU.max))
        dve.tensor_scalar(k_diag[:], c.ident[:], k_max[:], None, ALU.mult).then_inc(diag_ready, 1)
        dve.wait_ge(top_bc, 1)
        dve.tensor_tensor(k, k, c.bank[:, 5:6, 0:HID0].to_broadcast([P, TM, HID0]), ALU.subtract)\
            .then_inc(k_shift, 1)
        qh = q[:, 0:T, :].rearrange("p t (h d) -> p t h d", h=HEADS0)
        qs = [P, T, HEADS0, DH0]
        by_head = lambda b: b[:].rearrange("p (t h o) -> p t h o", h=HEADS0, o=1).to_broadcast(qs)
        ch.then(dve.tensor_reduce(q_max[:].rearrange("p (t h) -> p t h", h=HEADS0), qh, AX.X, ALU.max))
        dve.tensor_tensor(qh, qh, by_head(q_max), ALU.subtract).then_inc(q_shift, 1)
        dve.wait_ge(q_exp, 1)
        ch.then(dve.tensor_reduce(q_sum[:].rearrange("p (t h) -> p t h", h=HEADS0), qh, AX.X, ALU.add))
        ch.then(dve.reciprocal(q_sum[:], q_sum[:]))
        ch.then(dve.tensor_scalar(q_sum[:], q_sum[:], DH0 ** -0.5, None, ALU.mult))
        dve.tensor_tensor(qh, qh, by_head(q_sum), ALU.mult).then_inc(q_ready, 1)
        dve.wait_ge(ctx_ready, 1)
        ch.then(dve.reciprocal(inv_k[:], c.bank[:, 7, 0:1]))
        dve.tensor_tensor(ctx_t[:], c.bank[:, 6, 0:HID0], c.head32[:], ALU.mult).then_inc(ctx_out, 1)
        dve.wait_ge(mat_ready, 1)
        dve.tensor_scalar(mat[:], c.bank[:, 4, 0:D], inv_k[:], None, ALU.mult).then_inc(mat_out, 1)
        for t in range(T):
            dve.wait_ge(y_ready, t + 1)
            dve.tensor_tensor(y[:, t, :], c.bank[:, 2 + t % 2, 0:D], row[:, 0, :], ALU.add).then_inc(y_out, 1)
            dve.wait_ge(y_out, t + 1)
            ch.then(dve.scalar_tensor_tensor(scr[:], y[:, t, :], 1.0, y[:, t, :], ALU.mult, ALU.mult,
                                             accum_out=ss[:, t:t + 1]))
        dve.sem_inc(ss_ready, 1)
        dve.wait_ge(ss_root, 1)
        ch.then(dve.tensor_scalar(rn[:], rn[:], 1e-12, 1.0 / D ** 0.5, ALU.max, ALU.mult))
        ch.then(dve.reciprocal(rn[:], rn[:]))
        with dve.Fori(0, T) as t:
            flat = lambda b: b[:, ds(t, 1), :].rearrange("p a d -> p (a d)")
            ch.then(dve.scalar_tensor_tensor(flat(y), flat(y), rn[:, ds(t, 1)], row[:, 1, :],
                                             ALU.mult, ALU.mult), 3 * t)
            ch.then(dve.tensor_tensor(flat(y), flat(y), row[:, 2, :], ALU.add), 3 * t)
            ch.then(dve.tensor_tensor(flat(c.X), flat(c.X), flat(y), ALU.add), 3 * t)
        ch.n += 3 * (T - 1)
        meet(dve, met, met_n)




def load_slots(c, block, ctx, e):
    if e.slot is None:
        e.slot = c.sb(ctx, f"slot_{e.name}", [P, e.tiles, 4])
    e.slot_in = c.sem(ctx, f"slot_loaded_{e.name}")

    @block.sync
    def _(sp):
        sp.dma_start(e.slot[:].rearrange("p t w -> p (t w)"), e.slots.rearrange("(p t) w -> p (t w)", p=P))\
          .then_inc(e.slot_in, 16)


def gather_rows(c, block, ctx, e, table, width, used, credit=0):
    e.rows_in = c.sb(ctx, f"rows_{e.name}", [P, RING, width])
    idx = c.sb(ctx, f"gather_idx_{e.name}", [P, RING], I32)
    staged = c.sem(ctx, f"gather_idx_ready_{e.name}")
    turns = c.sem(ctx, f"gather_turns_{e.name}")
    e.gathered = [c.sem(ctx, f"gathered_{e.name}_{k}") for k in range(RING)]

    @block.gpsimd
    def _(pool):
        pool.wait_ge(e.slot_in, 16)
        with pool.Fori(0, e.tiles // RING) as i:
            for h in range(2):
                at = HALF * h
                for k in range(at, at + HALF):
                    pool.wait_ge(e.gathered[k], i * 16)
                pool.tensor_copy(idx[:, at:at + HALF],
                                 e.slot[:, ds(i * RING + at, HALF), 0:1].bitcast(I32).rearrange("p t o -> p (t o)"))\
                    .then_inc(staged, 1)
                pool.wait_ge(staged, i * 2 + h + 1)
                for k in range(at, at + HALF):
                    pool.wait_ge(used, i * RING + k + 1)
                    pool.sem_inc(turns, 1)
                    pool.indirect_dma_start(e.rows_in[:, k, :], None, table, bass.IndirectOffsetOnAxis(idx[:, k:k + 1], 0))\
                        .then_inc(e.gathered[k], 16)


def sum0_stage(c, block, ctx, e):
    hot = c.sb(ctx, "one_hot0", [P, RING, P])
    used = c.sem(ctx, "rows_used0")
    hot_ready = c.sem(ctx, "one_hot_ready0")
    added = c.sem(ctx, "group_added0")
    gather_rows(c, block, ctx, e, c.support, D, used)
    steps = e.tiles // RING
    per = GROUP // P

    @block.tensor
    def _(pe):
        pe.sem_inc(used, RING)
        with pe.Fori(0, steps) as i:
            for k in range(RING):
                g = k // per
                pe.wait_ge(hot_ready, i * RING + k + 1)
                pe.wait_ge(e.gathered[k], i * 16 + 16)
                if k % per == 0:
                    pe.wait_ge(added, i * BODY_GROUPS + g + 1)
                pe.matmul(c.bank[:, g, 0:D], hot[:, k, :], e.rows_in[:, k, :], start=k % per == 0,
                          stop=k % per == per - 1).then_inc(used, 1)

    @block.vector
    def _(dve):
        dve.sem_inc(added, BODY_GROUPS)
        dve.wait_ge(e.slot_in, 16)

        def add_group(i, g):
            tile = dve.value_load(e.group_tile[0:1, ds(i * BODY_GROUPS + g, 1)], min_val=0, max_val=T - 1)
            dve.wait_ge(used, i * RING + RING + per * (g + 1))
            dve.wait_ge(added, i * BODY_GROUPS + BODY_GROUPS + g)
            x = c.X[:, ds(tile, 1), :].rearrange("p a d -> p (a d)")
            dve.tensor_tensor(x, c.bank[:, g, 0:D], x, ALU.add).then_inc(added, 1)

        with dve.Fori(0, steps) as i:
            for g in range(BODY_GROUPS + 2):
                if g < BODY_GROUPS:
                    for k in range(per * g, per * g + per):
                        dve.wait_ge(used, i * RING + k + 1)
                        col = lambda w: e.slot[:, ds(i * RING + k, 1), w:w + 1].rearrange("p t o -> p (t o)")
                        dve.tensor_scalar(hot[:, k, :], c.iota[:, 0:P], col(1), col(2), ALU.is_equal, ALU.mult)\
                            .then_inc(hot_ready, 1)
                if g >= 2:
                    add_group(i, g - 2)




CHUNK_TILES = 5
CHUNK = CHUNK_TILES * P
HALF_CHUNK = CHUNK // 2
CHUNKS = T // CHUNK_TILES


def top2_gates(c, dve, ch, ctx, name, logits, n, gates, to_exp, exped):
    s = [P, T, n]
    buf = lambda k, shape: c.sb(ctx, f"{k}_{name}", shape)
    rank, rest, eq, pick, sel = (buf(k, s) for k in ("rank", "rest", "equal", "pick", "sel"))
    top, best = buf("top", [P, T]), buf("best", [P, T])
    wide = lambda b: b[:].rearrange("p (t o) -> p t o", o=1).to_broadcast(s)
    ch.then(dve.tensor_scalar(rank[:], c.iota[:, 0:n].rearrange("p (o e) -> p o e", o=1).to_broadcast(s),
                              -1.0, float(n), ALU.mult, ALU.add))
    ch.then(dve.tensor_copy(rest[:], logits))
    for turn in range(2):
        ch.then(dve.tensor_reduce(top[:], rest[:], AX.X, ALU.max))
        if turn == 0:
            ch.then(dve.tensor_tensor(gates, logits, wide(top), ALU.subtract))
            dve.sem_inc(to_exp, 1)
            dve.wait_ge(exped, 1)
        ch.then(dve.tensor_tensor(eq[:], rest[:], wide(top), ALU.is_equal))
        ch.then(dve.tensor_tensor(eq[:], eq[:], rank[:], ALU.mult))
        ch.then(dve.tensor_reduce(best[:], eq[:], AX.X, ALU.max))
        ch.then(dve.tensor_tensor(pick[:], eq[:], wide(best), ALU.is_equal))
        if turn == 0:
            ch.then(dve.tensor_copy(sel[:], pick[:]))
            ch.then(dve.scalar_tensor_tensor(rest[:].rearrange("p t e -> p (t e)"), pick[:].rearrange("p t e -> p (t e)"),
                                             3.0e38, rest[:].rearrange("p t e -> p (t e)"), ALU.mult, ALU.subtract))
            ch.then(dve.tensor_scalar(rest[:], rest[:], -1.0, None, ALU.mult))
        else:
            ch.then(dve.tensor_tensor(sel[:], sel[:], pick[:], ALU.add))
    ch.then(dve.tensor_tensor(gates, gates, sel[:], ALU.mult))
    ch.then(dve.tensor_reduce(top[:], gates, AX.X, ALU.add))
    ch.then(dve.reciprocal(top[:], top[:]))
    ch.then(dve.tensor_tensor(gates, gates, wide(top), ALU.mult))
    return sel, pick


EXPERTS0, FF0 = 8, 1024
CHOSEN = 2
PAIRS0 = CHOSEN * N
GROUPS0 = up((PAIRS0 + EXPERTS0 * (GROUP - 1)) // GROUP, 2)
SLOTS0 = GROUPS0 * GROUP


def clear_slots0(c, block, ctx):
    zero = c.sb(ctx, "zero_rows", [P, 2048])
    zeroed = c.sem(ctx, "zero_rows_ready")
    rows = c.slot_x[0:SLOTS0, :].rearrange("(p r) d -> p (r d)", p=P)
    width = SLOTS0 // P * D

    @block.scalar
    def _(act):
        act.wait_ge(zeroed, 1)
        for at in range(0, width, 2048):
            act.dma_start(rows[:, at:at + 2048], zero[:]).then_inc(c.slots_cleared, 16)
        act.wait_ge(c.slots_cleared, 16 * (width // 2048))

    @block.vector
    def _(dve):
        dve.memset(zero[:], 0.0).then_inc(zeroed, 1)


def router0_stage(c, block, ctx, met_n):
    n = EXPERTS0
    s3 = [P, T, n]
    wr = c.sb(ctx, "w_router", [P, KD, n])
    gates = c.sb(ctx, "gates0", s3)
    slot = c.sb(ctx, "slot_of", s3)
    upto = c.sb(ctx, "taken_upto", s3)
    num_i = c.sb(ctx, "expert_groups_i", [P, n], I32)
    num = c.sb(ctx, "expert_groups", [P, n])
    last = c.sb(ctx, "expert_last", [P, n])
    first = c.sb(ctx, "expert_first", [P, n])
    real = c.sb(ctx, "real", [P, 2])
    at = c.sb(ctx, "slot_at", [P, T, CHOSEN])
    of = c.sb(ctx, "expert_of", [1, GROUPS0])
    loaded, ready, to_exp, exped, step, picked, ranked = (
        c.sem(ctx, f"router_{k}") for k in ("loaded", "logits", "shifted", "exped", "step", "picked", "counted"))
    met = c.met
    mask = [None]

    @block.vector
    def _(dve):
        ch = Chain(dve, step)
        dve.wait_ge(ready, 1)
        sel, pick = top2_gates(c, dve, ch, ctx, "0", c.bank[:, 0, 0:T * n].rearrange("p (t e) -> p t e", e=n), n,
                               gates[:], to_exp, exped)
        mask[0] = sel
        ch.then(dve.tensor_scalar(real[:, 0:1], c.part[:], float(LAST), None, ALU.is_lt))
        ch.then(dve.tensor_scalar(sel[:, T - 1, :], sel[:, T - 1, :], real[:, 0:1], None, ALU.mult))
        dve.sem_inc(picked, 1)
        dve.wait_ge(ranked, 1)
        total = c.bank[:, 1, 0:T * n].rearrange("p (t e) -> p t e", e=n)
        for e in range(n):
            ch.then(dve.tensor_tensor_scan(upto[:, :, e], c.ones[:, 0:T], total[:, :, e], 0.0, ALU.mult, ALU.add))
        ch.then(dve.tensor_scalar(num_i[:], upto[:, T - 1, :], float(GROUP - 1), None, ALU.add))
        ch.then(dve.tensor_scalar(num_i[:], num_i[:], GROUP.bit_length() - 1, None, ALU.logical_shift_right))
        ch.then(dve.tensor_copy(num[:], num_i[:]))
        ch.then(dve.tensor_tensor_scan(last[:], c.ones[:, 0:n], num[:], 0.0, ALU.mult, ALU.add))
        ch.then(dve.tensor_tensor(first[:], last[:], num[:], ALU.subtract))
        ch.then(dve.tensor_scalar(first[:], first[:], float(GROUP), None, ALU.mult))
        ch.then(dve.tensor_tensor(slot[:], upto[:], total, ALU.subtract))
        ch.then(dve.tensor_tensor(slot[:], slot[:], c.bank[:, 2, 0:T * n].rearrange("p (t e) -> p t e", e=n), ALU.add))
        ch.then(dve.tensor_tensor(slot[:], slot[:],
                                  first[:].rearrange("p (o e) -> p o e", o=1).to_broadcast(s3), ALU.add))
        ch.then(dve.memset(of[:], 0.0))
        for e in range(n):
            ch.then(dve.scalar_tensor_tensor(of[:], c.iota[0:1, 0:GROUPS0], last[0:1, e:e + 1], of[:],
                                             ALU.is_ge, ALU.add))
        ch.then(dve.tensor_scalar(c.group_expert[:], of[:], float(n - 1), None, ALU.min))
        ch.then(dve.tensor_scalar(pick[:, T - 1, :], pick[:, T - 1, :], real[:, 0:1], None, ALU.mult))
        for k in (1, 0):
            if k == 0:
                ch.then(dve.tensor_tensor(pick[:], sel[:], pick[:], ALU.subtract))
            ch.then(dve.tensor_tensor(upto[:], slot[:], pick[:], ALU.mult))
            ch.then(dve.tensor_reduce(at[:, :, k], upto[:], AX.X, ALU.add))
            ch.then(dve.tensor_tensor(upto[:], gates[:], pick[:], ALU.mult))
            ch.then(dve.tensor_reduce(c.gate_of[:, :, k], upto[:], AX.X, ALU.add))
        ch.then(dve.tensor_copy(c.slot_from[:], at[:]))
        ch.then(dve.tensor_scalar(real[:, 0:1], real[:, 0:1], -1.0, 1.0, ALU.mult, ALU.add))
        for k in range(CHOSEN):
            ch.then(dve.tensor_scalar(real[:, 1:2], c.part[:], float(SLOTS0 + k * P), real[:, 0:1], ALU.add, ALU.mult))
            ch.then(dve.tensor_scalar(at[:, T - 1, k:k + 1], at[:, T - 1, k:k + 1], real[:, 1:2], None, ALU.add))
        ch.then(dve.tensor_copy(c.slot_to[:], at[:]))
        dve.sem_inc(c.routed, 1)
        meet(dve, met, met_n)

    @block.sync
    def _(sp):
        sp.dma_start(wr[:], c.a["router0_w"].rearrange("(k p) n -> p k n", p=P)).then_inc(loaded, 16)
        meet(sp, met, met_n)

    @block.tensor
    def _(pe):
        pe.wait_ge(loaded, 16)
        for t in range(T):
            for k in range(KD):
                mm = pe.matmul(c.bank[:, 0, t * n:(t + 1) * n], c.xT[:, k, t * P:(t + 1) * P], wr[:, k, :],
                               start=k == 0, stop=k == KD - 1)
        mm.then_inc(ready, 1)
        pe.wait_ge(picked, 1)
        sel = mask[0][:].rearrange("p t e -> p (t e)")
        pe.matmul(c.bank[:, 1, 0:T * n], c.ones[:, 0:P], sel, start=True, stop=True)
        pe.matmul(c.bank[:, 2, 0:T * n], c.before[:], sel, start=True, stop=True).then_inc(ranked, 1)
        meet(pe, met, met_n)

    @block.scalar
    def _(act):
        act.wait_ge(to_exp, 1)
        act.activation(gates[:], gates[:], ACT.Exp).then_inc(exped, 1)
        meet(act, met, met_n)


def send_nodes0(c, block, ctx):
    sent = c.sem(ctx, "nodes_sent")

    @block.gpsimd
    def _(pool):
        pool.wait_ge(c.routed, 1)
        pool.wait_ge(c.slots_cleared, 16 * (SLOTS0 // P * D // 2048))
        for t in range(T):
            for k in range(CHOSEN):
                pool.indirect_dma_start(c.slot_x, bass.IndirectOffsetOnAxis(c.slot_to[:, t, k:k + 1], 0),
                                        c.XN[:, t, :], None).then_inc(sent, 16)
        pool.wait_ge(sent, 16 * T * CHOSEN)
        pool.sem_inc(c.sent_all, 1)


def fetch_outputs0(c, block, ctx):
    c.out_ring = c.sb(ctx, "expert_row_ring", [P, RING, D])
    c.ring_in = [c.sem(ctx, f"expert_row_in_{k}") for k in range(RING)]
    c.ring_used = c.sem(ctx, "expert_row_used")

    @block.gpsimd
    def _(pool):
        pool.wait_ge(c.outputs_stored, 1)
        for j in range(T * CHOSEN):
            if j >= RING:
                pool.wait_ge(c.ring_used, j - RING + 1)
            pool.indirect_dma_start(c.out_ring[:, j % RING, :], None, c.slot_y,
                                    bass.IndirectOffsetOnAxis(c.slot_from[:, j // CHOSEN, j % CHOSEN:j % CHOSEN + 1], 0))\
                .then_inc(c.ring_in[j % RING], 16)


def private_experts_stage(c, block, ctx, met_n):
    a, met, FC, SUB = c.a, c.met, FF0 // P, GROUP // P
    w1 = c.sb(ctx, "w1_private", [P, 2, KD, FF0])
    w2 = c.sb(ctx, "w2_private", [P, 2, FC, D])
    b1 = c.sb(ctx, "b1_private", [P, 2, FC])
    b2 = c.sb(ctx, "b2_private", [P, 2, D])
    rows = c.sb(ctx, "slot_rows", [P, 2, SUB, D])
    xT = c.sb(ctx, "slot_xT", [P, 2, KD, GROUP])
    hid = c.sb(ctx, "hidden_private", [P, FC, GROUP])
    y = c.sb(ctx, "slot_out", [P, 2, SUB, D])
    weights_in = [c.sem(ctx, f"weights_in_{k}") for k in range(2)]
    rows_in = [c.sem(ctx, f"slot_rows_in_{k}") for k in range(2)]
    stored = [c.sem(ctx, f"slot_out_stored_{k}") for k in range(2)]
    turned = c.sem(ctx, "slot_rows_turned")
    x_ready = c.sem(ctx, "slot_xT_ready")
    h_ready = c.sem(ctx, "hidden_ready_private")
    h_done = c.sem(ctx, "hidden_gelu_private")
    y_ready = c.sem(ctx, "out_ready_private")
    y_done = c.sem(ctx, "out_biased_private")
    pairs = GROUPS0 // 2

    @block.sync
    def _(sp):
        def load_rows(g, b):
            sp.dma_start(rows[:, b, :, :], c.slot_x[ds(g * GROUP, GROUP), :].rearrange("(j p) d -> p j d", p=P))\
                .then_inc(rows_in[b], 16)

        def load_weights(g, b):
            e = sp.value_load(c.group_expert[0:1, ds(g, 1)], min_val=0, max_val=EXPERTS0 - 1)
            sp.dma_start(w1[:, b, :, :], a["w1p"][ds(e, 1), :, :].rearrange("e (k p) f -> p (e k) f", p=P))\
                .then_inc(weights_in[b], 16)
            sp.dma_start(b1[:, b, :], a["b1_0"][:, ds(e * FC, FC)]).then_inc(weights_in[b], 16)
            sp.dma_start(b2[:, b, :], a["b2_0"][ds(e * D, D)].partition_broadcast(P)).then_inc(weights_in[b], 16)
            sp.dma_start(w2[:, b, :, :], a["w2p"][ds(e, 1), :, :].rearrange("e (f p) d -> p (e f) d", p=P))\
                .then_inc(weights_in[b], 16)

        def step(i, b, tail):
            g = i * 2 + b
            if not (tail and b == 1):
                sp.wait_ge(y_done, i * (2 * SUB) + (b * SUB + 2))
                load_weights(g + 1, 1 - b)
            if not tail:
                sp.wait_ge(turned, g + 1)
                load_rows(g + 2, b)
            sp.wait_ge(y_done, i * (2 * SUB) + (b + 1) * SUB + 2)
            sp.dma_start(c.slot_y[ds(g * GROUP, GROUP), :].rearrange("(j p) d -> p j d", p=P), y[:, b, :, :])\
                .then_inc(stored[b], 16)

        load_weights(0, 0)
        sp.wait_ge(c.sent_all, 1)
        load_rows(0, 0)
        load_rows(1, 1)
        with sp.Fori(0, pairs - 1) as i:
            step(i, 0, False)
            step(i, 1, False)
        step(pairs - 1, 0, True)
        step(pairs - 1, 1, True)
        for b in range(2):
            sp.wait_ge(stored[b], 16 * pairs + 16)
        sp.sem_inc(c.outputs_stored, 1)
        meet(sp, met, met_n)

    @block.tensor
    def _(pe):
        def turn(i, b):
            pe.wait_ge(rows_in[b], i * 16 + 16)
            pe.wait_ge(x_ready, i * 2 + b + 1)
            for j in range(SUB):
                for k in range(KD):
                    mm = pe.transpose(c.bank[:, 4 + b, k * GROUP + j * P:k * GROUP + (j + 1) * P],
                                      rows[:, b, j, k * P:(k + 1) * P], c.ident[:])
            mm.then_inc(turned, 1)

        def group(i, b, tail):
            pe.wait_ge(x_ready, i * 2 + b + 3)
            pe.wait_ge(weights_in[b], i * 64 + 64)
            for f in range(FC):
                pe.wait_ge(h_done, i * (2 * FC) + (b * FC + f + 1))
                for k in range(KD):
                    mm = pe.matmul(c.bank[:, f % 4, 0:GROUP], w1[:, b, k, f * P:(f + 1) * P], xT[:, b, k, :],
                                   start=k == 0, stop=k == KD - 1)
                mm.then_inc(h_ready, 1)
            if not (tail and b == 1):
                turn(i + b, 1 - b)
            for j in range(SUB):
                pe.wait_ge(y_done, i * (2 * SUB) + (b * SUB + j + 1))
                for f in range(FC):
                    if j == 0:
                        pe.wait_ge(h_done, i * (2 * FC) + (b * FC + f + 1 + 4))
                    mm = pe.matmul(c.bank[:, 6 + j, 0:D], hid[:, f, j * P:(j + 1) * P], w2[:, b, f, :],
                                   start=f == 0, stop=f == FC - 1)
                mm.then_inc(y_ready, 1)

        turn(0, 0)
        with pe.Fori(0, pairs - 1) as i:
            group(i, 0, False)
            group(i, 1, False)
        group(pairs - 1, 0, True)
        group(pairs - 1, 1, True)
        meet(pe, met, met_n)

    @block.scalar
    def _(act):
        act.sem_inc(h_done, 4)
        act.sem_inc(y_ready, 1)
        with act.Fori(0, pairs) as i:
            for b in range(2):
                act.wait_ge(weights_in[b], i * 64 + 64)
                act.wait_ge(y_ready, i * (2 * SUB) + (b * SUB + 1))
                for f in range(FC):
                    act.wait_ge(h_ready, i * (2 * FC) + (b * FC + f + 1))
                    act.activation(hid[:, f, :], c.bank[:, f % 4, 0:GROUP], ACT.Gelu, bias=b1[:, b, f:f + 1])\
                       .then_inc(h_done, 1)
        meet(act, met, met_n)

    @block.vector
    def _(dve):
        dve.sem_inc(x_ready, 2)
        dve.sem_inc(y_done, 2)
        dve.sem_inc(stored[0], 16)
        dve.sem_inc(stored[1], 16)

        def copy_xT(i, b):
            dve.wait_ge(turned, i * 2 + b + 1)
            dve.tensor_copy(xT[:, b, :, :].rearrange("p k n -> p (k n)"), c.bank[:, 4 + b, :]).then_inc(x_ready, 1)

        def group(i, b, tail):
            if not (tail and b == 1):
                copy_xT(i + b, 1 - b)
            dve.wait_ge(stored[b], i * 16 + 16)
            for j in range(SUB):
                dve.wait_ge(y_ready, i * (2 * SUB) + (b * SUB + j + 1 + 1))
                dve.tensor_tensor(y[:, b, j, :], c.bank[:, 6 + j, 0:D], b2[:, b, :], ALU.add).then_inc(y_done, 1)

        copy_xT(0, 0)
        with dve.Fori(0, pairs - 1) as i:
            group(i, 0, False)
            group(i, 1, False)
        group(pairs - 1, 0, True)
        group(pairs - 1, 1, True)
        for j in range(T * CHOSEN):
            dve.wait_ge(c.ring_in[j % RING], 16 * (j // RING + 1))
            if j >= 1:
                dve.wait_ge(c.ring_used, j)
            x = c.X[:, j // CHOSEN, :]
            dve.scalar_tensor_tensor(x, c.out_ring[:, j % RING, :], c.gate_of[:, j // CHOSEN, j % CHOSEN:j % CHOSEN + 1],
                                     x, ALU.mult, ALU.add).then_inc(c.ring_used, 1)
        meet(dve, met, met_n)


def experts_stage(c, block, ctx, name, met_n, F, experts, b1_rows, b2_rows, gates):
    E, FC = len(experts), F // P
    w1 = c.sb(ctx, f"w1_{name}", [P, 2, KD, F])
    w2 = c.sb(ctx, f"w2_{name}", [P, 2, FC, D])
    b1 = c.sb(ctx, f"b1_{name}", [P, E * FC])
    b2 = c.sb(ctx, f"b2_{name}", [P, E, D])
    hid = c.sb(ctx, f"hidden_{name}", [P, FC, 2, HALF_CHUNK])
    part = c.sb(ctx, f"expert_out_{name}", [P, 2, D])
    biases = c.sem(ctx, f"biases_loaded_{name}")
    loaded = [c.sem(ctx, f"expert_loaded_{name}_{k}") for k in range(2)]
    h_ready = c.sem(ctx, f"hidden_ready_{name}")
    h_done = c.sem(ctx, f"hidden_gelu_{name}")
    y_ready = c.sem(ctx, f"out_ready_{name}")
    y_done = c.sem(ctx, f"out_added_{name}")
    biased = c.sem(ctx, f"out_biased_{name}")
    met = c.met
    since = {0: 1, 4: 4}

    @block.sync
    def _(sp):
        sp.dma_start(b1[:], b1_rows).then_inc(biases, 16)
        sp.dma_start(b2[:].rearrange("p e d -> p (e d)"), b2_rows.partition_broadcast(P)).then_inc(biases, 16)
        for e, (W1, W2) in enumerate(experts):
            if e >= 2:
                sp.wait_ge(y_ready, (e - 1) * T)
            sp.dma_start(w1[:, e % 2, :, :], W1.rearrange("(k p) f -> p k f", p=P)).then_inc(loaded[e % 2], 16)
            sp.dma_start(w2[:, e % 2, :, :], W2.rearrange("(f p) d -> p f d", p=P)).then_inc(loaded[e % 2], 16)
        meet(sp, met, met_n)

    @block.tensor
    def _(pe):
        for e in range(E):
            pe.wait_ge(loaded[e % 2], 32 * (e // 2 + 1))
            with pe.Fori(0, CHUNKS) as i:
                for f in range(FC):
                    pe.wait_ge(h_done, i * FC + (e * CHUNKS * FC + f + 1))
                    for half in range(2):
                        for k in range(KD):
                            mm = pe.matmul(c.bank[:, 2 * (f % 2) + half, 0:HALF_CHUNK],
                                           w1[:, e % 2, k, f * P:(f + 1) * P],
                                           c.xT[:, k, ds(i * CHUNK + half * HALF_CHUNK, HALF_CHUNK)],
                                           start=k == 0, stop=k == KD - 1)
                    mm.then_inc(h_ready, 1)
                for t in range(CHUNK_TILES):
                    pe.wait_ge(y_done, i * CHUNK_TILES + (e * T + t + 1 + CHUNK_TILES - since.get(t, 5)))
                    for f in range(FC):
                        if t == 0:
                            pe.wait_ge(h_done, i * FC + (e * CHUNKS * FC + f + 1 + 2))
                        mm = pe.matmul(c.bank[:, 4 + t % 4, 0:D],
                                       hid[:, f, :, :].rearrange("p a n -> p (a n)")[:, t * P:(t + 1) * P],
                                       w2[:, e % 2, f, :], start=f == 0, stop=f == FC - 1)
                    mm.then_inc(y_ready, 1)
        meet(pe, met, met_n)

    @block.scalar
    def _(act):
        act.wait_ge(biases, 32)
        act.sem_inc(h_done, 2)
        for e in range(E):
            with act.Fori(0, CHUNKS) as i:
                act.wait_ge(y_ready, i * CHUNK_TILES + e * T)
                for f in range(FC):
                    act.wait_ge(h_ready, i * FC + (e * CHUNKS * FC + f + 1))
                    act.activation(hid[:, f, :, :], c.bank[:, 2 * (f % 2):2 * (f % 2) + 2, 0:HALF_CHUNK],
                                   ACT.Gelu, bias=b1[:, e * FC + f:e * FC + f + 1]).then_inc(h_done, 1)
        meet(act, met, met_n)

    @block.vector
    def _(dve):
        dve.wait_ge(biases, 32)
        dve.sem_inc(y_done, CHUNK_TILES)
        for e in range(E):
            with dve.Fori(0, CHUNKS) as i:
                for t in range(CHUNK_TILES):
                    tile = i * CHUNK_TILES + t
                    x = c.X[:, ds(tile, 1), :].rearrange("p a d -> p (a d)")
                    gate = 1.0 if gates is None else gates[:, ds(tile, 1), e:e + 1].rearrange("p a b -> p (a b)")
                    dve.wait_ge(y_ready, tile + (e * T + 1))
                    dve.wait_ge(y_done, tile + (e * T + CHUNK_TILES))
                    dve.tensor_tensor(part[:, 0, :], c.bank[:, 4 + t % 4, 0:D], b2[:, e, :], ALU.add)\
                        .then_inc(biased, 1)
                    dve.wait_ge(biased, tile + (e * T + 1))
                    dve.scalar_tensor_tensor(x, part[:, 0, :], gate, x, ALU.mult, ALU.add).then_inc(y_done, 1)
        meet(dve, met, met_n)




HEADS1, FEAT = 4, 64
MSG = FEAT + HEADS1
AGG = HEADS1 * (FEAT + 1)
INNER = 512
KV_GROUPS = 2 * INNER // FEAT


def table1_stage(c, block, ctx, met_n):
    a = c.a
    w_all = c.sb(ctx, "w_all", [P, KD, 2 * MSG])
    w_nat = c.sb(ctx, "w_nat", [FEAT, 2, D])
    att = c.sb(ctx, "att1", [FEAT, HEADS1])
    rows = c.sb(ctx, "table1_rows", [P, T, 2 * MSG])
    loaded, folded, copied, ready, out, stored = (c.sem(ctx, f"table1_{k}") for k in
                                                  ("loaded", "folded", "copied", "ready", "evacuated", "stored"))
    met = c.met

    @block.sync
    def _(sp):
        for i, d in enumerate(("wf", "wr")):
            sp.dma_start(w_all[:, :, i * MSG:i * MSG + FEAT], a[d + "_t"].rearrange("(k p) n -> p k n", p=P))\
              .then_inc(loaded, 16)
            sp.dma_start(w_nat[:, i, :], a[d]).then_inc(loaded, 16)
        sp.dma_start(att[:], a["att1_t"]).then_inc(loaded, 16)
        sp.wait_ge(out, T)
        sp.dma_start(c.table1.rearrange("(t p) w -> p t w", p=P), rows[:]).then_inc(stored, 16)
        sp.wait_ge(stored, 16)
        meet(sp, met, met_n)

    @block.tensor
    def _(pe):
        pe.wait_ge(loaded, 16 * 5)
        for i in range(2):
            for k in range(KD):
                mm = pe.matmul(c.bank[:, 7, (2 * i + k) * HEADS1:(2 * i + k + 1) * HEADS1],
                               w_nat[:, i, k * P:(k + 1) * P], att[:], start=True, stop=True)
        mm.then_inc(folded, 1)
        pe.wait_ge(copied, 1)
        for t in range(T):
            if t >= 4:
                pe.wait_ge(out, t - 3)
            for k in range(KD):
                mm = pe.matmul(c.bank[:, t % 4, 0:2 * MSG], c.xT[:, k, t * P:(t + 1) * P], w_all[:, k, :],
                               start=k == 0, stop=k == KD - 1)
            mm.then_inc(ready, 1)
        meet(pe, met, met_n)

    @block.scalar
    def _(act):
        for t in range(T):
            act.wait_ge(ready, t + 1)
            act.copy(rows[:, t, :], c.bank[:, t % 4, 0:2 * MSG]).then_inc(out, 1)
        meet(act, met, met_n)

    @block.vector
    def _(dve):
        dve.wait_ge(folded, 1)
        dve.wait_ge(loaded, 16 * 5)
        dve.tensor_copy(w_all[:].rearrange("p k (i m) -> p i k m", i=2)[:, :, :, FEAT:MSG],
                        c.bank[:, 7, 0:4 * HEADS1].rearrange("p (i k h) -> p i k h", i=2, k=KD)).then_inc(copied, 1)
        meet(dve, met, met_n)


def mix1_stage(c, block, ctx, met_n):
    a = c.a
    heads = INNER // FEAT
    pairs = INNER // P
    wkv = c.sb(ctx, "w_kv1", [P, KD, 2 * INNER])
    wq = c.sb(ctx, "w_q1", [P, pairs, D])
    wo = c.sb(ctx, "w_out1", [P, pairs, D])
    bo = c.sb(ctx, "b_out1", [P, D])
    kv = c.sb(ctx, "kv1", [P, 2, KV_GROUPS, FEAT])
    sq = c.sb(ctx, "kv_square", [P, KV_GROUPS, FEAT])
    mean = c.sb(ctx, "kv_mean", [P, 2, KV_GROUPS])
    var = c.sb(ctx, "kv_var", [P, 2, KV_GROUPS])
    dots = c.sb(ctx, "dots", [P, pairs, P])
    mat = c.sb(ctx, "mat1", [P, pairs, D])
    mat2 = c.sb(ctx, "mat2", [P, KD, D])
    y = c.sb(ctx, "mix1_out", [P, D])
    loaded, kv_ready, centred, squared, var_ready, rooted, normed, step = \
        (c.sem(ctx, f"mix1_{k}") for k in ("loaded", "kv_ready", "centred", "squared", "var", "rooted", "normed", "step"))
    kv_used, dots_ready, dots_out, mat_ready, mat_out, mat2_ready, mat2_out, y_ready, y_out = \
        (c.sem(ctx, f"mix1_{k}") for k in ("kv_used", "dots_ready", "dots_out", "mat_ready", "mat_out", "mat2_ready",
                                           "mat2_out", "y_ready", "y_out"))
    met = c.met

    @block.sync
    def _(sp):
        sp.dma_start(wkv[:], a["wkv1_t"].rearrange("(k p) n -> p k n", p=P)).then_inc(loaded, 16)
        sp.dma_start(wq[:], a["wq1"].rearrange("(j p) n -> p j n", p=P)).then_inc(loaded, 16)
        sp.dma_start(wo[:], a["wout1_t"].rearrange("(j p) n -> p j n", p=P)).then_inc(loaded, 16)
        sp.dma_start(bo[:], a["bout1"].partition_broadcast(P)).then_inc(loaded, 16)
        meet(sp, met, met_n)

    @block.tensor
    def _(pe):
        pe.wait_ge(loaded, 64)
        for t in range(T + 1):
            if t < T:
                b = 2 * (t % 2)
                if t >= 2:
                    pe.wait_ge(centred, t - 1)
                for half in range(2):
                    for k in range(KD):
                        mm = pe.matmul(c.bank[:, b + half, :], c.xT[:, k, t * P:(t + 1) * P],
                                       wkv[:, k, half * INNER:(half + 1) * INNER], start=k == 0, stop=k == KD - 1)
                mm.then_inc(kv_ready, 1)
            if t >= 1:
                u = t - 1
                n = P if u < T - 1 else LAST
                pe.wait_ge(normed, u + 1)
                row = kv[0:n, u % 2, :, :].rearrange("p g f -> p (g f)")
                for j in range(pairs):
                    mm = pe.matmul(c.bank[:, 4 + j, 0:P], row[:, INNER + j * P:INNER + (j + 1) * P],
                                   row[:, j * P:(j + 1) * P], start=u == 0, stop=u == T - 1)
                mm.then_inc(kv_used, 1)
        pe.wait_ge(dots_out, pairs)
        for j in range(pairs):
            pe.matmul(c.bank[:, j, 0:D], dots[:, j, :], wo[:, j, :], start=True, stop=True)\
              .then_inc(mat_ready, 1)
        pe.wait_ge(mat_out, pairs)
        for k in range(KD):
            for j in range(pairs):
                mm = pe.matmul(c.bank[:, 4 + k, 0:D], wq[:, j, k * P:(k + 1) * P], mat[:, j, :],
                               start=j == 0, stop=j == pairs - 1)
        mm.then_inc(mat2_ready, 1)
        pe.wait_ge(mat2_out, 1)
        for t in range(T):
            if t >= 4:
                pe.wait_ge(y_out, t - 3)
            for k in range(KD):
                mm = pe.matmul(c.bank[:, t % 4, 0:D], c.xT[:, k, t * P:(t + 1) * P], mat2[:, k, :],
                               start=k == 0, stop=k == KD - 1)
            mm.then_inc(y_ready, 1)
        meet(pe, met, met_n)

    @block.scalar
    def _(act):
        for t in range(T):
            act.wait_ge(centred, t + 1)
            if t >= 1:
                act.wait_ge(var_ready, t)
            act.activation(sq[:], kv[:, t % 2, :, :], ACT.Square).then_inc(squared, 1)
            act.wait_ge(var_ready, t + 1)
            act.activation(var[:, t % 2, :], var[:, t % 2, :], ACT.Sqrt).then_inc(rooted, 1)
        meet(act, met, met_n)

    @block.vector
    def _(dve):
        ch = Chain(dve, step)
        shape = [P, KV_GROUPS, FEAT]
        wide = lambda b: b.rearrange("p (g o) -> p g o", o=1).to_broadcast(shape)
        for t in range(T):
            b, r = 2 * (t % 2), t % 2
            raw = c.bank[:, b:b + 2, :].rearrange("p a (g f) -> p (a g) f", f=FEAT)
            dve.wait_ge(kv_ready, t + 1)
            ch.then(dve.tensor_reduce(mean[:, r, :], raw, AX.X, ALU.add))
            ch.then(dve.tensor_scalar(mean[:, r, :], mean[:, r, :], 1.0 / FEAT, None, ALU.mult))
            if t >= 2:
                dve.wait_ge(kv_used, t - 1)
            dve.tensor_tensor(kv[:, r, :, :], raw, wide(mean[:, r, :]), ALU.subtract).then_inc(centred, 1)
            dve.wait_ge(squared, t + 1)
            ch.then(dve.tensor_reduce(var[:, r, :], sq[:], AX.X, ALU.add))
            dve.tensor_scalar(var[:, r, :], var[:, r, :], 1.0 / FEAT, 1e-5, ALU.mult, ALU.add).then_inc(var_ready, 1)
            dve.wait_ge(rooted, t + 1)
            ch.then(dve.reciprocal(var[:, r, :], var[:, r, :]))
            dve.tensor_tensor(kv[:, r, :, :], kv[:, r, :, :], wide(var[:, r, :]), ALU.mult).then_inc(normed, 1)
        dve.wait_ge(kv_used, T)
        for j in range(pairs):
            dve.tensor_tensor(dots[:, j, :], c.bank[:, 4 + j, 0:P], c.head64[:], ALU.mult).then_inc(dots_out, 1)
        for j in range(pairs):
            dve.wait_ge(mat_ready, j + 1)
            dve.tensor_copy(mat[:, j, :], c.bank[:, j, 0:D]).then_inc(mat_out, 1)
        dve.wait_ge(mat2_ready, 1)
        dve.tensor_scalar(mat2[:], c.bank[:, 4:4 + KD, 0:D], 1.0 / N, None, ALU.mult).then_inc(mat2_out, 1)
        for t in range(T):
            dve.wait_ge(y_ready, t + 1)
            dve.tensor_tensor(y[:], c.bank[:, t % 4, 0:D], bo[:], ALU.add).then_inc(y_out, 1)
            dve.wait_ge(y_out, t + 1)
            ch.then(dve.tensor_tensor(c.X[:, t, :], c.X[:, t, :], y[:], ALU.add))
        meet(dve, met, met_n)




def messages_stage(c, block, ctx, e):
    tmp = c.sb(ctx, "reverse_part", [P, 2, MSG])
    used = c.sem(ctx, "rows_used1")
    half_way = c.sem(ctx, "reverse_part_ready")
    gather_rows(c, block, ctx, e, c.table1, 2 * MSG, used)

    @block.vector
    def _(dve):
        dve.sem_inc(used, RING)
        dve.wait_ge(e.slot_in, 16)
        with dve.Fori(0, e.tiles // RING) as i:
            for k in range(RING + 1):
                if k < RING:
                    dve.wait_ge(e.gathered[k], i * 16 + 16)
                    col = e.slot[:, ds(i * RING + k, 1), 3:4].rearrange("p t o -> p (t o)")
                    if k >= 2:
                        dve.wait_ge(used, i * RING + (RING + k - 1))
                    dve.tensor_scalar(tmp[:, k % 2, :], e.rows_in[:, k, MSG:2 * MSG], col, None, ALU.mult)\
                        .then_inc(half_way, 1)
                if k >= 1:
                    j = k - 1
                    dve.wait_ge(half_way, i * RING + (j + 1))
                    col = e.slot[:, ds(i * RING + j, 1), 2:3].rearrange("p t o -> p (t o)")
                    dve.scalar_tensor_tensor(c.msg[:, ds(i * RING + j, 1), :].rearrange("p a m -> p (a m)"),
                                             e.rows_in[:, j, 0:MSG], col, tmp[:, j % 2, :], ALU.mult, ALU.add)\
                        .then_inc(used, 1)
            dve.wait_ge(used, i * RING + 2 * RING)


def softmax1_stage(c, block, ctx, e, met_n):
    none = c.sb(ctx, "no_edge", [P, e.tiles])
    top = c.sb(ctx, "score_top", [P, HEADS1])
    top4 = c.sb(ctx, "score_max", [HEADS1, 1])
    diag = c.sb(ctx, "score_diag", [HEADS1, HEADS1])
    step, top_ready, turned, diag_ready, spread, shifted, exped = \
        (c.sem(ctx, f"softmax1_{k}") for k in ("step", "top", "turned", "diag", "spread", "shifted", "exped"))
    met = c.met

    @block.tensor
    def _(pe):
        pe.wait_ge(top_ready, 1)
        pe.transpose(c.bank[0:HEADS1, 0, 0:P], top[:], c.ident[:]).then_inc(turned, 1)
        pe.wait_ge(diag_ready, 1)
        pe.matmul(c.bank[:, 1, 0:HEADS1], c.ones[0:HEADS1, 0:P], diag[:], start=True, stop=True).then_inc(spread, 1)
        meet(pe, met, met_n)

    @block.scalar
    def _(act):
        act.wait_ge(shifted, 1)
        act.activation(c.prob[:], c.prob[:], ACT.Exp).then_inc(exped, 1)
        act.wait_ge(exped, 1)
        meet(act, met, met_n)

    @block.sync
    def _(sp):
        meet(sp, met, met_n)

    @block.vector
    def _(dve):
        ch = Chain(dve, step)
        s = c.msg[:, :, FEAT:MSG]
        ch.then(dve.tensor_scalar(none[:], e.slot[:, :, 1], 0.0, NEG, ALU.is_lt, ALU.mult))
        ch.then(dve.scalar_tensor_tensor(c.prob[:], s, 0.2, s, ALU.mult, ALU.max))
        ch.then(dve.tensor_tensor(c.prob[:], c.prob[:],
                                  none[:].rearrange("p (t o) -> p t o", o=1).to_broadcast([P, e.tiles, HEADS1]),
                                  ALU.add))
        ch.then(dve.memset(c.msg[:, :, FEAT:FEAT + 1], 1.0))
        dve.tensor_reduce(top[:], c.prob[:].rearrange("p t h -> p h t"), AX.X, ALU.max).then_inc(top_ready, 1)
        dve.wait_ge(turned, 1)
        ch.then(dve.tensor_reduce(top4[:], c.bank[0:HEADS1, 0, 0:P], AX.X, ALU.max))
        dve.tensor_scalar(diag[:], c.ident[0:HEADS1, 0:HEADS1], top4[:], None, ALU.mult).then_inc(diag_ready, 1)
        dve.wait_ge(spread, 1)
        dve.tensor_tensor(c.prob[:], c.prob[:],
                          c.bank[:, 1:2, 0:HEADS1].to_broadcast([P, e.tiles, HEADS1]), ALU.subtract)\
            .then_inc(shifted, 1)
        ch.then(dve.memset(c.agg[:], 0.0))
        meet(dve, met, met_n)


def sum1_stage(c, block, ctx, e):
    hot = c.sb(ctx, "one_hot1", [P, RING, P])
    val = c.sb(ctx, "weighted1", [P, RING, HEADS1, FEAT + 1])
    den = c.sb(ctx, "weight_sum", [P, T * HEADS1])
    used = c.sem(ctx, "slots_used1")
    hot_ready = c.sem(ctx, "one_hot_ready1")
    val_even, val_odd = c.sem(ctx, "weighted_even"), c.sem(ctx, "weighted_odd")
    added = c.sem(ctx, "group_added1")
    step = c.sem(ctx, "mean1_step")
    per = GROUP // P
    steps = e.tiles // RING
    shape = [P, HEADS1, FEAT + 1]

    def weigh(eng, i, k, sem):
        m = c.msg[:, ds(i * RING + k, 1), 0:FEAT + 1].to_broadcast(shape)
        w = c.prob[:, ds(i * RING + k, 1), :].rearrange("p a (h o) -> p (a h) o", o=1).to_broadcast(shape)
        eng.wait_ge(used, i * RING + k + 1)
        eng.tensor_tensor(val[:, k, :, :], m, w, ALU.mult).then_inc(sem, 1)

    @block.gpsimd
    def _(pool):
        pool.wait_ge(c.met, 4 * c.softmax1_met)
        with pool.Fori(0, steps) as i:
            for k in range(1, RING, 2):
                weigh(pool, i, k, val_odd)

    @block.tensor
    def _(pe):
        pe.sem_inc(used, RING)
        with pe.Fori(0, steps) as i:
            for k in range(RING):
                g = k // per
                pe.wait_ge(hot_ready, i * RING + k + 1)
                pe.wait_ge(val_odd if k % 2 else val_even, i * (RING // 2) + (k // 2 + 1))
                if k % per == 0:
                    pe.wait_ge(added, i * BODY_GROUPS + g + 1)
                pe.matmul(c.bank[:, g, 0:AGG], hot[:, k, :], val[:, k, :, :].rearrange("p h f -> p (h f)"),
                          start=k % per == 0, stop=k % per == per - 1).then_inc(used, 1)

    @block.vector
    def _(dve):
        ch = Chain(dve, step)
        dve.sem_inc(added, BODY_GROUPS)

        def add_group(i, g):
            tile = dve.value_load(e.group_tile[0:1, ds(i * BODY_GROUPS + g, 1)], min_val=0, max_val=T - 1)
            dve.wait_ge(used, i * RING + RING + per * (g + 1))
            dve.wait_ge(added, i * BODY_GROUPS + BODY_GROUPS + g)
            x = c.agg[:, ds(tile, 1), :].rearrange("p a d -> p (a d)")
            dve.tensor_tensor(x, c.bank[:, g, 0:AGG], x, ALU.add).then_inc(added, 1)

        with dve.Fori(0, steps) as i:
            for g in range(BODY_GROUPS + 2):
                if g < BODY_GROUPS:
                    for k in range(per * g, per * g + per):
                        dve.wait_ge(used, i * RING + k + 1)
                        lo = e.slot[:, ds(i * RING + k, 1), 1:2].rearrange("p t o -> p (t o)")
                        dve.tensor_scalar(hot[:, k, :], c.iota[:, 0:P], lo, None, ALU.is_equal).then_inc(hot_ready, 1)
                        if k % 2 == 0:
                            weigh(dve, i, k, val_even)
                if g >= 2:
                    add_group(i, g - 2)
        dve.wait_ge(added, BODY_GROUPS * (steps + 1))
        agg = c.agg[:].rearrange("p t (h f) -> p (t h) f", f=FEAT + 1)
        ch.then(dve.tensor_scalar(den[:], agg[:, :, FEAT], 1e-10, None, ALU.add))
        ch.then(dve.reciprocal(den[:], den[:]))
        ch.then(dve.tensor_tensor(agg[:, :, 0:FEAT], agg[:, :, 0:FEAT],
                                  den[:].rearrange("p (g o) -> p g o", o=1).to_broadcast([P, T * HEADS1, FEAT]),
                                  ALU.mult))
        x = c.X[:].rearrange("p t (h f) -> p (t h) f", f=FEAT)
        ch.then(dve.tensor_tensor(x, x, agg[:, :, 0:FEAT], ALU.add))




NE1 = 4
HID_G = NE1 * NE1
ROW_G = HID_G + NE1
FAR = NE1


def table_g_stage(c, block, ctx, met_n):
    a = c.a
    w = c.sb(ctx, "w_gat", [P, KD, HID_G])
    att = c.sb(ctx, "att_gat", [P, 2, HID_G])
    prod = c.sb(ctx, "att_prod", [P, T, HID_G])
    low = c.sb(ctx, "low", [P, 1])
    lowd = c.sb(ctx, "low_diag", [P, P])
    loaded, ready, step, stored, out, low_ready, low_back = \
        (c.sem(ctx, f"table_g_{k}") for k in ("loaded", "ready", "step", "stored", "out", "low", "low_back"))
    met = c.met
    h = c.tab[:, :, 0:HID_G]
    a_src = c.tab[:, :, HID_G:ROW_G]

    @block.sync
    def _(sp):
        sp.dma_start(w[:], a["w_gat"].rearrange("(k p) n -> p k n", p=P)).then_inc(loaded, 16)
        sp.dma_start(att[:, 0, :], a["att_src"].partition_broadcast(P)).then_inc(loaded, 16)
        sp.dma_start(att[:, 1, :], a["att_dst"].partition_broadcast(P)).then_inc(loaded, 16)
        sp.wait_ge(out, 1)
        sp.dma_start(c.table_g.rearrange("(t p) w -> p t w", p=P), c.tab[:]).then_inc(stored, 16)
        sp.wait_ge(stored, 16)
        meet(sp, met, met_n)

    @block.scalar
    def _(act):
        meet(act, met, met_n)

    @block.tensor
    def _(pe):
        pe.wait_ge(loaded, 48)
        for t in range(T):
            for k in range(KD):
                mm = pe.matmul(c.bank[:, 0, t * HID_G:(t + 1) * HID_G], c.xT[:, k, t * P:(t + 1) * P], w[:, k, :],
                               start=k == 0, stop=k == KD - 1)
        mm.then_inc(ready, 1)
        pe.wait_ge(low_ready, 1)
        pe.transpose(c.bank[0:1, 1, 0:P], low[:], c.ident[:]).then_inc(low_back, 1)
        pe.wait_ge(low_ready, 2)
        pe.matmul(c.bank[:, 2, 0:1], c.ones[0:1, 0:P], lowd[0:1, 0:1], start=True, stop=True).then_inc(low_back, 1)
        meet(pe, met, met_n)

    @block.vector
    def _(dve):
        ch = Chain(dve, step)
        shape = [P, T, HID_G]
        dve.wait_ge(ready, 1)
        ch.then(dve.tensor_copy(h, c.bank[:, 0, 0:T * HID_G].rearrange("p (t n) -> p t n", n=HID_G)))
        for i, to in ((0, a_src), (1, c.edge_tab[:, :, 0:NE1])):
            ch.then(dve.tensor_tensor(prod[:], h, att[:, i:i + 1, :].to_broadcast(shape), ALU.mult))
            ch.then(dve.tensor_reduce(to, prod[:].rearrange("p t (h e) -> p t h e", e=NE1), AX.X, ALU.add))
        dve.sem_inc(out, 1)
        dve.tensor_reduce(low[:], a_src, AX.XY, ALU.min).then_inc(low_ready, 1)
        dve.wait_ge(low_back, 1)
        dve.tensor_reduce(lowd[0:1, 0:1], c.bank[0:1, 1, 0:P], AX.X, ALU.min).then_inc(low_ready, 1)
        dve.wait_ge(low_back, 2)
        ch.then(dve.tensor_scalar(c.lift[:], c.bank[:, 2, 0:1], -1.0, 1.0, ALU.mult, ALU.add))
        ch.then(dve.tensor_scalar(c.high[:], a_src, c.lift[:], None, ALU.add))
        meet(dve, met, met_n)


def segment_max_stage(c, block, ctx, e):
    hot = c.sb(ctx, "one_hot_m", [P, 2, P])
    lifted = c.sb(ctx, "lifted", [P, RING, NE1])
    diag = c.sb(ctx, "score_diags", [P, 2, NE1, P])
    mx = c.sb(ctx, "tile_max", [P, NE1])
    used = c.sem(ctx, "rows_used_g")
    lift_ready = c.sem(ctx, "lifted_ready")
    hot_ready = c.sem(ctx, "one_hot_ready_m")
    diag_ready = c.sem(ctx, "diag_ready")
    spread = c.sem(ctx, "scores_spread")
    taken = c.sem(ctx, "spread_taken")
    mx_step = c.sem(ctx, "tile_max_step")
    per = GROUP // P
    gather_rows(c, block, ctx, e, c.table_g, ROW_G, used)

    @block.scalar
    def _(act):
        with act.Fori(0, e.tiles // RING) as i:
            for k in range(RING):
                act.wait_ge(lift_ready, i * RING + k + 1)
                act.wait_ge(spread, i * RING + k + 1)
                for h in range(NE1):
                    op = act.activation(diag[:, k % 2, h, :], c.ident[:], ACT.Copy, scale=lifted[:, k, h:h + 1])
                op.then_inc(diag_ready, 1)

    @block.tensor
    def _(pe):
        pe.sem_inc(spread, 2)
        with pe.Fori(0, e.tiles // RING) as i:
            for k in range(RING):
                pe.wait_ge(hot_ready, i * RING + k + 1)
                pe.wait_ge(diag_ready, i * RING + k + 1)
                pe.wait_ge(taken, i * RING + k + 1)
                pe.matmul(c.bank[:, k % 2, :], hot[:, k % 2, :],
                          diag[:, k % 2, :, :].rearrange("p h n -> p (h n)"), start=True, stop=True)\
                  .then_inc(spread, 1)

    @block.vector
    def _(dve):
        dve.sem_inc(used, RING)
        dve.sem_inc(taken, 2)
        dve.wait_ge(e.slot_in, 16)

        def prepare(i, k):
            dve.wait_ge(e.gathered[k], i * 16 + 16)
            row = c.rows_g[:, ds(i * RING + k, 1), :].rearrange("p a w -> p (a w)")
            dve.tensor_scalar(lifted[:, k, :], e.rows_in[:, k, HID_G:ROW_G], c.lift[:], None, ALU.add)\
                .then_inc(lift_ready, 1)
            dve.tensor_copy(row, e.rows_in[:, k, :]).then_inc(used, 1)
            dve.wait_ge(spread, i * RING + k + 1)
            lo = e.slot[:, ds(i * RING + k, 1), 1:2].rearrange("p t o -> p (t o)")
            dve.tensor_scalar(hot[:, k % 2, :], c.iota[:, 0:P], lo, None, ALU.is_equal).then_inc(hot_ready, 1)

        def reduce(i, k, tile):
            high = c.high[:, ds(tile, 1), :].rearrange("p a h -> p (a h)")
            dve.wait_ge(spread, i * RING + k + 3)
            dve.wait_ge(mx_step, i * RING + k)
            dve.tensor_reduce(mx[:], c.bank[:, k % 2, :].rearrange("p (h n) -> p h n", h=NE1), AX.X, ALU.max)\
                .then_inc(taken, 1)
            dve.wait_ge(taken, i * RING + k + 3)
            dve.tensor_tensor(high, high, mx[:], ALU.max).then_inc(mx_step, 1)

        with dve.Fori(0, e.tiles // RING) as i:
            for k in range(RING + 1):
                if k < RING:
                    prepare(i, k)
                if k >= 1:
                    if (k - 1) % per == 0:
                        tile = dve.value_load(e.group_tile[0:1, ds(i * BODY_GROUPS + (k - 1) // per, 1)],
                                              min_val=0, max_val=T - 1)
                    reduce(i, k - 1, tile)


def sum_g_stage(c, block, ctx, e, met_n):
    a = c.a
    top = c.sb(ctx, "edge_max", [P, T, NE1])
    none = c.sb(ctx, "no_edge_g", [P, e.tiles])
    hot = c.sb(ctx, "one_hot_g", [P, RING, P])
    hot_t = c.sb(ctx, "one_hot_t", [P, RING, P])
    z = c.sb(ctx, "edge_score", [P, 2, RING, NE1])
    val = c.sb(ctx, "weighted_g", [P, RING, ROW_G])
    agg = c.sb(ctx, "agg_g", [P, T, ROW_G])
    own = c.sb(ctx, "own_weight", [P, T, NE1])
    step = c.sem(ctx, "sum_g_step")
    z_ready, z_exped = c.sem(ctx, "edge_score_ready"), c.sem(ctx, "edge_score_exped")
    hot_ready, turned, t_copied, spread = (c.sem(ctx, f"g_{k}") for k in ("hot", "turned", "hot_t", "spread"))
    val_ready = c.sem(ctx, "weighted_ready_g")
    done = c.sem(ctx, "group_summed_g")
    added = c.sem(ctx, "group_added_g")
    loop_step = c.sem(ctx, "g_loop_step")
    met = c.met
    per = GROUP // P
    steps = e.tiles // RING
    src = c.tab[:, :, HID_G:ROW_G]
    far = c.edge_tab[:, :, 0:NE1]
    et = c.edge_tab[:, :, NE1:2 * NE1]
    LOOP = 5

    @block.scalar
    def _(act):
        act.wait_ge(z_ready, 1)
        act.activation(own[:], own[:], ACT.Exp).then_inc(z_exped, 1)
        with act.Fori(0, steps) as i:
            for k in range(RING):
                if k % 4 == 0:
                    act.wait_ge(turned, i * RING + k + 4)
                    act.copy(hot_t[:, k:k + 4, :], c.bank[:, k // 4, :].rearrange("p (a n) -> p a n", n=P))\
                       .then_inc(t_copied, 1)
            act.wait_ge(z_ready, i + 2)
            act.activation(z[:, 0, :, :], z[:, 0, :, :], ACT.Exp).then_inc(z_exped, 1)
        meet(act, met, met_n)

    @block.tensor
    def _(pe):
        with pe.Fori(0, steps) as i:
            for k in range(RING):
                pe.wait_ge(hot_ready, i * RING + k + 1)
                if k % 4 == 0:
                    pe.wait_ge(t_copied, i * 2)
                pe.transpose(c.bank[:, k // 4, (k % 4) * P:(k % 4 + 1) * P], hot[:, k, :], c.ident[:])\
                  .then_inc(turned, 1)
            for k in range(RING):
                if k % per == 0:
                    tile = pe.value_load(e.group_tile[0:1, ds(i * BODY_GROUPS + k // per, 1)],
                                         min_val=0, max_val=T - 1)
                if k % 4 == 0:
                    pe.wait_ge(t_copied, i * 2 + (k // 4 + 1))
                mm = pe.matmul(c.bank[:, 2, k * 2 * NE1:(k + 1) * 2 * NE1], hot_t[:, k, :],
                               c.edge_tab[:, ds(tile, 1), :].rearrange("p a w -> p (a w)"), start=True, stop=True)
            mm.then_inc(spread, 1)
            pe.wait_ge(val_ready, i + 1)
            for k in range(RING):
                g = k // per
                mm = pe.matmul(c.bank[:, 3, g * ROW_G:(g + 1) * ROW_G], hot[:, k, :], val[:, k, :],
                               start=k % per == 0, stop=k % per == per - 1)
            mm.then_inc(done, 1)
        meet(pe, met, met_n)

    @block.sync
    def _(sp):
        sp.dma_start(c.row_g[:, 0, :], a["b_gat"].partition_broadcast(P)).then_inc(c.row_g_in, 16)
        sp.dma_start(c.row_g[:, 1, :], a["ln_gamma"].partition_broadcast(P)).then_inc(c.row_g_in, 16)
        sp.dma_start(c.row_g[:, 2, :], a["ln_beta"].partition_broadcast(P)).then_inc(c.row_g_in, 16)
        meet(sp, met, met_n)

    @block.vector
    def _(dve):
        ch = Chain(dve, step)
        lift_b = c.lift[:]
        ch.then(dve.tensor_scalar(top[:], c.high[:], lift_b, None, ALU.subtract))
        ch.then(dve.tensor_tensor(top[:], top[:], far, ALU.add))
        ch.then(dve.scalar_tensor_tensor(et, top[:], 0.2, top[:], ALU.mult, ALU.max))
        ch.then(dve.tensor_tensor(own[:], src, far, ALU.add))
        ch.then(dve.scalar_tensor_tensor(own[:], own[:], 0.2, own[:], ALU.mult, ALU.max))
        dve.tensor_tensor(own[:], own[:], et, ALU.subtract).then_inc(z_ready, 1)
        ch.then(dve.tensor_scalar(none[:], e.slot[:, :, 1], 0.0, NEG, ALU.is_lt, ALU.mult))
        dve.wait_ge(z_exped, 1)
        ch.then(dve.tensor_tensor(agg[:, :, 0:HID_G].rearrange("p t (h e) -> p t h e", e=NE1),
                                  c.tab[:, :, 0:HID_G].rearrange("p t (h e) -> p t h e", e=NE1),
                                  own[:].rearrange("p t (h o) -> p t h o", o=1).to_broadcast([P, T, NE1, NE1]),
                                  ALU.mult))
        ch.then(dve.tensor_copy(agg[:, :, HID_G:ROW_G], own[:]))
        with dve.Fori(0, steps) as i:
            for k in range(RING):
                if k == 0:
                    dve.wait_ge(done, i)
                lo = e.slot[:, ds(i * RING + k, 1), 1:2].rearrange("p t o -> p (t o)")
                dve.tensor_scalar(hot[:, k, :], c.iota[:, 0:P], lo, None, ALU.is_equal).then_inc(hot_ready, 1)
            rows = c.rows_g[:, ds(i * RING, RING), :]
            zz = z[:, 0, :, :]
            ps = c.bank[:, 2, 0:RING * 2 * NE1].rearrange("p (k w) -> p k w", w=2 * NE1)
            dve.wait_ge(spread, i + 1)
            ls = lambda ins, n: (ins.then_inc(loop_step, 1), dve.wait_ge(loop_step, i * LOOP + n))
            ls(dve.tensor_tensor(zz, rows[:, :, HID_G:ROW_G], ps[:, :, 0:NE1], ALU.add), 1)
            ls(dve.scalar_tensor_tensor(zz, zz, 0.2, zz, ALU.mult, ALU.max), 2)
            ls(dve.tensor_tensor(zz, zz, ps[:, :, NE1:2 * NE1], ALU.subtract), 3)
            dve.tensor_tensor(zz, zz, none[:, ds(i * RING, RING)].rearrange("p (k o) -> p k o", o=1)
                              .to_broadcast([P, RING, NE1]), ALU.add).then_inc(z_ready, 1)
            dve.wait_ge(z_exped, i + 2)
            ls(dve.tensor_copy(val[:, :, HID_G:ROW_G], zz), 4)
            dve.tensor_tensor(val[:, :, 0:HID_G].rearrange("p k (h e) -> p k h e", e=NE1),
                              rows[:, :, 0:HID_G].rearrange("p k (h e) -> p k h e", e=NE1),
                              zz.rearrange("p k (h o) -> p k h o", o=1).to_broadcast([P, RING, NE1, NE1]),
                              ALU.mult).then_inc(val_ready, 1)
            dve.wait_ge(val_ready, i + 1)
            dve.wait_ge(done, i + 1)
            for g in range(BODY_GROUPS):
                tile = dve.value_load(e.group_tile[0:1, ds(i * BODY_GROUPS + g, 1)], min_val=0, max_val=T - 1)
                dve.wait_ge(added, i * BODY_GROUPS + g)
                x = agg[:, ds(tile, 1), :].rearrange("p a d -> p (a d)")
                dve.tensor_tensor(x, c.bank[:, 3, g * ROW_G:(g + 1) * ROW_G], x, ALU.add).then_inc(added, 1)
            ls(dve.tensor_copy(z[:, 1, 0, :], z[:, 0, 0, :]), 5)
        dve.wait_ge(added, BODY_GROUPS * steps)
        ch.then(dve.tensor_scalar(own[:], agg[:, :, HID_G:ROW_G], 1e-16, None, ALU.add))
        ch.then(dve.reciprocal(own[:], own[:]))
        ch.then(dve.tensor_tensor(c.score16[:].rearrange("p t (h e) -> p t h e", e=NE1),
                                  agg[:, :, 0:HID_G].rearrange("p t (h e) -> p t h e", e=NE1),
                                  own[:].rearrange("p t (h o) -> p t h o", o=1).to_broadcast([P, T, NE1, NE1]),
                                  ALU.mult))
        meet(dve, met, met_n)


def gates1_stage(c, block, ctx, met_n):
    sq = c.sb(ctx, "score_square", [P, T, HID_G])
    m = c.sb(ctx, "score_mean", [P, T])
    v = c.sb(ctx, "score_var", [P, T])
    s4 = c.sb(ctx, "score4", [P, T, NE1])
    step, var_ready, rooted, to_exp, exped = (c.sem(ctx, f"gates1_{k}") for k in
                                              ("step", "var", "rooted", "shifted", "exped"))
    met = c.met
    shape = [P, T, HID_G]

    @block.scalar
    def _(act):
        act.wait_ge(var_ready, 1)
        act.activation(v[:], v[:], ACT.Sqrt).then_inc(rooted, 1)
        act.wait_ge(to_exp, 1)
        act.activation(c.gates1[:], c.gates1[:], ACT.Exp).then_inc(exped, 1)
        meet(act, met, met_n)

    @block.tensor
    def _(pe):
        meet(pe, met, met_n)

    @block.sync
    def _(sp):
        meet(sp, met, met_n)

    @block.vector
    def _(dve):
        ch = Chain(dve, step)
        s = c.score16[:]
        wide = lambda b: b[:].rearrange("p (t o) -> p t o", o=1).to_broadcast(shape)
        row = lambda i: c.row_g[:, i:i + 1, :].to_broadcast(shape)
        dve.wait_ge(c.row_g_in, 48)
        ch.then(dve.tensor_tensor(s, s, row(0), ALU.add))
        ch.then(dve.tensor_reduce(m[:], s, AX.X, ALU.add))
        ch.then(dve.tensor_scalar(m[:], m[:], 1.0 / HID_G, None, ALU.mult))
        ch.then(dve.tensor_tensor(s, s, wide(m), ALU.subtract))
        ch.then(dve.tensor_tensor(sq[:], s, s, ALU.mult))
        ch.then(dve.tensor_reduce(v[:], sq[:], AX.X, ALU.add))
        dve.tensor_scalar(v[:], v[:], 1.0 / HID_G, 1e-5, ALU.mult, ALU.add).then_inc(var_ready, 1)
        dve.wait_ge(rooted, 1)
        ch.then(dve.reciprocal(v[:], v[:]))
        ch.then(dve.tensor_tensor(s, s, wide(v), ALU.mult))
        ch.then(dve.tensor_tensor(s, s, row(1), ALU.mult))
        ch.then(dve.tensor_tensor(s, s, row(2), ALU.add))
        ch.then(dve.tensor_reduce(s4[:], s.rearrange("p t (h e) -> p t e h", e=NE1), AX.X, ALU.add))
        ch.then(dve.tensor_scalar(s4[:], s4[:], 1.0 / NE1, None, ALU.mult))
        top2_gates(c, dve, ch, ctx, "1", s4[:], NE1, c.gates1[:], to_exp, exped)
        meet(dve, met, met_n)




def build(nc, a, out, upto=4):
    c = Core(nc, a, out)
    c.upto = upto
    with ExitStack() as top:
        top.enter_context(nc.allow_non_contiguous_dma("small strided rows"))
        c.kept.append(top)
        stage_setup(c, top)
        c.support = nc.dram_tensor("support", [NP, D], F32, kind="Internal").ap()
        c.slot_x = nc.dram_tensor("slot_x", [SLOTS0 + CHOSEN * P, D], F32, kind="Internal").ap()
        c.slot_y = nc.dram_tensor("slot_y", [SLOTS0, D], F32, kind="Internal").ap()
        c.slots_cleared = c.sem(top, "slots_cleared")
        e1 = Edges(c, "gnn1", a["dst"], a["src"], a["edge_attr_2"], 125, top)
        eg = Edges(c, "router", a["router_dst"], a["router_src"], None, P, top)
        records = top.enter_context(ExitStack())
        e1.hold_records(c, records)
        eg.hold_records(c, records)
        with ExitStack() as l0:
            c.kept.append(l0)
            e0 = Edges(c, "gnn0", a["src"], a["dst"], a["edge_weight"], 125, l0)
            e0.hold_records(c, l0)
            with ExitStack() as s, nc.Block() as block:
                rank_stage(c, block, s, e0, 1)
            c.clear_spent()
            with ExitStack() as s, nc.Block() as block:
                scatter_records(c, block, s, e0)
                with ExitStack() as st:
                    norm_stage(c, block, st, "0", 2, True)
                with ExitStack() as st:
                    mix0_stage(c, block, st, 3)
                with ExitStack() as st:
                    rank_stage(c, block, st, e1, 4)
                with ExitStack() as st:
                    rank_stage(c, block, st, eg, 5)
            c.clear_spent()
            with ExitStack() as s, nc.Block() as block:
                clear_slots0(c, block, s)
                load_slots(c, block, s, e0)
                sum0_stage(c, block, s, e0)
            c.clear_spent()
        if c.upto >= 2:
            with ExitStack() as l1:
                c.kept.append(l1)
                m = 5
                with ExitStack() as s, nc.Block() as block:
                    c.group_expert = c.sb(s, "group_expert", [1, GROUPS0], I32)
                    c.XN = c.sb(s, "normed_rows", [P, T, D])
                    c.slot_from = c.sb(s, "slot_from", [P, T, CHOSEN], I32)
                    c.slot_to = c.sb(s, "slot_to", [P, T, CHOSEN], I32)
                    c.gate_of = c.sb(s, "gate_of", [P, T, CHOSEN])
                    c.routed = c.sem(s, "routed")
                    c.sent_all = c.sem(s, "all_nodes_sent")
                    c.outputs_stored = c.sem(s, "slot_out_all_stored")
                    send_nodes0(c, block, s)
                    scatter_records(c, block, s, e1)
                    fetch_outputs0(c, block, s)
                    for stage in (lambda st, m: norm_stage(c, block, st, "1", m, False, c.XN),
                                  lambda st, m: router0_stage(c, block, st, m),
                                  lambda st, m: experts_stage(
                                      c, block, st, "0", m, FF0, [(a["w1s"], a["w2s"])],
                                      a["b1_0"][:, EXPERTS0 * FF0 // P:], a["b2_0"][EXPERTS0 * D:], None),
                                  lambda st, m: private_experts_stage(c, block, st, m)):
                        m += 1
                        with ExitStack() as st:
                            stage(st, m)
                c.clear_spent()
                if c.upto >= 3:
                    c.table1 = nc.dram_tensor("table1", [NP, 2 * MSG], F32, kind="Internal").ap()
                    with ExitStack() as s, nc.Block() as block:
                        scatter_records(c, block, s, eg)
                        for stage in (lambda st, m: norm_stage(c, block, st, "2", m, False),
                                      lambda st, m: table1_stage(c, block, st, m),
                                      lambda st, m: mix1_stage(c, block, st, m)):
                            m += 1
                            with ExitStack() as st:
                                stage(st, m)
                    c.clear_spent()
                    records.close()
                    with ExitStack() as s:
                        c.msg = c.sb(s, "messages", [P, e1.tiles, MSG])
                        c.prob = c.sb(s, "edge_weight", [P, e1.tiles, HEADS1])
                        c.agg = c.XT[:].rearrange("p (t f) -> p t f", t=T)
                        with ExitStack() as s2:
                            e1.slot = c.sb(s, "slot_gnn1", [P, e1.tiles, 4])
                            with nc.Block() as block:
                                load_slots(c, block, s2, e1)
                                messages_stage(c, block, s2, e1)
                            c.clear_spent()
                        with ExitStack() as s2, nc.Block() as block:
                            m += 1
                            with ExitStack() as st:
                                softmax1_stage(c, block, st, e1, m)
                            c.softmax1_met = m
                            sum1_stage(c, block, s2, e1)
                        c.clear_spent()
                if c.upto >= 4:
                    c.table_g = nc.dram_tensor("table_g", [NP, ROW_G], F32, kind="Internal").ap()
                    c.tab = c.sb(l1, "tab_g", [P, T, ROW_G])
                    c.edge_tab = c.sb(l1, "edge_tab", [P, T, 2 * NE1])
                    c.high = c.sb(l1, "high", [P, T, NE1])
                    c.lift = c.sb(l1, "lift", [P, 1])
                    c.row_g = c.sb(l1, "row_g", [P, 3, HID_G])
                    c.row_g_in = c.sem(l1, "row_g_loaded")
                    c.score16 = c.sb(l1, "score16", [P, T, HID_G])
                    c.gates1 = c.sb(l1, "gates1", [P, T, NE1])
                    c.rows_g = c.sb(l1, "rows_g", [P, eg.tiles, ROW_G])
                    eg.slot = c.sb(l1, "slot_router", [P, eg.tiles, 4])
                    with nc.Block() as block:
                        for stage in (lambda st, m: norm_stage(c, block, st, "3", m, False),
                                      lambda st, m: table_g_stage(c, block, st, m)):
                            m += 1
                            with ExitStack() as st:
                                stage(st, m)
                    c.clear_spent()
                    with ExitStack() as s, nc.Block() as block:
                        load_slots(c, block, s, eg)
                        segment_max_stage(c, block, s, eg)
                    c.clear_spent()
                    with nc.Block() as block:
                        for stage in (lambda st, m: sum_g_stage(c, block, st, eg, m),
                                      lambda st, m: gates1_stage(c, block, st, m),
                                      lambda st, m: experts_stage(
                                          c, block, st, "1", m, 512,
                                          [(a["w1e"][i], a["w2e"][i]) for i in range(4)],
                                          a["b1_1"], a["b2_1"], c.gates1)):
                            m += 1
                            with ExitStack() as st:
                                stage(st, m)
                    c.clear_spent()
        stored = c.sem(top, "stored")
        with nc.Block() as block:
            @block.sync
            def _(sp):
                sp.dma_start(out[0:(T - 1) * P, :].rearrange("(t p) d -> p t d", p=P), c.X[:, 0:T - 1, :])\
                  .then_inc(stored, 16)
                sp.dma_start(out[(T - 1) * P:N, :], c.X[0:LAST, T - 1, :]).then_inc(stored, 16)
                sp.wait_ge(stored, 32)


        c.clear_spent()
def laid_out(x):
    import numpy as np
    n = {k: np.asarray(v) for k, v in x.items()}
    cols = lambda b: np.ascontiguousarray(b.reshape(-1, P).T)
    return {
        "x": n["x"], "src": n["src"], "dst": n["dst"], "edge_weight": n["edge_weight"],
        "gnn0_w": n["L0_gnn_weight"], "gnn0_b": n["L0_gnn_bias"], "qkv0_w": n["L0_mix_w_qkv"],
        "out0_w": n["L0_mix_w_out"], "b_out0": n["L0_mix_b_out"], "g_out0": n["L0_mix_g_out"],
        "g_pre0": cols(n["L0_mix_g_pre"]),
        "edge_attr_2": n["edge_attr_2"], "router0_w": n["L0_ffn_Wr"],
        "w1p": n["L0_ffn_W1p"], "w2p": n["L0_ffn_W2p"], "w1s": n["L0_ffn_W1s"], "w2s": n["L0_ffn_W2s"],
        "b1_0": cols(np.concatenate([n["L0_ffn_b1p"].reshape(-1), n["L0_ffn_b1s"]])),
        "b2_0": np.concatenate([n["L0_ffn_b2p"].reshape(-1), n["L0_ffn_b2s"]]),
        "wf": n["L1_gnn_W_forward"], "wr": n["L1_gnn_W_reverse"],
        "wf_t": np.ascontiguousarray(n["L1_gnn_W_forward"].T), "wr_t": np.ascontiguousarray(n["L1_gnn_W_reverse"].T),
        "att1_t": np.ascontiguousarray(n["L1_gnn_attn_forward"][0].T),
        "wkv1_t": np.ascontiguousarray(n["L1_mix_Wqkv"][INNER:].T), "wq1": n["L1_mix_Wqkv"][:INNER],
        "wout1_t": np.ascontiguousarray(n["L1_mix_Wout"].T), "bout1": n["L1_mix_bout"],
        "w_gat": n["L1_ffn_W_gat"], "att_src": n["L1_ffn_att_src"].reshape(-1),
        "att_dst": n["L1_ffn_att_dst"].reshape(-1), "b_gat": n["L1_ffn_b_gat"],
        "ln_gamma": n["L1_ffn_ln_gamma"], "ln_beta": n["L1_ffn_ln_beta"],
        "w1e": n["L1_ffn_W1"], "w2e": n["L1_ffn_W2"], "b1_1": cols(n["L1_ffn_b1"]), "b2_1": n["L1_ffn_b2"].reshape(-1),
        "router_src": np.ascontiguousarray(n["L1_ffn_edge_index"][0]),
        "router_dst": np.ascontiguousarray(n["L1_ffn_edge_index"][1]),
        "mem0": np.ascontiguousarray(n["L0_mix_mem_kv"].transpose(0, 3, 1, 2)).reshape(2, MEM, HID0),
    }


def kernel(**inputs):
    import numpy as np
    from concourse import bacc
    from concourse.bass_utils import run_bass_kernel_spmd

    nc = bacc.Bacc("TRN2", target_bir_lowering=False, num_devices=1)
    arrays = {f"in_{k}": v for k, v in laid_out(inputs).items()}
    aps = {k[3:]: nc.dram_tensor(k, v.shape, mybir.dt.from_np(v.dtype), kind="ExternalInput").ap()
           for k, v in arrays.items()}
    out = nc.dram_tensor("out", (N, D), F32, kind="ExternalOutput").ap()
    build(nc, aps, out)
    return run_bass_kernel_spmd(nc, [arrays], core_ids=[0]).results[0]["out"]
```

```python
from contextlib import ExitStack

import concourse.bass as bass
from concourse import mybir

F32 = mybir.dt.float32
I32 = mybir.dt.int32
ALU = mybir.AluOpType
ACT = mybir.ActivationFunctionType
AX = mybir.AxisListType
ds = bass.ds

P = 128
D = 256
N = 3125
T = -(-N // P)
LAST = N - (T - 1) * P
NP = T * P
KD = D // P
GROUP = 256
RING = 8
HALF = RING // 2
BODY_GROUPS = RING * P // GROUP
NEG = -1.0e30


def up(a, b):
    return -(-a // b) * b


def slot_tiles(edges):
    return up((edges + T * (GROUP - 1)) // GROUP * (GROUP // P), RING)


class Chain:

    def __init__(self, eng, sem):
        self.eng, self.sem, self.n = eng, sem, 0

    def then(self, ins, extra=0):
        ins.then_inc(self.sem, 1)
        self.n += 1
        self.eng.wait_ge(self.sem, self.n + extra)


class Core:

    def __init__(self, nc, inputs, out):
        self.nc, self.a, self.out = nc, inputs, out
        self.kept = []
        self.spent = []

    def sb(self, ctx, name, shape, dt=F32):
        return ctx.enter_context(self.nc.sbuf_tensor(name, shape, dt))

    def sem(self, ctx, name):
        if any(ctx is k for k in self.kept):
            return ctx.enter_context(self.nc.semaphore(name))
        self.spent.append(self.nc.alloc_semaphore(name=name))
        return self.spent[-1]

    def clear_spent(self):
        self.nc.all_engine_barrier()
        self.nc.clear_and_free_semaphores(self.spent)
        self.nc.all_engine_barrier()
        self.spent = []


def meet(eng, met, n):
    eng.drain().then_inc(met, 1)
    eng.wait_ge(met, 4 * n)


def everyone_meets(block, met, n):
    block.sync(lambda e: meet(e, met, n))
    block.scalar(lambda e: meet(e, met, n))
    block.vector(lambda e: meet(e, met, n))
    block.tensor(lambda e: meet(e, met, n))




def stage_setup(c, ctx):
    nc = c.nc
    c.bank = ctx.enter_context(nc.psum_tensor("banks", [P, 8, 512], F32))
    c.met = c.sem(ctx, "met")
    c.row_norm = c.sb(ctx, "row_norm", [P, T])
    c.X = c.sb(ctx, "x", [P, T, D])
    c.XT = c.sb(ctx, "xT", [P, T * 260])
    c.xT = c.XT[:, 0:KD * NP].rearrange("p (k n) -> p k n", k=KD)
    c.ident = c.sb(ctx, "ident", [P, P])
    c.before = c.sb(ctx, "before", [P, P])
    c.ones = c.sb(ctx, "ones", [P, 512])
    c.iota_i = c.sb(ctx, "iota_i", [P, 512], I32)
    c.iota = c.sb(ctx, "iota", [P, 512])
    c.part_i = c.sb(ctx, "part_i", [P, 1], I32)
    c.part = c.sb(ctx, "part", [P, 1])
    c.head32 = c.sb(ctx, "head32", [P, P])
    c.head64 = c.sb(ctx, "head64", [P, P])
    load_sem = c.sem(ctx, "setup_loaded")
    const_sem = c.sem(ctx, "constants_made")
    zero_sem = c.sem(ctx, "tail_zeroed")
    with nc.Block() as block:
        @block.sync
        def _(sp):
            sp.dma_start(c.X[:, 0:T - 1, :], c.a["x"][0:(T - 1) * P, :].rearrange("(t p) d -> p t d", p=P))\
              .then_inc(load_sem, 16)
            sp.wait_ge(zero_sem, 1)
            sp.dma_start(c.X[0:LAST, T - 1, :], c.a["x"][(T - 1) * P:N, :]).then_inc(load_sem, 16)
            sp.wait_ge(load_sem, 32)

        @block.vector
        def _(dve):
            dve.memset(c.X[:, T - 1, :], 0.0).then_inc(zero_sem, 1)

        @block.gpsimd
        def _(pool):
            ch = Chain(pool, const_sem)
            ch.then(pool.memset(c.ones[:], 1.0))
            ch.then(pool.memset(c.ident[:], 0.0))
            ch.then(pool.affine_select(out=c.ident[:], in_=c.ident[:], compare_op=ALU.not_equal, fill=1.0,
                                       base=0, pattern=[[-1, P]], channel_multiplier=1))
            ch.then(pool.affine_select(out=c.before[:], in_=c.ones[:, 0:P], compare_op=ALU.is_gt, fill=0.0,
                                       base=0, pattern=[[1, P]], channel_multiplier=-1))
            ch.then(pool.iota(c.iota_i[:], pattern=[[1, 512]], base=0, channel_multiplier=0))
            ch.then(pool.tensor_copy(c.iota[:], c.iota_i[:]))
            ch.then(pool.iota(c.part_i[:], pattern=[[1, 1]], base=0, channel_multiplier=1))
            ch.then(pool.tensor_copy(c.part[:], c.part_i[:]))
            for mask, d in ((c.head32, DH0), (c.head64, FEAT)):
                heads = mask[:].rearrange("p (h d) -> p h d", d=d)
                ch.then(pool.affine_select(out=heads, in_=c.ones[:, 0:P].rearrange("p (h d) -> p h d", d=d),
                                           compare_op=ALU.is_ge, fill=0.0, base=0,
                                           pattern=[[-d, P // d], [0, d]], channel_multiplier=1))
                ch.then(pool.affine_select(out=heads, in_=heads, compare_op=ALU.is_ge, fill=0.0, base=d - 1,
                                           pattern=[[d, P // d], [0, d]], channel_multiplier=-1))




class Edges:

    def __init__(self, c, name, key, val, payload, parts, ctx):
        self.name, self.key, self.val, self.payload = name, key, val, payload
        self.parts, self.slot = parts, None
        self.count = key.shape[0]
        self.per = self.count // parts
        assert self.per * parts == self.count and self.per % RING == 0
        self.tiles = slot_tiles(self.count)
        self.groups = self.tiles * P // GROUP
        self.slots = c.nc.dram_tensor(f"slots_{name}", [P * self.tiles, 4], F32, kind="Internal").ap()
        self.group_tile = c.sb(ctx, f"group_tile_{name}", [1, self.groups], I32)
        self.filled = c.sem(ctx, f"slots_filled_{name}")
        self.ranked = c.sem(ctx, f"ranked_{name}")

    def hold_records(self, c, ctx):
        self.rows = c.sb(ctx, f"slot_row_{self.name}", [P, self.per], I32)
        self.rec = c.sb(ctx, f"rec_{self.name}", [P, self.per, 4])


def rank_stage(c, block, ctx, e, met_n):
    nc, J, n = c.nc, e.per, e.parts
    key = c.sb(ctx, f"key_{e.name}", [P, J], I32)
    val = c.sb(ctx, f"val_{e.name}", [P, J], I32)
    hi_i = c.sb(ctx, f"hi_i_{e.name}", [P, J], I32)
    hi = c.sb(ctx, f"hi_{e.name}", [P, J])
    pay = c.sb(ctx, f"pay_{e.name}", [P, J, 2])
    one_hot = c.sb(ctx, f"in_tile_{e.name}", [P, 2, J])
    seen = c.sb(ctx, f"seen_{e.name}", [P, 2, J])
    pos = c.sb(ctx, f"pos_{e.name}", [P, J])
    posf = c.sb(ctx, f"posf_{e.name}", [P, J])
    cnt = c.sb(ctx, f"cnt_{e.name}", [P, T])
    num_i = c.sb(ctx, f"num_i_{e.name}", [P, T], I32)
    num = c.sb(ctx, f"num_{e.name}", [P, T])
    upto = c.sb(ctx, f"upto_{e.name}", [P, T])
    first = c.sb(ctx, f"first_{e.name}", [P, T])
    gt = c.sb(ctx, f"gt_{e.name}", [1, e.groups])
    fill = c.sb(ctx, f"fill_{e.name}", [P, e.tiles, 4])
    ps = c.bank[:, 0:2, :]
    loaded = c.sem(ctx, f"edges_loaded_{e.name}")
    step = c.sem(ctx, f"rank_step_{e.name}")
    counted = c.sem(ctx, f"counted_{e.name}")
    summed = c.sem(ctx, f"count_summed_{e.name}")
    empty = c.sem(ctx, f"empty_slots_{e.name}")
    met = c.met

    @block.sync
    def _(sp):
        sp.dma_start(key[0:n, :], e.key.rearrange("(p j) -> p j", p=n)).then_inc(loaded, 16)
        sp.dma_start(val[0:n, :], e.val.rearrange("(p j) -> p j", p=n)).then_inc(loaded, 16)
        if e.payload is not None:
            w = e.payload.shape[1] if len(e.payload.shape) == 2 else 1
            src = e.payload.rearrange("(p j) w -> p j w", p=n) if w > 1 else \
                e.payload.rearrange("(p j w) -> p j w", p=n, w=1)
            sp.dma_start(pay[0:n, :, 0:w] if w > 1 else pay[0:n, :, 0:1], src).then_inc(loaded, 16)
        sp.wait_ge(empty, 1)
        sp.dma_start(e.slots.rearrange("(p t) w -> p (t w)", p=P), fill[:].rearrange("p t w -> p (t w)"))\
          .then_inc(e.filled, 16)
        sp.wait_ge(e.filled, 16)
        meet(sp, met, met_n)

    @block.scalar
    def _(act):
        meet(act, met, met_n)

    @block.tensor
    def _(pe):
        pe.wait_ge(counted, 1)
        pe.matmul(ps[:, 0, 0:T], c.ones[0:n, 0:P], cnt[0:n, :], start=True, stop=True)
        pe.matmul(ps[0:n, 1, 0:T], c.before[0:n, 0:n], cnt[0:n, :], start=True, stop=True).then_inc(summed, 1)
        meet(pe, met, met_n)

    @block.vector
    def _(dve):
        ch = Chain(dve, step)
        ch.then(dve.memset(fill[:], 0.0))
        ch.then(dve.memset(fill[:, :, 1:2], -1.0))
        dve.sem_inc(empty, 1)
        payload_dmas = 0 if e.payload is None else 1
        dve.wait_ge(loaded, 32 + 16 * payload_dmas)
        ch.then(dve.tensor_copy(e.rec[0:n, :, 0:1].bitcast(I32).rearrange("p j o -> p (j o)"), val[0:n, :]))
        ch.then(dve.memset(e.rec[0:n, :, 2:4], 0.0))
        if e.payload is not None:
            w = e.payload.shape[1] if len(e.payload.shape) == 2 else 1
            ch.then(dve.tensor_copy(e.rec[0:n, :, 2:2 + w], pay[0:n, :, 0:w]))
        ch.then(dve.tensor_scalar(hi_i[0:n, :], key[0:n, :], 7, None, ALU.logical_shift_right))
        ch.then(dve.tensor_copy(hi[0:n, :], hi_i[0:n, :]))
        ch.then(dve.tensor_scalar(hi_i[0:n, :], key[0:n, :], P - 1, None, ALU.bitwise_and))
        ch.then(dve.tensor_copy(e.rec[0:n, :, 1:2].rearrange("p j o -> p (j o)"), hi_i[0:n, :]))
        def count(b, place, order):
            dve.wait_ge(step, order)
            dve.tensor_scalar(one_hot[0:n, place, :], hi[0:n, :], c.iota[0:n, ds(b, 1)], 0.0, ALU.is_equal,
                              ALU.add, accum_out=cnt[0:n, ds(b, 1)]).then_inc(step, 1)

        with dve.Fori(0, T // 2) as i:
            for k in range(2):
                count(i * 2 + k, k, i * 2 + (ch.n + k - 1))
        count(T - 1, 0, ch.n + T - 2)
        ch.n += T
        dve.wait_ge(step, ch.n)
        dve.sem_inc(counted, 1)
        dve.wait_ge(summed, 1)
        ch.then(dve.tensor_scalar(num_i[:], ps[:, 0, 0:T], float(GROUP - 1), None, ALU.add))
        ch.then(dve.tensor_scalar(num_i[:], num_i[:], GROUP.bit_length() - 1, None, ALU.logical_shift_right))
        ch.then(dve.tensor_copy(num[:], num_i[:]))
        ch.then(dve.tensor_tensor_scan(upto[:], c.ones[:, 0:T], num[:], 0.0, ALU.mult, ALU.add))
        ch.then(dve.tensor_tensor(first[:], upto[:], num[:], ALU.subtract))
        ch.then(dve.tensor_scalar(first[:], first[:], float(GROUP), -1.0, ALU.mult, ALU.add))
        ch.then(dve.tensor_tensor(first[0:n, :], first[0:n, :], ps[0:n, 1, 0:T], ALU.add))
        ch.then(dve.memset(gt[:], 0.0))
        with dve.Fori(0, T) as b:
            ch.then(dve.scalar_tensor_tensor(gt[:], c.iota[0:1, 0:e.groups], upto[0:1, ds(b, 1)], gt[:],
                                             ALU.is_ge, ALU.add), b)
        ch.n += T - 1
        ch.then(dve.tensor_scalar(e.group_tile[:], gt[:], float(T - 1), None, ALU.min))
        ch.then(dve.memset(pos[0:n, :], 0.0))
        def find(b, places, done):
            w = len(places)
            for k in places:
                dve.wait_ge(step, done + (k - w - 1))
                dve.tensor_scalar(one_hot[0:n, k, :], hi[0:n, :], c.iota[0:n, ds(b + k, 1)], None,
                                  ALU.is_equal).then_inc(step, 1)
            for k in places:
                dve.wait_ge(step, done + (k + 1))
                dve.tensor_tensor_scan(seen[0:n, k, :], c.ones[0:n, 0:J], one_hot[0:n, k, :],
                                       first[0:n, ds(b + k, 1)], ALU.mult, ALU.add).then_inc(step, 1)
            for k in places:
                dve.wait_ge(step, done + (w + k + 1))
                dve.tensor_tensor(seen[0:n, k, :], seen[0:n, k, :], one_hot[0:n, k, :], ALU.mult).then_inc(step, 1)
            for k in places:
                dve.wait_ge(step, done + (2 * w + k + 1 if k == 0 else 3 * w + k))
                dve.tensor_tensor(pos[0:n, :], pos[0:n, :], seen[0:n, k, :], ALU.add).then_inc(step, 1)

        with dve.Fori(0, T // 2) as i:
            find(i * 2, (0, 1), i * 8 + ch.n)
        ch.n += 4 * (T - 1)
        dve.wait_ge(step, ch.n)
        find(T - 1, (0,), ch.n)
        ch.n += 4
        dve.wait_ge(step, ch.n)
        ch.then(dve.tensor_copy(e.rows[0:n, :], pos[0:n, :]))
        ch.then(dve.tensor_scalar(hi_i[0:n, :], e.rows[0:n, :], P - 1, None, ALU.bitwise_and))
        ch.then(dve.tensor_scalar(e.rows[0:n, :], e.rows[0:n, :], 7, None, ALU.logical_shift_right))
        ch.then(dve.tensor_copy(posf[0:n, :], e.rows[0:n, :]))
        ch.then(dve.scalar_tensor_tensor(e.rows[0:n, :], hi_i[0:n, :], float(e.tiles), posf[0:n, :],
                                         ALU.mult, ALU.add))
        dve.sem_inc(e.ranked, 1)
        meet(dve, met, met_n)


def scatter_records(c, block, ctx, e):
    n = e.parts
    idx = c.sb(ctx, f"scatter_idx_{e.name}", [P, RING], I32)
    rec = c.sb(ctx, f"scatter_rec_{e.name}", [P, RING, 4])
    staged = c.sem(ctx, f"record_staged_{e.name}")
    turns = c.sem(ctx, f"scatter_turns_{e.name}")
    moved = [c.sem(ctx, f"records_moved_{e.name}_{k}") for k in range(RING)]

    @block.gpsimd
    def _(pool):
        pool.wait_ge(e.ranked, 1)
        pool.wait_ge(e.filled, 16)

        def round_of(i, first):
            for h in range(2):
                if not first:
                    for k in range(HALF * h, HALF * h + HALF):
                        pool.wait_ge(moved[k], i * 16)
                at = HALF * h
                pool.tensor_copy(idx[0:n, at:at + HALF], e.rows[0:n, ds(i * RING + at, HALF)]).then_inc(staged, 1)
                pool.tensor_copy(rec[0:n, at:at + HALF, :], e.rec[0:n, ds(i * RING + at, HALF), :])\
                    .then_inc(staged, 1)
                pool.wait_ge(staged, i * 4 + 2 * h + 2)
                pool.sem_inc(turns, 1)
                for k in range(at, at + HALF):
                    pool.indirect_dma_start(e.slots, bass.IndirectOffsetOnAxis(idx[0:n, k:k + 1], 0),
                                            rec[0:n, k, :], None).then_inc(moved[k], 16)

        round_of(0, True)
        with pool.Fori(1, e.per // RING) as i:
            round_of(i, False)
        for k in range(RING):
            pool.wait_ge(moved[k], 16 * (e.per // RING))




def norm_stage(c, block, ctx, name, met_n, first, rows=None):
    X = c.X
    stats = c.sb(ctx, f"stats_{name}", [P, T, 6])
    mv = c.sb(ctx, f"mean_var_{name}", [P, T, 2])
    var = c.sb(ctx, f"var_{name}", [P, T])
    rstd = c.sb(ctx, f"rstd_{name}", [P, T])
    scale = c.sb(ctx, f"scale_{name}", [P, T])
    gain = c.sb(ctx, f"gain_{name}", [P, T])
    shift = c.sb(ctx, f"shift_{name}", [P, T])
    sd = c.sb(ctx, f"sd_{name}", [P, T])
    xn = c.sb(ctx, f"xn_{name}", [P, 1, D])
    xn2 = c.sb(ctx, f"xn2_{name}", [P, 1, D])
    bufs = [xn, xn2]
    ps = [c.bank[:, k, 0:KD * P].rearrange("p (h n) -> p h n", h=KD) for k in range(2)]
    step = c.sem(ctx, f"norm_step_{name}")
    var_ready = c.sem(ctx, f"var_ready_{name}")
    root_ready = c.sem(ctx, f"root_ready_{name}")
    normed = c.sem(ctx, f"normed_{name}")
    turned = c.sem(ctx, f"turned_{name}")
    copied = c.sem(ctx, f"turned_copied_{name}")
    kept = c.sem(ctx, f"residual_kept_{name}")
    met = c.met
    pairs = T // 2

    @block.vector
    def _(dve):
        ch = Chain(dve, step)
        with dve.Fori(0, T) as t:
            dve.bn_stats(stats[:, ds(t, 1), :].rearrange("p a d -> p (a d)"),
                         X[:, ds(t, 1), :].rearrange("p a d -> p (a d)")).then_inc(step, 1)
        ch.n += T
        dve.wait_ge(step, ch.n)
        for t in range(T):
            dve.bn_aggr(mv[:, t, :], stats[:, t, :]).then_inc(step, 1)
        ch.n += T
        dve.wait_ge(step, ch.n)
        ch.then(dve.tensor_scalar(var[:], mv[:, :, 1], 1e-5, None, ALU.add))
        dve.sem_inc(var_ready, 1)
        dve.wait_ge(root_ready, 1)
        ch.then(dve.reciprocal(rstd[:], sd[:]))
        if first:
            ch.then(dve.tensor_tensor(scale[:], rstd[:], rstd[:], ALU.mult))
            ch.then(dve.tensor_tensor(scale[:], scale[:], mv[:, :, 1], ALU.mult))
            ch.then(dve.tensor_scalar(var[:], scale[:], float(D), None, ALU.mult))
            dve.sem_inc(var_ready, 1)
            dve.wait_ge(root_ready, 2)
            ch.then(dve.tensor_scalar(sd[:], sd[:], 1e-12, 1.0 / D ** 0.5, ALU.max, ALU.mult))
            ch.then(dve.tensor_copy(c.row_norm[:], sd[:]))
            ch.then(dve.reciprocal(scale[:], sd[:]))
            ch.then(dve.tensor_tensor(scale[:], scale[:], rstd[:], ALU.mult))
            ch.then(dve.tensor_scalar(gain[:], rstd[:], 1.0, None, ALU.add))
            ch.then(dve.tensor_tensor(shift[:], rstd[:], mv[:, :, 0], ALU.mult))
        else:
            ch.then(dve.tensor_copy(scale[:], rstd[:]))

        def tile(t, k, order):
            dve.wait_ge(turned, order)
            dve.tensor_scalar(bufs[k][:, 0, :], X[:, ds(t, 1), :].rearrange("p a d -> p (a d)"),
                              mv[:, ds(t, 1), 0:1].rearrange("p a b -> p (a b)"), scale[:, ds(t, 1)],
                              ALU.subtract, ALU.mult).then_inc(normed, 1)
            if rows is not None:
                dve.tensor_scalar(rows[:, ds(t, 1), :].rearrange("p a d -> p (a d)"),
                                  X[:, ds(t, 1), :].rearrange("p a d -> p (a d)"),
                                  mv[:, ds(t, 1), 0:1].rearrange("p a b -> p (a b)"), scale[:, ds(t, 1)],
                                  ALU.subtract, ALU.mult)
            if first:
                dve.wait_ge(normed, order)
                dve.tensor_scalar(X[:, ds(t, 1), :].rearrange("p a d -> p (a d)"),
                                  X[:, ds(t, 1), :].rearrange("p a d -> p (a d)"),
                                  gain[:, ds(t, 1)], shift[:, ds(t, 1)], ALU.mult, ALU.subtract)\
                    .then_inc(kept, 1)

        with dve.Fori(0, pairs) as i:
            for k in range(2):
                tile(i * 2 + k, k, i * 2 + k + 1)
        tile(T - 1, 0, T)
        meet(dve, met, met_n)

    @block.tensor
    def _(pe):
        pe.sem_inc(turned, 2)

        def tile(k, order):
            pe.wait_ge(normed, order)
            pe.wait_ge(copied, order)
            for h in range(KD):
                mm = pe.transpose(ps[k][:, h, :], bufs[k][:, 0, h * P:(h + 1) * P], c.ident[:])
            mm.then_inc(turned, 1)

        with pe.Fori(0, pairs) as i:
            for k in range(2):
                tile(k, i * 2 + k + 1)
        tile(0, T)
        meet(pe, met, met_n)

    @block.scalar
    def _(act):
        act.wait_ge(var_ready, 1)
        act.activation(sd[:], var[:], ACT.Sqrt).then_inc(root_ready, 1)
        if first:
            act.wait_ge(var_ready, 2)
            act.activation(sd[:], var[:], ACT.Sqrt).then_inc(root_ready, 1)
        act.sem_inc(copied, 2)

        def tile(t, k, order):
            act.wait_ge(turned, order + 2)
            act.copy(c.xT[:, :, ds(t * P, P)], ps[k][:, :, :]).then_inc(copied, 1)

        with act.Fori(0, pairs) as i:
            for k in range(2):
                tile(i * 2 + k, k, i * 2 + k + 1)
        tile(T - 1, 0, T)
        meet(act, met, met_n)

    @block.sync
    def _(sp):
        meet(sp, met, met_n)




HEADS0, DH0, MEM = 4, 32, 4
HID0 = HEADS0 * DH0


def mix0_stage(c, block, ctx, met_n):
    nc, a = c.nc, c.a
    TM = T + 1
    wg = c.sb(ctx, "w_gnn0", [P, KD, D])
    wq = c.sb(ctx, "w_qkv0", [P, KD, 3 * HID0])
    wo = c.sb(ctx, "w_out0", [P, D])
    g_pre = c.sb(ctx, "g_pre0", [P, KD])
    row = c.sb(ctx, "rows0", [P, 3, D])
    qkv = c.sb(ctx, "qkv0", [P, TM, 3 * HID0])
    sup = c.sb(ctx, "support_ring", [P, 2, D])
    y = c.sb(ctx, "y0", [P, T, D])
    scr = c.sb(ctx, "square0", [P, D])
    k_top = c.sb(ctx, "k_top", [P, HID0])
    k_max = c.sb(ctx, "k_max", [P, 1])
    k_diag = c.sb(ctx, "k_diag", [P, HID0])
    off = c.sb(ctx, "k_off", [P, 2])
    q_max = c.sb(ctx, "q_max", [P, T * HEADS0])
    q_sum = c.sb(ctx, "q_sum", [P, T * HEADS0])
    inv_k = c.sb(ctx, "inv_k", [P, 1])
    ctx_t = c.sb(ctx, "context_t", [P, HID0])
    mat = c.sb(ctx, "context_out", [P, D])
    q_t = c.sb(ctx, "q_t", [P, 2, P])
    ss = c.sb(ctx, "y_square", [P, T])
    rn = c.sb(ctx, "y_norm", [P, T])
    in_w = c.sem(ctx, "mix0_loaded")
    mem_zero = c.sem(ctx, "mem_zeroed")
    step = c.sem(ctx, "mix0_step")
    sup_ready = c.sem(ctx, "support_ready")
    sup_out = c.sem(ctx, "support_evacuated")
    sup_stored = [c.sem(ctx, f"support_stored_{k}") for k in range(2)]
    qkv_ready = c.sem(ctx, "qkv_ready")
    qkv_out = c.sem(ctx, "qkv_evacuated")
    scaled = c.sem(ctx, "g_pre_applied")
    top_ready, top_t, diag_ready, top_bc = (c.sem(ctx, f"k_top_{s}") for s in ("ready", "t", "diag", "bc"))
    k_shift, k_exp, q_shift, q_exp = (c.sem(ctx, s) for s in ("k_shifted", "k_exped", "q_shifted", "q_exped"))
    ctx_ready, ctx_out, mat_ready, mat_out = (c.sem(ctx, s) for s in ("ctx_ready", "ctx_out", "mat_ready", "mat_out"))
    q_ready, q_turned, q_copied, y_ready, y_out = \
        (c.sem(ctx, s) for s in ("q_ready", "q_turned", "q_copied", "y0_ready", "y0_out"))
    ss_ready, ss_root = c.sem(ctx, "ss_ready"), c.sem(ctx, "ss_root")
    met = c.met
    q, k, v = (qkv[:, :, i * HID0:(i + 1) * HID0] for i in range(3))

    @block.sync
    def _(sp):
        sp.dma_start(wg[:], a["gnn0_w"].rearrange("(k p) n -> p k n", p=P)).then_inc(in_w, 16)
        sp.dma_start(wq[:], a["qkv0_w"].rearrange("(k p) n -> p k n", p=P)).then_inc(in_w, 16)
        sp.dma_start(wo[:], a["out0_w"]).then_inc(in_w, 16)
        sp.dma_start(g_pre[:], a["g_pre0"]).then_inc(in_w, 16)
        for i, name in enumerate(("b_out0", "g_out0", "gnn0_b")):
            sp.dma_start(row[:, i, :], a[name].partition_broadcast(P)).then_inc(in_w, 16)
        sp.wait_ge(mem_zero, 1)
        for i in range(2):
            sp.dma_start(qkv[0:MEM, T, (1 + i) * HID0:(2 + i) * HID0], a["mem0"][i]).then_inc(in_w, 16)
        for t in range(T):
            sp.wait_ge(sup_out, t + 1)
            sp.dma_start(c.support[t * P:(t + 1) * P, :], sup[:, t % 2, :]).then_inc(sup_stored[t % 2], 16)
        sp.wait_ge(sup_stored[0], 16 * (-(-T // 2)))
        sp.wait_ge(sup_stored[1], 16 * (T // 2))
        meet(sp, met, met_n)

    @block.tensor
    def _(pe):
        pe.wait_ge(in_w, 16 * 9)
        pe.wait_ge(scaled, 1)
        for t in range(T):
            if t >= 2:
                pe.wait_ge(sup_out, t - 1)
                pe.wait_ge(qkv_out, t - 1)
            for kk in range(KD):
                mm = pe.matmul(c.bank[:, t % 2, 0:D], c.xT[:, kk, t * P:(t + 1) * P], wg[:, kk, :],
                               start=kk == 0, stop=kk == KD - 1)
            mm.then_inc(sup_ready, 1)
            for kk in range(KD):
                mm = pe.matmul(c.bank[:, 2 + t % 2, 0:3 * HID0], c.xT[:, kk, t * P:(t + 1) * P], wq[:, kk, :],
                               start=kk == 0, stop=kk == KD - 1)
            mm.then_inc(qkv_ready, 1)
        pe.wait_ge(top_ready, 1)
        pe.transpose(c.bank[:, 4, 0:P], k_top[:], c.ident[:]).then_inc(top_t, 1)
        pe.wait_ge(diag_ready, 1)
        pe.matmul(c.bank[:, 5, 0:HID0], c.ones[:, 0:P], k_diag[:], start=True, stop=True).then_inc(top_bc, 1)
        pe.wait_ge(k_exp, 1)
        for t in range(TM):
            pe.matmul(c.bank[:, 6, 0:HID0], v[:, t, :], k[:, t, :], start=t == 0, stop=t == TM - 1)
            mm = pe.matmul(c.bank[:, 7, 0:1], k[:, t, :], c.ones[:, 0:1], start=t == 0, stop=t == TM - 1)
        mm.then_inc(ctx_ready, 1)
        pe.wait_ge(ctx_out, 1)
        pe.matmul(c.bank[:, 4, 0:D], ctx_t[:], wo[:], start=True, stop=True).then_inc(mat_ready, 1)
        pe.wait_ge(q_ready, 1)
        pe.wait_ge(mat_out, 1)
        for t in range(T + 1):
            if t < T:
                if t >= 2:
                    pe.wait_ge(q_copied, t - 1)
                pe.transpose(c.bank[:, t % 2, 0:P], q[:, t, :], c.ident[:]).then_inc(q_turned, 1)
            if t >= 1:
                pe.wait_ge(q_copied, t)
                if t >= 3:
                    pe.wait_ge(y_out, t - 2)
                pe.matmul(c.bank[:, 2 + (t - 1) % 2, 0:D], q_t[:, (t - 1) % 2, :], mat[:],
                          start=True, stop=True).then_inc(y_ready, 1)
        meet(pe, met, met_n)

    @block.scalar
    def _(act):
        for t in range(T):
            act.wait_ge(qkv_ready, t + 1)
            act.copy(qkv[:, t, :], c.bank[:, 2 + t % 2, 0:3 * HID0]).then_inc(qkv_out, 1)
        act.wait_ge(k_shift, 1)
        act.activation(k, k, ACT.Exp).then_inc(k_exp, 1)
        act.wait_ge(q_shift, 1)
        act.activation(q[:, 0:T, :], q[:, 0:T, :], ACT.Exp).then_inc(q_exp, 1)
        for t in range(T):
            act.wait_ge(q_turned, t + 1)
            if t >= 2:
                act.wait_ge(y_ready, t - 1)
            act.copy(q_t[:, t % 2, :], c.bank[:, t % 2, 0:P]).then_inc(q_copied, 1)
        act.wait_ge(ss_ready, 1)
        act.activation(rn[:], ss[:], ACT.Sqrt).then_inc(ss_root, 1)
        meet(act, met, met_n)

    @block.vector
    def _(dve):
        ch = Chain(dve, step)
        dve.memset(qkv[:, T, :], 0.0).then_inc(mem_zero, 1)
        ch.then(dve.tensor_scalar(off[:, 0:1], c.part[:], float(LAST), NEG, ALU.is_ge, ALU.mult))
        ch.then(dve.tensor_scalar(off[:, 1:2], c.part[:], float(MEM), NEG, ALU.is_ge, ALU.mult))
        dve.wait_ge(in_w, 16 * 9)
        for kk in range(KD):
            ch.then(dve.tensor_scalar(wq[:, kk, :], wq[:, kk, :], g_pre[:, kk:kk + 1], None, ALU.mult))
        dve.sem_inc(scaled, 1)
        for t in range(T):
            dve.wait_ge(sup_ready, t + 1)
            if t >= 2:
                dve.wait_ge(sup_stored[t % 2], 16 * (t // 2))
            dve.tensor_scalar(sup[:, t % 2, :], c.bank[:, t % 2, 0:D], c.row_norm[:, t:t + 1], None, ALU.mult)\
                .then_inc(sup_out, 1)
        dve.wait_ge(qkv_out, T)
        ch.then(dve.tensor_scalar(k[:, T - 1, :], k[:, T - 1, :], off[:, 0:1], None, ALU.add))
        ch.then(dve.tensor_scalar(k[:, T, :], k[:, T, :], off[:, 1:2], None, ALU.add))
        dve.tensor_reduce(k_top[:], k.rearrange("p t c -> p c t"), AX.X, ALU.max).then_inc(top_ready, 1)
        dve.wait_ge(top_t, 1)
        ch.then(dve.tensor_reduce(k_max[:], c.bank[:, 4, 0:P], AX.X, ALU.max))
        dve.tensor_scalar(k_diag[:], c.ident[:], k_max[:], None, ALU.mult).then_inc(diag_ready, 1)
        dve.wait_ge(top_bc, 1)
        dve.tensor_tensor(k, k, c.bank[:, 5:6, 0:HID0].to_broadcast([P, TM, HID0]), ALU.subtract)\
            .then_inc(k_shift, 1)
        qh = q[:, 0:T, :].rearrange("p t (h d) -> p t h d", h=HEADS0)
        qs = [P, T, HEADS0, DH0]
        by_head = lambda b: b[:].rearrange("p (t h o) -> p t h o", h=HEADS0, o=1).to_broadcast(qs)
        ch.then(dve.tensor_reduce(q_max[:].rearrange("p (t h) -> p t h", h=HEADS0), qh, AX.X, ALU.max))
        dve.tensor_tensor(qh, qh, by_head(q_max), ALU.subtract).then_inc(q_shift, 1)
        dve.wait_ge(q_exp, 1)
        ch.then(dve.tensor_reduce(q_sum[:].rearrange("p (t h) -> p t h", h=HEADS0), qh, AX.X, ALU.add))
        ch.then(dve.reciprocal(q_sum[:], q_sum[:]))
        ch.then(dve.tensor_scalar(q_sum[:], q_sum[:], DH0 ** -0.5, None, ALU.mult))
        dve.tensor_tensor(qh, qh, by_head(q_sum), ALU.mult).then_inc(q_ready, 1)
        dve.wait_ge(ctx_ready, 1)
        ch.then(dve.reciprocal(inv_k[:], c.bank[:, 7, 0:1]))
        dve.tensor_tensor(ctx_t[:], c.bank[:, 6, 0:HID0], c.head32[:], ALU.mult).then_inc(ctx_out, 1)
        dve.wait_ge(mat_ready, 1)
        dve.tensor_scalar(mat[:], c.bank[:, 4, 0:D], inv_k[:], None, ALU.mult).then_inc(mat_out, 1)
        for t in range(T):
            dve.wait_ge(y_ready, t + 1)
            dve.tensor_tensor(y[:, t, :], c.bank[:, 2 + t % 2, 0:D], row[:, 0, :], ALU.add).then_inc(y_out, 1)
            dve.wait_ge(y_out, t + 1)
            ch.then(dve.scalar_tensor_tensor(scr[:], y[:, t, :], 1.0, y[:, t, :], ALU.mult, ALU.mult,
                                             accum_out=ss[:, t:t + 1]))
        dve.sem_inc(ss_ready, 1)
        dve.wait_ge(ss_root, 1)
        ch.then(dve.tensor_scalar(rn[:], rn[:], 1e-12, 1.0 / D ** 0.5, ALU.max, ALU.mult))
        ch.then(dve.reciprocal(rn[:], rn[:]))
        with dve.Fori(0, T) as t:
            flat = lambda b: b[:, ds(t, 1), :].rearrange("p a d -> p (a d)")
            ch.then(dve.scalar_tensor_tensor(flat(y), flat(y), rn[:, ds(t, 1)], row[:, 1, :],
                                             ALU.mult, ALU.mult), 3 * t)
            ch.then(dve.tensor_tensor(flat(y), flat(y), row[:, 2, :], ALU.add), 3 * t)
            ch.then(dve.tensor_tensor(flat(c.X), flat(c.X), flat(y), ALU.add), 3 * t)
        ch.n += 3 * (T - 1)
        meet(dve, met, met_n)




def load_slots(c, block, ctx, e):
    if e.slot is None:
        e.slot = c.sb(ctx, f"slot_{e.name}", [P, e.tiles, 4])
    e.slot_in = c.sem(ctx, f"slot_loaded_{e.name}")

    @block.sync
    def _(sp):
        sp.dma_start(e.slot[:].rearrange("p t w -> p (t w)"), e.slots.rearrange("(p t) w -> p (t w)", p=P))\
          .then_inc(e.slot_in, 16)


def tiles_of_groups(c, engine, e, first, n):
    return c.nc.values_load_multi_w_load_instructions(
        e.group_tile[0:1, ds(first, n)], engines=[engine], min_val=0, max_val=T - 1,
        skip_runtime_bounds_check_because="rank_stage clamps every entry to a tile's number")[1]


def one_hots_of_half(dve, c, e, hot, i, h):
    shape = [P, HALF, P]
    at = HALF * h
    return dve.tensor_tensor(hot[:, at:at + HALF, :], c.iota[:, 0:P].rearrange("p (o n) -> p o n", o=1).to_broadcast(shape),
                             e.slot[:, ds(i * RING + at, HALF), 1:2].to_broadcast(shape), ALU.is_equal)


def gather_rows(c, block, ctx, e, table, width, used):
    e.rows_in = c.sb(ctx, f"rows_{e.name}", [P, RING, width])
    idx = c.sb(ctx, f"gather_idx_{e.name}", [P, RING], I32)
    staged = c.sem(ctx, f"gather_idx_ready_{e.name}")
    turns = c.sem(ctx, f"gather_turns_{e.name}")
    e.gathered = [c.sem(ctx, f"gathered_{e.name}_{k}") for k in range(RING)]

    @block.gpsimd
    def _(pool):
        pool.wait_ge(e.slot_in, 16)
        with pool.Fori(0, e.tiles // RING) as i:
            for h in range(2):
                at = HALF * h
                pool.wait_ge(used, i * RING + at + HALF)
                pool.tensor_copy(idx[:, at:at + HALF],
                                 e.slot[:, ds(i * RING + at, HALF), 0:1].bitcast(I32).rearrange("p t o -> p (t o)"))\
                    .then_inc(staged, 1)
                pool.wait_ge(staged, i * 2 + h + 1)
                pool.sem_inc(turns, 1)
                for k in range(at, at + HALF):
                    pool.indirect_dma_start(e.rows_in[:, k, :], None, table, bass.IndirectOffsetOnAxis(idx[:, k:k + 1], 0))\
                        .then_inc(e.gathered[k], 16)


def sum0_stage(c, block, ctx, e):
    hot = c.sb(ctx, "one_hot0", [P, RING, P])
    used = c.sem(ctx, "rows_used0")
    hot_ready = c.sem(ctx, "one_hot_ready0")
    added = c.sem(ctx, "group_added0")
    gather_rows(c, block, ctx, e, c.support, D, used)
    steps = e.tiles // RING
    per = GROUP // P

    @block.tensor
    def _(pe):
        pe.sem_inc(used, RING)
        with pe.Fori(0, steps) as i:
            for k in range(RING):
                g = k // per
                pe.wait_ge(hot_ready, i * RING + k + 1)
                pe.wait_ge(e.gathered[k], i * 16 + 16)
                if k % per == 0:
                    pe.wait_ge(added, i * BODY_GROUPS + g + 1)
                pe.matmul(c.bank[:, g, 0:D], hot[:, k, :], e.rows_in[:, k, :], start=k % per == 0,
                          stop=k % per == per - 1).then_inc(used, 1)

    @block.vector
    def _(dve):
        dve.sem_inc(added, BODY_GROUPS)
        dve.wait_ge(e.slot_in, 16)

        def add_group(i, g):
            tile = dve.value_load(e.group_tile[0:1, ds(i * BODY_GROUPS + g, 1)], min_val=0, max_val=T - 1)
            dve.wait_ge(used, i * RING + RING + per * (g + 1))
            dve.wait_ge(added, i * BODY_GROUPS + BODY_GROUPS + g)
            x = c.X[:, ds(tile, 1), :].rearrange("p a d -> p (a d)")
            dve.tensor_tensor(x, c.bank[:, g, 0:D], x, ALU.add).then_inc(added, 1)

        with dve.Fori(0, steps) as i:
            for g in range(BODY_GROUPS + 2):
                if g < BODY_GROUPS:
                    for k in range(per * g, per * g + per):
                        dve.wait_ge(used, i * RING + k + 1)
                        col = lambda w: e.slot[:, ds(i * RING + k, 1), w:w + 1].rearrange("p t o -> p (t o)")
                        dve.tensor_scalar(hot[:, k, :], c.iota[:, 0:P], col(1), col(2), ALU.is_equal, ALU.mult)\
                            .then_inc(hot_ready, 1)
                if g >= 2:
                    add_group(i, g - 2)




CHUNK_TILES = 5
CHUNK = CHUNK_TILES * P
HALF_CHUNK = CHUNK // 2
CHUNKS = T // CHUNK_TILES


def top2_gates(c, dve, ch, ctx, name, logits, n, gates, to_exp, exped):
    s = [P, T, n]
    buf = lambda k, shape: c.sb(ctx, f"{k}_{name}", shape)
    rank, rest, eq, pick, sel = (buf(k, s) for k in ("rank", "rest", "equal", "pick", "sel"))
    top, best = buf("top", [P, T]), buf("best", [P, T])
    wide = lambda b: b[:].rearrange("p (t o) -> p t o", o=1).to_broadcast(s)
    ch.then(dve.tensor_scalar(rank[:], c.iota[:, 0:n].rearrange("p (o e) -> p o e", o=1).to_broadcast(s),
                              -1.0, float(n), ALU.mult, ALU.add))
    ch.then(dve.tensor_copy(rest[:], logits))
    for turn in range(2):
        ch.then(dve.tensor_reduce(top[:], rest[:], AX.X, ALU.max))
        if turn == 0:
            ch.then(dve.tensor_tensor(gates, logits, wide(top), ALU.subtract))
            dve.sem_inc(to_exp, 1)
            dve.wait_ge(exped, 1)
        ch.then(dve.tensor_tensor(eq[:], rest[:], wide(top), ALU.is_equal))
        ch.then(dve.tensor_tensor(eq[:], eq[:], rank[:], ALU.mult))
        ch.then(dve.tensor_reduce(best[:], eq[:], AX.X, ALU.max))
        ch.then(dve.tensor_tensor(pick[:], eq[:], wide(best), ALU.is_equal))
        if turn == 0:
            ch.then(dve.tensor_copy(sel[:], pick[:]))
            ch.then(dve.scalar_tensor_tensor(rest[:].rearrange("p t e -> p (t e)"), pick[:].rearrange("p t e -> p (t e)"),
                                             3.0e38, rest[:].rearrange("p t e -> p (t e)"), ALU.mult, ALU.subtract))
            ch.then(dve.tensor_scalar(rest[:], rest[:], -1.0, None, ALU.mult))
        else:
            ch.then(dve.tensor_tensor(sel[:], sel[:], pick[:], ALU.add))
    ch.then(dve.tensor_tensor(gates, gates, sel[:], ALU.mult))
    ch.then(dve.tensor_reduce(top[:], gates, AX.X, ALU.add))
    ch.then(dve.reciprocal(top[:], top[:]))
    ch.then(dve.tensor_tensor(gates, gates, wide(top), ALU.mult))
    return sel, pick


EXPERTS0, FF0 = 8, 1024
CHOSEN = 2
PAIRS0 = CHOSEN * N
GROUPS0 = up((PAIRS0 + EXPERTS0 * (GROUP - 1)) // GROUP, 2)
SLOTS0 = GROUPS0 * GROUP


def clear_slots0(c, block, ctx):
    zero = c.sb(ctx, "zero_rows", [P, 2048])
    zeroed = c.sem(ctx, "zero_rows_ready")
    rows = c.slot_x[0:SLOTS0, :].rearrange("(p r) d -> p (r d)", p=P)
    width = SLOTS0 // P * D

    @block.scalar
    def _(act):
        act.wait_ge(zeroed, 1)
        for at in range(0, width, 2048):
            act.dma_start(rows[:, at:at + 2048], zero[:]).then_inc(c.slots_cleared, 16)
        act.wait_ge(c.slots_cleared, 16 * (width // 2048))

    @block.vector
    def _(dve):
        dve.memset(zero[:], 0.0).then_inc(zeroed, 1)


def router0_stage(c, block, ctx, met_n):
    n = EXPERTS0
    s3 = [P, T, n]
    wr = c.sb(ctx, "w_router", [P, KD, n])
    gates = c.sb(ctx, "gates0", s3)
    slot = c.sb(ctx, "slot_of", s3)
    upto = c.sb(ctx, "taken_upto", s3)
    num_i = c.sb(ctx, "expert_groups_i", [P, n], I32)
    num = c.sb(ctx, "expert_groups", [P, n])
    last = c.sb(ctx, "expert_last", [P, n])
    first = c.sb(ctx, "expert_first", [P, n])
    real = c.sb(ctx, "real", [P, 2])
    at = c.sb(ctx, "slot_at", [P, T, CHOSEN])
    of = c.sb(ctx, "expert_of", [1, GROUPS0])
    loaded, ready, to_exp, exped, step, picked, ranked = (
        c.sem(ctx, f"router_{k}") for k in ("loaded", "logits", "shifted", "exped", "step", "picked", "counted"))
    met = c.met
    mask = [None]

    @block.vector
    def _(dve):
        ch = Chain(dve, step)
        dve.wait_ge(ready, 1)
        sel, pick = top2_gates(c, dve, ch, ctx, "0", c.bank[:, 0, 0:T * n].rearrange("p (t e) -> p t e", e=n), n,
                               gates[:], to_exp, exped)
        mask[0] = sel
        ch.then(dve.tensor_scalar(real[:, 0:1], c.part[:], float(LAST), None, ALU.is_lt))
        ch.then(dve.tensor_scalar(sel[:, T - 1, :], sel[:, T - 1, :], real[:, 0:1], None, ALU.mult))
        dve.sem_inc(picked, 1)
        dve.wait_ge(ranked, 1)
        total = c.bank[:, 1, 0:T * n].rearrange("p (t e) -> p t e", e=n)
        for e in range(n):
            ch.then(dve.tensor_tensor_scan(upto[:, :, e], c.ones[:, 0:T], total[:, :, e], 0.0, ALU.mult, ALU.add))
        ch.then(dve.tensor_scalar(num_i[:], upto[:, T - 1, :], float(GROUP - 1), None, ALU.add))
        ch.then(dve.tensor_scalar(num_i[:], num_i[:], GROUP.bit_length() - 1, None, ALU.logical_shift_right))
        ch.then(dve.tensor_copy(num[:], num_i[:]))
        ch.then(dve.tensor_tensor_scan(last[:], c.ones[:, 0:n], num[:], 0.0, ALU.mult, ALU.add))
        ch.then(dve.tensor_tensor(first[:], last[:], num[:], ALU.subtract))
        ch.then(dve.tensor_scalar(first[:], first[:], float(GROUP), None, ALU.mult))
        ch.then(dve.tensor_tensor(slot[:], upto[:], total, ALU.subtract))
        ch.then(dve.tensor_tensor(slot[:], slot[:], c.bank[:, 2, 0:T * n].rearrange("p (t e) -> p t e", e=n), ALU.add))
        ch.then(dve.tensor_tensor(slot[:], slot[:],
                                  first[:].rearrange("p (o e) -> p o e", o=1).to_broadcast(s3), ALU.add))
        ch.then(dve.memset(of[:], 0.0))
        for e in range(n):
            ch.then(dve.scalar_tensor_tensor(of[:], c.iota[0:1, 0:GROUPS0], last[0:1, e:e + 1], of[:],
                                             ALU.is_ge, ALU.add))
        ch.then(dve.tensor_scalar(c.group_expert[:], of[:], float(n - 1), None, ALU.min))
        ch.then(dve.tensor_scalar(pick[:, T - 1, :], pick[:, T - 1, :], real[:, 0:1], None, ALU.mult))
        for k in (1, 0):
            if k == 0:
                ch.then(dve.tensor_tensor(pick[:], sel[:], pick[:], ALU.subtract))
            ch.then(dve.tensor_tensor(upto[:], slot[:], pick[:], ALU.mult))
            ch.then(dve.tensor_reduce(at[:, :, k], upto[:], AX.X, ALU.add))
            ch.then(dve.tensor_tensor(upto[:], gates[:], pick[:], ALU.mult))
            ch.then(dve.tensor_reduce(c.gate_of[:, :, k], upto[:], AX.X, ALU.add))
        ch.then(dve.tensor_copy(c.slot_from[:], at[:]))
        ch.then(dve.tensor_scalar(real[:, 0:1], real[:, 0:1], -1.0, 1.0, ALU.mult, ALU.add))
        for k in range(CHOSEN):
            ch.then(dve.tensor_scalar(real[:, 1:2], c.part[:], float(SLOTS0 + k * P), real[:, 0:1], ALU.add, ALU.mult))
            ch.then(dve.tensor_scalar(at[:, T - 1, k:k + 1], at[:, T - 1, k:k + 1], real[:, 1:2], None, ALU.add))
        ch.then(dve.tensor_copy(c.slot_to[:], at[:]))
        dve.sem_inc(c.routed, 1)
        meet(dve, met, met_n)

    @block.sync
    def _(sp):
        sp.dma_start(wr[:], c.a["router0_w"].rearrange("(k p) n -> p k n", p=P)).then_inc(loaded, 16)
        meet(sp, met, met_n)

    @block.tensor
    def _(pe):
        pe.wait_ge(loaded, 16)
        for t in range(T):
            for k in range(KD):
                mm = pe.matmul(c.bank[:, 0, t * n:(t + 1) * n], c.xT[:, k, t * P:(t + 1) * P], wr[:, k, :],
                               start=k == 0, stop=k == KD - 1)
        mm.then_inc(ready, 1)
        pe.wait_ge(picked, 1)
        sel = mask[0][:].rearrange("p t e -> p (t e)")
        pe.matmul(c.bank[:, 1, 0:T * n], c.ones[:, 0:P], sel, start=True, stop=True)
        pe.matmul(c.bank[:, 2, 0:T * n], c.before[:], sel, start=True, stop=True).then_inc(ranked, 1)
        meet(pe, met, met_n)

    @block.scalar
    def _(act):
        act.wait_ge(to_exp, 1)
        act.activation(gates[:], gates[:], ACT.Exp).then_inc(exped, 1)
        meet(act, met, met_n)


def send_nodes0(c, block, ctx):
    sent = c.sem(ctx, "nodes_sent")

    @block.gpsimd
    def _(pool):
        pool.wait_ge(c.routed, 1)
        pool.wait_ge(c.slots_cleared, 16 * (SLOTS0 // P * D // 2048))
        for t in range(T):
            for k in range(CHOSEN):
                pool.indirect_dma_start(c.slot_x, bass.IndirectOffsetOnAxis(c.slot_to[:, t, k:k + 1], 0),
                                        c.XN[:, t, :], None).then_inc(sent, 16)
        pool.wait_ge(sent, 16 * T * CHOSEN)
        pool.sem_inc(c.sent_all, 1)


def fetch_outputs0(c, block, ctx):
    c.out_ring = c.sb(ctx, "expert_row_ring", [P, RING, D])
    c.ring_in = [c.sem(ctx, f"expert_row_in_{k}") for k in range(RING)]
    c.ring_used = c.sem(ctx, "expert_row_used")

    @block.gpsimd
    def _(pool):
        pool.wait_ge(c.outputs_stored, 1)
        for j in range(T * CHOSEN):
            if j >= RING:
                pool.wait_ge(c.ring_used, j - RING + 1)
            pool.indirect_dma_start(c.out_ring[:, j % RING, :], None, c.slot_y,
                                    bass.IndirectOffsetOnAxis(c.slot_from[:, j // CHOSEN, j % CHOSEN:j % CHOSEN + 1], 0))\
                .then_inc(c.ring_in[j % RING], 16)


def private_experts_stage(c, block, ctx, met_n):
    a, met, FC, SUB = c.a, c.met, FF0 // P, GROUP // P
    w1 = c.sb(ctx, "w1_private", [P, 2, KD, FF0])
    w2 = c.sb(ctx, "w2_private", [P, 2, FC, D])
    b1 = c.sb(ctx, "b1_private", [P, 2, FC])
    b2 = c.sb(ctx, "b2_private", [P, 2, D])
    rows = c.sb(ctx, "slot_rows", [P, 2, SUB, D])
    xT = c.sb(ctx, "slot_xT", [P, 2, KD, GROUP])
    hid = c.sb(ctx, "hidden_private", [P, FC, GROUP])
    y = c.sb(ctx, "slot_out", [P, 2, SUB, D])
    weights_in = [c.sem(ctx, f"weights_in_{k}") for k in range(2)]
    rows_in = [c.sem(ctx, f"slot_rows_in_{k}") for k in range(2)]
    stored = [c.sem(ctx, f"slot_out_stored_{k}") for k in range(2)]
    turned = c.sem(ctx, "slot_rows_turned")
    x_ready = c.sem(ctx, "slot_xT_ready")
    h_ready = c.sem(ctx, "hidden_ready_private")
    h_done = c.sem(ctx, "hidden_gelu_private")
    y_ready = c.sem(ctx, "out_ready_private")
    y_done = c.sem(ctx, "out_biased_private")
    pairs = GROUPS0 // 2

    @block.sync
    def _(sp):
        def load_rows(g, b):
            sp.dma_start(rows[:, b, :, :], c.slot_x[ds(g * GROUP, GROUP), :].rearrange("(j p) d -> p j d", p=P))\
                .then_inc(rows_in[b], 16)

        def load_weights(g, b):
            e = sp.value_load(c.group_expert[0:1, ds(g, 1)], min_val=0, max_val=EXPERTS0 - 1)
            sp.dma_start(w1[:, b, :, :], a["w1p"][ds(e, 1), :, :].rearrange("e (k p) f -> p (e k) f", p=P))\
                .then_inc(weights_in[b], 16)
            sp.dma_start(b1[:, b, :], a["b1_0"][:, ds(e * FC, FC)]).then_inc(weights_in[b], 16)
            sp.dma_start(b2[:, b, :], a["b2_0"][ds(e * D, D)].partition_broadcast(P)).then_inc(weights_in[b], 16)
            sp.dma_start(w2[:, b, :, :], a["w2p"][ds(e, 1), :, :].rearrange("e (f p) d -> p (e f) d", p=P))\
                .then_inc(weights_in[b], 16)

        def step(i, b, tail):
            g = i * 2 + b
            if not (tail and b == 1):
                sp.wait_ge(y_done, i * (2 * SUB) + (b * SUB + 2))
                load_weights(g + 1, 1 - b)
            if not tail:
                sp.wait_ge(turned, g + 1)
                load_rows(g + 2, b)
            sp.wait_ge(y_done, i * (2 * SUB) + (b + 1) * SUB + 2)
            sp.dma_start(c.slot_y[ds(g * GROUP, GROUP), :].rearrange("(j p) d -> p j d", p=P), y[:, b, :, :])\
                .then_inc(stored[b], 16)

        load_weights(0, 0)
        sp.wait_ge(c.sent_all, 1)
        load_rows(0, 0)
        load_rows(1, 1)
        with sp.Fori(0, pairs - 1) as i:
            step(i, 0, False)
            step(i, 1, False)
        step(pairs - 1, 0, True)
        step(pairs - 1, 1, True)
        for b in range(2):
            sp.wait_ge(stored[b], 16 * pairs + 16)
        sp.sem_inc(c.outputs_stored, 1)
        meet(sp, met, met_n)

    @block.tensor
    def _(pe):
        def turn(i, b):
            pe.wait_ge(rows_in[b], i * 16 + 16)
            pe.wait_ge(x_ready, i * 2 + b + 1)
            for j in range(SUB):
                for k in range(KD):
                    mm = pe.transpose(c.bank[:, 4 + b, k * GROUP + j * P:k * GROUP + (j + 1) * P],
                                      rows[:, b, j, k * P:(k + 1) * P], c.ident[:])
            mm.then_inc(turned, 1)

        def group(i, b, tail):
            pe.wait_ge(x_ready, i * 2 + b + 3)
            pe.wait_ge(weights_in[b], i * 64 + 64)
            for f in range(FC):
                pe.wait_ge(h_done, i * (2 * FC) + (b * FC + f + 1))
                for k in range(KD):
                    mm = pe.matmul(c.bank[:, f % 4, 0:GROUP], w1[:, b, k, f * P:(f + 1) * P], xT[:, b, k, :],
                                   start=k == 0, stop=k == KD - 1)
                mm.then_inc(h_ready, 1)
            if not (tail and b == 1):
                turn(i + b, 1 - b)
            for j in range(SUB):
                pe.wait_ge(y_done, i * (2 * SUB) + (b * SUB + j + 1))
                for f in range(FC):
                    if j == 0:
                        pe.wait_ge(h_done, i * (2 * FC) + (b * FC + f + 1 + 4))
                    mm = pe.matmul(c.bank[:, 6 + j, 0:D], hid[:, f, j * P:(j + 1) * P], w2[:, b, f, :],
                                   start=f == 0, stop=f == FC - 1)
                mm.then_inc(y_ready, 1)

        turn(0, 0)
        with pe.Fori(0, pairs - 1) as i:
            group(i, 0, False)
            group(i, 1, False)
        group(pairs - 1, 0, True)
        group(pairs - 1, 1, True)
        meet(pe, met, met_n)

    @block.scalar
    def _(act):
        act.sem_inc(h_done, 4)
        act.sem_inc(y_ready, 1)
        with act.Fori(0, pairs) as i:
            for b in range(2):
                act.wait_ge(weights_in[b], i * 64 + 64)
                act.wait_ge(y_ready, i * (2 * SUB) + (b * SUB + 1))
                for f in range(FC):
                    act.wait_ge(h_ready, i * (2 * FC) + (b * FC + f + 1))
                    act.activation(hid[:, f, :], c.bank[:, f % 4, 0:GROUP], ACT.Gelu, bias=b1[:, b, f:f + 1])\
                       .then_inc(h_done, 1)
        meet(act, met, met_n)

    @block.vector
    def _(dve):
        dve.sem_inc(x_ready, 2)
        dve.sem_inc(y_done, 2)
        dve.sem_inc(stored[0], 16)
        dve.sem_inc(stored[1], 16)

        def copy_xT(i, b):
            dve.wait_ge(turned, i * 2 + b + 1)
            dve.tensor_copy(xT[:, b, :, :].rearrange("p k n -> p (k n)"), c.bank[:, 4 + b, :]).then_inc(x_ready, 1)

        def group(i, b, tail):
            if not (tail and b == 1):
                copy_xT(i + b, 1 - b)
            dve.wait_ge(stored[b], i * 16 + 16)
            for j in range(SUB):
                dve.wait_ge(y_ready, i * (2 * SUB) + (b * SUB + j + 1 + 1))
                dve.tensor_tensor(y[:, b, j, :], c.bank[:, 6 + j, 0:D], b2[:, b, :], ALU.add).then_inc(y_done, 1)

        copy_xT(0, 0)
        with dve.Fori(0, pairs - 1) as i:
            group(i, 0, False)
            group(i, 1, False)
        group(pairs - 1, 0, True)
        group(pairs - 1, 1, True)
        for j in range(T * CHOSEN):
            dve.wait_ge(c.ring_in[j % RING], 16 * (j // RING + 1))
            if j >= 1:
                dve.wait_ge(c.ring_used, j)
            x = c.X[:, j // CHOSEN, :]
            dve.scalar_tensor_tensor(x, c.out_ring[:, j % RING, :], c.gate_of[:, j // CHOSEN, j % CHOSEN:j % CHOSEN + 1],
                                     x, ALU.mult, ALU.add).then_inc(c.ring_used, 1)
        meet(dve, met, met_n)


def experts_stage(c, block, ctx, name, met_n, F, experts, b1_rows, b2_rows, gates):
    E, FC = len(experts), F // P
    w1 = c.sb(ctx, f"w1_{name}", [P, 2, KD, F])
    w2 = c.sb(ctx, f"w2_{name}", [P, 2, FC, D])
    b1 = c.sb(ctx, f"b1_{name}", [P, E * FC])
    b2 = c.sb(ctx, f"b2_{name}", [P, E, D])
    hid = c.sb(ctx, f"hidden_{name}", [P, FC, 2, HALF_CHUNK])
    part = c.sb(ctx, f"expert_out_{name}", [P, 2, D])
    biases = c.sem(ctx, f"biases_loaded_{name}")
    loaded = [c.sem(ctx, f"expert_loaded_{name}_{k}") for k in range(2)]
    h_ready = c.sem(ctx, f"hidden_ready_{name}")
    h_done = c.sem(ctx, f"hidden_gelu_{name}")
    y_ready = c.sem(ctx, f"out_ready_{name}")
    y_done = c.sem(ctx, f"out_added_{name}")
    biased = c.sem(ctx, f"out_biased_{name}")
    met = c.met
    since = {0: 1, 4: 4}

    @block.sync
    def _(sp):
        sp.dma_start(b1[:], b1_rows).then_inc(biases, 16)
        sp.dma_start(b2[:].rearrange("p e d -> p (e d)"), b2_rows.partition_broadcast(P)).then_inc(biases, 16)
        for e, (W1, W2) in enumerate(experts):
            if e >= 2:
                sp.wait_ge(y_ready, (e - 1) * T)
            sp.dma_start(w1[:, e % 2, :, :], W1.rearrange("(k p) f -> p k f", p=P)).then_inc(loaded[e % 2], 16)
            sp.dma_start(w2[:, e % 2, :, :], W2.rearrange("(f p) d -> p f d", p=P)).then_inc(loaded[e % 2], 16)
        meet(sp, met, met_n)

    @block.tensor
    def _(pe):
        for e in range(E):
            pe.wait_ge(loaded[e % 2], 32 * (e // 2 + 1))
            with pe.Fori(0, CHUNKS) as i:
                for f in range(FC):
                    pe.wait_ge(h_done, i * FC + (e * CHUNKS * FC + f + 1))
                    for half in range(2):
                        for k in range(KD):
                            mm = pe.matmul(c.bank[:, 2 * (f % 2) + half, 0:HALF_CHUNK],
                                           w1[:, e % 2, k, f * P:(f + 1) * P],
                                           c.xT[:, k, ds(i * CHUNK + half * HALF_CHUNK, HALF_CHUNK)],
                                           start=k == 0, stop=k == KD - 1)
                    mm.then_inc(h_ready, 1)
                for t in range(CHUNK_TILES):
                    pe.wait_ge(y_done, i * CHUNK_TILES + (e * T + t + 1 + CHUNK_TILES - since.get(t, 5)))
                    for f in range(FC):
                        if t == 0:
                            pe.wait_ge(h_done, i * FC + (e * CHUNKS * FC + f + 1 + 2))
                        mm = pe.matmul(c.bank[:, 4 + t % 4, 0:D],
                                       hid[:, f, :, :].rearrange("p a n -> p (a n)")[:, t * P:(t + 1) * P],
                                       w2[:, e % 2, f, :], start=f == 0, stop=f == FC - 1)
                    mm.then_inc(y_ready, 1)
        meet(pe, met, met_n)

    @block.scalar
    def _(act):
        act.wait_ge(biases, 32)
        act.sem_inc(h_done, 2)
        for e in range(E):
            with act.Fori(0, CHUNKS) as i:
                act.wait_ge(y_ready, i * CHUNK_TILES + e * T)
                for f in range(FC):
                    act.wait_ge(h_ready, i * FC + (e * CHUNKS * FC + f + 1))
                    act.activation(hid[:, f, :, :], c.bank[:, 2 * (f % 2):2 * (f % 2) + 2, 0:HALF_CHUNK],
                                   ACT.Gelu, bias=b1[:, e * FC + f:e * FC + f + 1]).then_inc(h_done, 1)
        meet(act, met, met_n)

    @block.vector
    def _(dve):
        dve.wait_ge(biases, 32)
        dve.sem_inc(y_done, CHUNK_TILES)
        for e in range(E):
            with dve.Fori(0, CHUNKS) as i:
                for t in range(CHUNK_TILES):
                    tile = i * CHUNK_TILES + t
                    x = c.X[:, ds(tile, 1), :].rearrange("p a d -> p (a d)")
                    gate = 1.0 if gates is None else gates[:, ds(tile, 1), e:e + 1].rearrange("p a b -> p (a b)")
                    dve.wait_ge(y_ready, tile + (e * T + 1))
                    dve.wait_ge(y_done, tile + (e * T + CHUNK_TILES))
                    dve.tensor_tensor(part[:, 0, :], c.bank[:, 4 + t % 4, 0:D], b2[:, e, :], ALU.add)\
                        .then_inc(biased, 1)
                    dve.wait_ge(biased, tile + (e * T + 1))
                    dve.scalar_tensor_tensor(x, part[:, 0, :], gate, x, ALU.mult, ALU.add).then_inc(y_done, 1)
        meet(dve, met, met_n)




HEADS1, FEAT = 4, 64
MSG = FEAT + HEADS1
AGG = HEADS1 * (FEAT + 1)
INNER = 512
KV_GROUPS = 2 * INNER // FEAT


def table1_stage(c, block, ctx, met_n):
    a = c.a
    w_all = c.sb(ctx, "w_all", [P, KD, 2 * MSG])
    w_nat = c.sb(ctx, "w_nat", [FEAT, 2, D])
    att = c.sb(ctx, "att1", [FEAT, HEADS1])
    rows = c.sb(ctx, "table1_rows", [P, T, 2 * MSG])
    loaded, folded, copied, ready, out, stored = (c.sem(ctx, f"table1_{k}") for k in
                                                  ("loaded", "folded", "copied", "ready", "evacuated", "stored"))
    met = c.met

    @block.sync
    def _(sp):
        for i, d in enumerate(("wf", "wr")):
            sp.dma_start(w_all[:, :, i * MSG:i * MSG + FEAT], a[d + "_t"].rearrange("(k p) n -> p k n", p=P))\
              .then_inc(loaded, 16)
            sp.dma_start(w_nat[:, i, :], a[d]).then_inc(loaded, 16)
        sp.dma_start(att[:], a["att1_t"]).then_inc(loaded, 16)
        sp.wait_ge(out, T)
        sp.dma_start(c.table1.rearrange("(t p) w -> p t w", p=P), rows[:]).then_inc(stored, 16)
        sp.wait_ge(stored, 16)
        meet(sp, met, met_n)

    @block.tensor
    def _(pe):
        pe.wait_ge(loaded, 16 * 5)
        for i in range(2):
            for k in range(KD):
                mm = pe.matmul(c.bank[:, 7, (2 * i + k) * HEADS1:(2 * i + k + 1) * HEADS1],
                               w_nat[:, i, k * P:(k + 1) * P], att[:], start=True, stop=True)
        mm.then_inc(folded, 1)
        pe.wait_ge(copied, 1)
        for t in range(T):
            if t >= 4:
                pe.wait_ge(out, t - 3)
            for k in range(KD):
                mm = pe.matmul(c.bank[:, t % 4, 0:2 * MSG], c.xT[:, k, t * P:(t + 1) * P], w_all[:, k, :],
                               start=k == 0, stop=k == KD - 1)
            mm.then_inc(ready, 1)
        meet(pe, met, met_n)

    @block.scalar
    def _(act):
        for t in range(T):
            act.wait_ge(ready, t + 1)
            act.copy(rows[:, t, :], c.bank[:, t % 4, 0:2 * MSG]).then_inc(out, 1)
        meet(act, met, met_n)

    @block.vector
    def _(dve):
        dve.wait_ge(folded, 1)
        dve.wait_ge(loaded, 16 * 5)
        dve.tensor_copy(w_all[:].rearrange("p k (i m) -> p i k m", i=2)[:, :, :, FEAT:MSG],
                        c.bank[:, 7, 0:4 * HEADS1].rearrange("p (i k h) -> p i k h", i=2, k=KD)).then_inc(copied, 1)
        meet(dve, met, met_n)


def mix1_stage(c, block, ctx, met_n):
    a = c.a
    heads = INNER // FEAT
    pairs = INNER // P
    wkv = c.sb(ctx, "w_kv1", [P, KD, 2 * INNER])
    wq = c.sb(ctx, "w_q1", [P, pairs, D])
    wo = c.sb(ctx, "w_out1", [P, pairs, D])
    bo = c.sb(ctx, "b_out1", [P, D])
    kv = c.sb(ctx, "kv1", [P, 2, KV_GROUPS, FEAT])
    sq = c.sb(ctx, "kv_square", [P, KV_GROUPS, FEAT])
    mean = c.sb(ctx, "kv_mean", [P, 2, KV_GROUPS])
    var = c.sb(ctx, "kv_var", [P, 2, KV_GROUPS])
    dots = c.sb(ctx, "dots", [P, pairs, P])
    mat = c.sb(ctx, "mat1", [P, pairs, D])
    mat2 = c.sb(ctx, "mat2", [P, KD, D])
    y = c.sb(ctx, "mix1_out", [P, D])
    loaded, kv_ready, centred, squared, var_ready, rooted, normed, step = \
        (c.sem(ctx, f"mix1_{k}") for k in ("loaded", "kv_ready", "centred", "squared", "var", "rooted", "normed", "step"))
    kv_used, dots_ready, dots_out, mat_ready, mat_out, mat2_ready, mat2_out, y_ready, y_out = \
        (c.sem(ctx, f"mix1_{k}") for k in ("kv_used", "dots_ready", "dots_out", "mat_ready", "mat_out", "mat2_ready",
                                           "mat2_out", "y_ready", "y_out"))
    met = c.met

    @block.sync
    def _(sp):
        sp.dma_start(wkv[:], a["wkv1_t"].rearrange("(k p) n -> p k n", p=P)).then_inc(loaded, 16)
        sp.dma_start(wq[:], a["wq1"].rearrange("(j p) n -> p j n", p=P)).then_inc(loaded, 16)
        sp.dma_start(wo[:], a["wout1_t"].rearrange("(j p) n -> p j n", p=P)).then_inc(loaded, 16)
        sp.dma_start(bo[:], a["bout1"].partition_broadcast(P)).then_inc(loaded, 16)
        meet(sp, met, met_n)

    @block.tensor
    def _(pe):
        pe.wait_ge(loaded, 64)
        for t in range(T + 1):
            if t < T:
                b = 2 * (t % 2)
                if t >= 2:
                    pe.wait_ge(centred, t - 1)
                for half in range(2):
                    for k in range(KD):
                        mm = pe.matmul(c.bank[:, b + half, :], c.xT[:, k, t * P:(t + 1) * P],
                                       wkv[:, k, half * INNER:(half + 1) * INNER], start=k == 0, stop=k == KD - 1)
                mm.then_inc(kv_ready, 1)
            if t >= 1:
                u = t - 1
                n = P if u < T - 1 else LAST
                pe.wait_ge(normed, u + 1)
                row = kv[0:n, u % 2, :, :].rearrange("p g f -> p (g f)")
                for j in range(pairs):
                    mm = pe.matmul(c.bank[:, 4 + j, 0:P], row[:, INNER + j * P:INNER + (j + 1) * P],
                                   row[:, j * P:(j + 1) * P], start=u == 0, stop=u == T - 1)
                mm.then_inc(kv_used, 1)
        pe.wait_ge(dots_out, pairs)
        for j in range(pairs):
            pe.matmul(c.bank[:, j, 0:D], dots[:, j, :], wo[:, j, :], start=True, stop=True)\
              .then_inc(mat_ready, 1)
        pe.wait_ge(mat_out, pairs)
        for k in range(KD):
            for j in range(pairs):
                mm = pe.matmul(c.bank[:, 4 + k, 0:D], wq[:, j, k * P:(k + 1) * P], mat[:, j, :],
                               start=j == 0, stop=j == pairs - 1)
        mm.then_inc(mat2_ready, 1)
        pe.wait_ge(mat2_out, 1)
        for t in range(T):
            if t >= 4:
                pe.wait_ge(y_out, t - 3)
            for k in range(KD):
                mm = pe.matmul(c.bank[:, t % 4, 0:D], c.xT[:, k, t * P:(t + 1) * P], mat2[:, k, :],
                               start=k == 0, stop=k == KD - 1)
            mm.then_inc(y_ready, 1)
        meet(pe, met, met_n)

    @block.scalar
    def _(act):
        for t in range(T):
            act.wait_ge(centred, t + 1)
            if t >= 1:
                act.wait_ge(var_ready, t)
            act.activation(sq[:], kv[:, t % 2, :, :], ACT.Square).then_inc(squared, 1)
            act.wait_ge(var_ready, t + 1)
            act.activation(var[:, t % 2, :], var[:, t % 2, :], ACT.Sqrt).then_inc(rooted, 1)
        meet(act, met, met_n)

    @block.vector
    def _(dve):
        ch = Chain(dve, step)
        shape = [P, KV_GROUPS, FEAT]
        wide = lambda b: b.rearrange("p (g o) -> p g o", o=1).to_broadcast(shape)
        for t in range(T):
            b, r = 2 * (t % 2), t % 2
            raw = c.bank[:, b:b + 2, :].rearrange("p a (g f) -> p (a g) f", f=FEAT)
            dve.wait_ge(kv_ready, t + 1)
            ch.then(dve.tensor_reduce(mean[:, r, :], raw, AX.X, ALU.add))
            ch.then(dve.tensor_scalar(mean[:, r, :], mean[:, r, :], 1.0 / FEAT, None, ALU.mult))
            if t >= 2:
                dve.wait_ge(kv_used, t - 1)
            dve.tensor_tensor(kv[:, r, :, :], raw, wide(mean[:, r, :]), ALU.subtract).then_inc(centred, 1)
            dve.wait_ge(squared, t + 1)
            ch.then(dve.tensor_reduce(var[:, r, :], sq[:], AX.X, ALU.add))
            dve.tensor_scalar(var[:, r, :], var[:, r, :], 1.0 / FEAT, 1e-5, ALU.mult, ALU.add).then_inc(var_ready, 1)
            dve.wait_ge(rooted, t + 1)
            ch.then(dve.reciprocal(var[:, r, :], var[:, r, :]))
            dve.tensor_tensor(kv[:, r, :, :], kv[:, r, :, :], wide(var[:, r, :]), ALU.mult).then_inc(normed, 1)
        dve.wait_ge(kv_used, T)
        for j in range(pairs):
            dve.tensor_tensor(dots[:, j, :], c.bank[:, 4 + j, 0:P], c.head64[:], ALU.mult).then_inc(dots_out, 1)
        for j in range(pairs):
            dve.wait_ge(mat_ready, j + 1)
            dve.tensor_copy(mat[:, j, :], c.bank[:, j, 0:D]).then_inc(mat_out, 1)
        dve.wait_ge(mat2_ready, 1)
        dve.tensor_scalar(mat2[:], c.bank[:, 4:4 + KD, 0:D], 1.0 / N, None, ALU.mult).then_inc(mat2_out, 1)
        for t in range(T):
            dve.wait_ge(y_ready, t + 1)
            dve.tensor_tensor(y[:], c.bank[:, t % 4, 0:D], bo[:], ALU.add).then_inc(y_out, 1)
            dve.wait_ge(y_out, t + 1)
            ch.then(dve.tensor_tensor(c.X[:, t, :], c.X[:, t, :], y[:], ALU.add))
        meet(dve, met, met_n)




def messages_stage(c, block, ctx, e):
    tmp = c.sb(ctx, "reverse_part", [P, 2, MSG])
    used = c.sem(ctx, "rows_used1")
    half_way = c.sem(ctx, "reverse_part_ready")
    gather_rows(c, block, ctx, e, c.table1, 2 * MSG, used)

    @block.vector
    def _(dve):
        dve.sem_inc(used, RING)
        dve.wait_ge(e.slot_in, 16)
        with dve.Fori(0, e.tiles // RING) as i:
            for k in range(RING + 1):
                if k < RING:
                    dve.wait_ge(e.gathered[k], i * 16 + 16)
                    col = e.slot[:, ds(i * RING + k, 1), 3:4].rearrange("p t o -> p (t o)")
                    if k >= 2:
                        dve.wait_ge(used, i * RING + (RING + k - 1))
                    dve.tensor_scalar(tmp[:, k % 2, :], e.rows_in[:, k, MSG:2 * MSG], col, None, ALU.mult)\
                        .then_inc(half_way, 1)
                if k >= 1:
                    j = k - 1
                    dve.wait_ge(half_way, i * RING + (j + 1))
                    col = e.slot[:, ds(i * RING + j, 1), 2:3].rearrange("p t o -> p (t o)")
                    dve.scalar_tensor_tensor(c.msg[:, ds(i * RING + j, 1), :].rearrange("p a m -> p (a m)"),
                                             e.rows_in[:, j, 0:MSG], col, tmp[:, j % 2, :], ALU.mult, ALU.add)\
                        .then_inc(used, 1)
            dve.wait_ge(used, i * RING + 2 * RING)


def softmax1_stage(c, block, ctx, e, met_n):
    none = c.sb(ctx, "no_edge", [P, e.tiles])
    top = c.sb(ctx, "score_top", [P, HEADS1])
    top4 = c.sb(ctx, "score_max", [HEADS1, 1])
    diag = c.sb(ctx, "score_diag", [HEADS1, HEADS1])
    step, top_ready, turned, diag_ready, spread, shifted, exped = \
        (c.sem(ctx, f"softmax1_{k}") for k in ("step", "top", "turned", "diag", "spread", "shifted", "exped"))
    met = c.met

    @block.tensor
    def _(pe):
        pe.wait_ge(top_ready, 1)
        pe.transpose(c.bank[0:HEADS1, 0, 0:P], top[:], c.ident[:]).then_inc(turned, 1)
        pe.wait_ge(diag_ready, 1)
        pe.matmul(c.bank[:, 1, 0:HEADS1], c.ones[0:HEADS1, 0:P], diag[:], start=True, stop=True).then_inc(spread, 1)
        meet(pe, met, met_n)

    @block.scalar
    def _(act):
        act.wait_ge(shifted, 1)
        act.activation(c.prob[:], c.prob[:], ACT.Exp).then_inc(exped, 1)
        act.wait_ge(exped, 1)
        meet(act, met, met_n)

    @block.sync
    def _(sp):
        meet(sp, met, met_n)

    @block.vector
    def _(dve):
        ch = Chain(dve, step)
        s = c.msg[:, :, FEAT:MSG]
        ch.then(dve.tensor_scalar(none[:], e.slot[:, :, 1], 0.0, NEG, ALU.is_lt, ALU.mult))
        ch.then(dve.scalar_tensor_tensor(c.prob[:], s, 0.2, s, ALU.mult, ALU.max))
        ch.then(dve.tensor_tensor(c.prob[:], c.prob[:],
                                  none[:].rearrange("p (t o) -> p t o", o=1).to_broadcast([P, e.tiles, HEADS1]),
                                  ALU.add))
        ch.then(dve.memset(c.msg[:, :, FEAT:FEAT + 1], 1.0))
        dve.tensor_reduce(top[:], c.prob[:].rearrange("p t h -> p h t"), AX.X, ALU.max).then_inc(top_ready, 1)
        dve.wait_ge(turned, 1)
        ch.then(dve.tensor_reduce(top4[:], c.bank[0:HEADS1, 0, 0:P], AX.X, ALU.max))
        dve.tensor_scalar(diag[:], c.ident[0:HEADS1, 0:HEADS1], top4[:], None, ALU.mult).then_inc(diag_ready, 1)
        dve.wait_ge(spread, 1)
        dve.tensor_tensor(c.prob[:], c.prob[:],
                          c.bank[:, 1:2, 0:HEADS1].to_broadcast([P, e.tiles, HEADS1]), ALU.subtract)\
            .then_inc(shifted, 1)
        ch.then(dve.memset(c.agg[:], 0.0))
        meet(dve, met, met_n)


def sum1_stage(c, block, ctx, e):
    hot = c.sb(ctx, "one_hot1", [P, RING, P])
    val = c.sb(ctx, "weighted1", [P, RING, HEADS1, FEAT + 1])
    den = c.sb(ctx, "weight_sum", [P, T * HEADS1])
    used = c.sem(ctx, "halves_summed1")
    hot_ready = c.sem(ctx, "one_hots_ready1")
    val_dve, val_pool = c.sem(ctx, "weighted_dve"), c.sem(ctx, "weighted_pool")
    added = c.sem(ctx, "group_added1")
    step = c.sem(ctx, "mean1_step")
    per = GROUP // P
    steps = e.tiles // RING
    half_groups = HALF // per
    own = 1

    def weigh(eng, i, at, n, sem):
        shape = [P, n, HEADS1, FEAT + 1]
        m = c.msg[:, ds(i * RING + at, n), 0:FEAT + 1].rearrange("p t (o f) -> p t o f", o=1).to_broadcast(shape)
        w = c.prob[:, ds(i * RING + at, n), :].rearrange("p t (h o) -> p t h o", o=1).to_broadcast(shape)
        eng.tensor_tensor(val[:, at:at + n, :, :], m, w, ALU.mult).then_inc(sem, 1)

    @block.gpsimd
    def _(pool):
        pool.wait_ge(c.met, 4 * c.softmax1_met)
        with pool.Fori(0, steps) as i:
            for h in range(2):
                pool.wait_ge(used, i * 2 + h + 1)
                weigh(pool, i, HALF * h + own, HALF - own, val_pool)

    @block.tensor
    def _(pe):
        pe.sem_inc(used, 2)
        with pe.Fori(0, steps) as i:
            for h in range(2):
                pe.wait_ge(hot_ready, i * 2 + h + 1)
                pe.wait_ge(val_dve, i * 2 + h + 1)
                pe.wait_ge(val_pool, i * 2 + h + 1)
                pe.wait_ge(added, i * BODY_GROUPS + half_groups * (h + 1))
                for k in range(HALF * h, HALF * h + HALF):
                    mm = pe.matmul(c.bank[:, k // per, 0:AGG], hot[:, k, :], val[:, k, :, :].rearrange("p h f -> p (h f)"),
                                   start=k % per == 0, stop=k % per == per - 1)
                mm.then_inc(used, 1)

    @block.vector
    def _(dve):
        ch = Chain(dve, step)
        dve.sem_inc(added, BODY_GROUPS)

        def prepare(i, h):
            dve.wait_ge(used, i * 2 + h + 1)
            one_hots_of_half(dve, c, e, hot, i, h).then_inc(hot_ready, 1)
            weigh(dve, i, HALF * h, own, val_dve)

        def add_half(i, h, tiles):
            dve.wait_ge(used, i * 2 + h + 3)
            for k, tile in enumerate(tiles):
                g = half_groups * h + k
                dve.wait_ge(added, i * BODY_GROUPS + (BODY_GROUPS + g))
                x = c.agg[:, ds(tile, 1), :].rearrange("p a d -> p (a d)")
                dve.tensor_tensor(x, c.bank[:, g % BODY_GROUPS, 0:AGG], x, ALU.add).then_inc(added, 1)

        tiles = lambda first, n: tiles_of_groups(c, mybir.EngineType.DVE, e, first, n)
        prepare(0, 0)
        prepare(0, 1)
        add_half(0, 0, tiles(0, half_groups))
        with dve.Fori(1, steps) as i:
            now = tiles(i * BODY_GROUPS - half_groups, 2 * half_groups)
            prepare(i, 0)
            add_half(i, -1, now[:half_groups])
            prepare(i, 1)
            add_half(i, 0, now[half_groups:])
        add_half(steps, -1, tiles(steps * BODY_GROUPS - half_groups, half_groups))
        dve.wait_ge(added, BODY_GROUPS * (steps + 1))
        agg = c.agg[:].rearrange("p t (h f) -> p (t h) f", f=FEAT + 1)
        ch.then(dve.tensor_scalar(den[:], agg[:, :, FEAT], 1e-10, None, ALU.add))
        ch.then(dve.reciprocal(den[:], den[:]))
        ch.then(dve.tensor_tensor(agg[:, :, 0:FEAT], agg[:, :, 0:FEAT],
                                  den[:].rearrange("p (g o) -> p g o", o=1).to_broadcast([P, T * HEADS1, FEAT]),
                                  ALU.mult))
        x = c.X[:].rearrange("p t (h f) -> p (t h) f", f=FEAT)
        ch.then(dve.tensor_tensor(x, x, agg[:, :, 0:FEAT], ALU.add))




NE1 = 4
HID_G = NE1 * NE1
ROW_G = HID_G + NE1
FAR = NE1


def table_g_stage(c, block, ctx, met_n):
    a = c.a
    w = c.sb(ctx, "w_gat", [P, KD, HID_G])
    att = c.sb(ctx, "att_gat", [P, 2, HID_G])
    prod = c.sb(ctx, "att_prod", [P, T, HID_G])
    low = c.sb(ctx, "low", [P, 1])
    lowd = c.sb(ctx, "low_diag", [P, P])
    loaded, ready, step, stored, out, low_ready, low_back = \
        (c.sem(ctx, f"table_g_{k}") for k in ("loaded", "ready", "step", "stored", "out", "low", "low_back"))
    met = c.met
    h = c.tab[:, :, 0:HID_G]
    a_src = c.tab[:, :, HID_G:ROW_G]

    @block.sync
    def _(sp):
        sp.dma_start(w[:], a["w_gat"].rearrange("(k p) n -> p k n", p=P)).then_inc(loaded, 16)
        sp.dma_start(att[:, 0, :], a["att_src"].partition_broadcast(P)).then_inc(loaded, 16)
        sp.dma_start(att[:, 1, :], a["att_dst"].partition_broadcast(P)).then_inc(loaded, 16)
        sp.wait_ge(out, 1)
        sp.dma_start(c.table_g.rearrange("(t p) w -> p t w", p=P), c.tab[:]).then_inc(stored, 16)
        sp.wait_ge(stored, 16)
        meet(sp, met, met_n)

    @block.scalar
    def _(act):
        meet(act, met, met_n)

    @block.tensor
    def _(pe):
        pe.wait_ge(loaded, 48)
        for t in range(T):
            for k in range(KD):
                mm = pe.matmul(c.bank[:, 0, t * HID_G:(t + 1) * HID_G], c.xT[:, k, t * P:(t + 1) * P], w[:, k, :],
                               start=k == 0, stop=k == KD - 1)
        mm.then_inc(ready, 1)
        pe.wait_ge(low_ready, 1)
        pe.transpose(c.bank[0:1, 1, 0:P], low[:], c.ident[:]).then_inc(low_back, 1)
        pe.wait_ge(low_ready, 2)
        pe.matmul(c.bank[:, 2, 0:1], c.ones[0:1, 0:P], lowd[0:1, 0:1], start=True, stop=True).then_inc(low_back, 1)
        meet(pe, met, met_n)

    @block.vector
    def _(dve):
        ch = Chain(dve, step)
        shape = [P, T, HID_G]
        dve.wait_ge(ready, 1)
        ch.then(dve.tensor_copy(h, c.bank[:, 0, 0:T * HID_G].rearrange("p (t n) -> p t n", n=HID_G)))
        for i, to in ((0, a_src), (1, c.edge_tab[:, :, 0:NE1])):
            ch.then(dve.tensor_tensor(prod[:], h, att[:, i:i + 1, :].to_broadcast(shape), ALU.mult))
            ch.then(dve.tensor_reduce(to, prod[:].rearrange("p t (h e) -> p t h e", e=NE1), AX.X, ALU.add))
        dve.sem_inc(out, 1)
        dve.tensor_reduce(low[:], a_src, AX.XY, ALU.min).then_inc(low_ready, 1)
        dve.wait_ge(low_back, 1)
        dve.tensor_reduce(lowd[0:1, 0:1], c.bank[0:1, 1, 0:P], AX.X, ALU.min).then_inc(low_ready, 1)
        dve.wait_ge(low_back, 2)
        ch.then(dve.tensor_scalar(c.lift[:], c.bank[:, 2, 0:1], -1.0, 1.0, ALU.mult, ALU.add))
        ch.then(dve.tensor_scalar(c.high[:], a_src, c.lift[:], None, ALU.add))
        meet(dve, met, met_n)


def segment_max_stage(c, block, ctx, e):
    per = GROUP // P
    hot = c.sb(ctx, "one_hot_m", [P, RING, P])
    lifted = c.sb(ctx, "lifted", [P, RING, NE1])
    diag = c.sb(ctx, "score_diags", [P, RING, NE1, P])
    mx = c.sb(ctx, "group_max", [P, 2, NE1])
    used = c.sem(ctx, "rows_used_g")
    lift_ready = c.sem(ctx, "lifted_ready")
    hot_ready = c.sem(ctx, "one_hot_ready_m")
    diag_ready = c.sem(ctx, "diag_ready")
    spread = c.sem(ctx, "scores_spread")
    taken = c.sem(ctx, "spread_taken")
    mx_step = c.sem(ctx, "group_max_taken_in")
    steps = e.tiles // RING
    half_groups = HALF // per
    own = 1
    gather_rows(c, block, ctx, e, c.table_g, ROW_G, used)

    @block.scalar
    def _(act):
        with act.Fori(0, steps) as i:
            for half in range(2):
                act.wait_ge(lift_ready, i * 2 + half + 1)
                act.wait_ge(spread, i * 2 + half + 1)
                for k in range(HALF * half + own, HALF * half + HALF):
                    for h in range(NE1):
                        op = act.activation(diag[:, k, h, :], c.ident[:], ACT.Copy, scale=lifted[:, k, h:h + 1])
                op.then_inc(diag_ready, 1)

    @block.tensor
    def _(pe):
        pe.sem_inc(spread, 2)
        with pe.Fori(0, steps) as i:
            for half in range(2):
                pe.wait_ge(taken, i * BODY_GROUPS + half_groups * (half + 1))
                pe.wait_ge(hot_ready, i * 2 + half + 1)
                pe.wait_ge(diag_ready, i * 2 + half + 1)
                for k in range(HALF * half, HALF * half + HALF):
                    mm = pe.matmul(c.bank[:, k, :], hot[:, k, :], diag[:, k, :, :].rearrange("p h n -> p (h n)"),
                                   start=True, stop=True)
                mm.then_inc(spread, 1)

    @block.vector
    def _(dve):
        dve.sem_inc(used, RING)
        dve.sem_inc(taken, BODY_GROUPS)
        dve.sem_inc(mx_step, 1)
        dve.wait_ge(e.slot_in, 16)

        def prepare(i, half):
            at = half * HALF
            for k in range(at, at + HALF):
                dve.wait_ge(e.gathered[k], i * 16 + 16)
            dve.wait_ge(spread, i * 2 + half + 1)
            dve.tensor_scalar(lifted[:, at:at + HALF, :], e.rows_in[:, at:at + HALF, HID_G:ROW_G], c.lift[:], None,
                              ALU.add).then_inc(lift_ready, 1)
            dve.tensor_copy(c.rows_g[:, ds(i * RING + at, HALF), :], e.rows_in[:, at:at + HALF, :])\
                .then_inc(used, HALF)
            dve.wait_ge(lift_ready, i * 2 + half + 1)
            shape = [P, NE1, P]
            for k in range(at, at + own):
                dve.tensor_tensor(diag[:, k, :, :], c.ident[:].rearrange("p (o n) -> p o n", o=1).to_broadcast(shape),
                                  lifted[:, k, :].rearrange("p (h o) -> p h o", o=1).to_broadcast(shape), ALU.mult)
            one_hots_of_half(dve, c, e, hot, i, half).then_inc(hot_ready, 1)

        def take_max(i, half, tiles):
            dve.wait_ge(spread, i * 2 + half + 1)
            for k, tile in enumerate(tiles):
                b = half_groups * half + k
                g = b - BODY_GROUPS
                high = c.high[:, ds(tile, 1), :].rearrange("p a h -> p (a h)")
                dve.tensor_reduce(mx[:, k, :], c.bank[:, per * b:per * b + per, :].rearrange("p a (h n) -> p h a n", h=NE1),
                                  AX.XY, ALU.max).then_inc(taken, 1)
                dve.wait_ge(taken, i * BODY_GROUPS + (g + 1 + BODY_GROUPS))
                dve.wait_ge(mx_step, i * BODY_GROUPS + (g + 1))
                dve.tensor_tensor(high, high, mx[:, k, :], ALU.max).then_inc(mx_step, 1)

        tiles = lambda i: tiles_of_groups(c, mybir.EngineType.DVE, e, i * BODY_GROUPS, BODY_GROUPS)
        prepare(0, 0)
        prepare(0, 1)
        with dve.Fori(1, steps) as i:
            before = tiles(i - 1)
            for half in range(2):
                prepare(i, half)
                take_max(i, half, before[half_groups * half:half_groups * (half + 1)])
        before = tiles(steps - 1)
        for half in range(2):
            take_max(steps, half, before[half_groups * half:half_groups * (half + 1)])


def sum_g_stage(c, block, ctx, e, met_n):
    a = c.a
    top = c.sb(ctx, "edge_max", [P, T, NE1])
    none = c.sb(ctx, "no_edge_g", [P, e.tiles])
    hot = c.sb(ctx, "one_hot_g", [P, RING, P])
    hot_t = c.sb(ctx, "one_hot_t", [P, RING, P])
    at_slot = c.sb(ctx, "target_at_slot", [P, e.tiles, 2 * NE1])
    z = c.sb(ctx, "edge_score", [P, e.tiles, NE1])
    agg = c.sb(ctx, "agg_g", [P, T, ROW_G])
    own = c.sb(ctx, "own_weight", [P, T, NE1])
    step, z_ready, z_exped = (c.sem(ctx, f"sum_g_{k}") for k in ("step", "shifted", "exped"))
    tab_ready = c.sem(ctx, "targets_table_ready")
    hot_ready = c.sem(ctx, "one_hot_ready_g")
    turned = c.sem(ctx, "one_hot_turned_g")
    t_copied = c.sem(ctx, "one_hot_t_copied")
    spread = c.sem(ctx, "targets_spread")
    kept = c.sem(ctx, "targets_kept")
    hot2_ready = c.sem(ctx, "one_hot_ready_g2")
    used = c.sem(ctx, "halves_summed_g")
    added = c.sem(ctx, "group_added_g")
    weighted = c.sem(ctx, "weighted_g")
    met = c.met
    per = GROUP // P
    steps = e.tiles // RING
    src = c.tab[:, :, HID_G:ROW_G]
    far = c.edge_tab[:, :, 0:NE1]
    et = c.edge_tab[:, :, NE1:2 * NE1]
    half_groups = HALF // per

    @block.scalar
    def _(act):
        act.wait_ge(z_ready, 1)
        act.activation(own[:], own[:], ACT.Exp).then_inc(z_exped, 1)
        act.sem_inc(t_copied, 2)
        act.sem_inc(kept, 2)

        def copy_t(i, h):
            act.wait_ge(turned, i * 2 + (h + 3))
            act.copy(hot_t[:, HALF * h:HALF * h + HALF, :], c.bank[:, h, :].rearrange("p (a n) -> p a n", n=P))\
               .then_inc(t_copied, 1)

        def keep(i, h):
            act.wait_ge(spread, i * 2 + (h + 1))
            act.copy(at_slot[:, ds(i * RING + h * HALF, HALF), :],
                     c.bank[:, 2 + h % 2, 0:HALF * 2 * NE1].rearrange("p (k w) -> p k w", w=2 * NE1))\
               .then_inc(kept, 1)

        copy_t(0, 0)
        copy_t(0, 1)
        keep(0, 0)
        with act.Fori(1, steps) as i:
            copy_t(i, 0)
            keep(i, -1)
            copy_t(i, 1)
            keep(i, 0)
        keep(steps, -1)
        act.wait_ge(z_ready, 2)
        act.activation(z[:], z[:], ACT.Exp).then_inc(z_exped, 1)
        meet(act, met, met_n)

    @block.tensor
    def _(pe):
        pe.sem_inc(turned, 2)
        pe.sem_inc(used, 2)

        def turn(i, h):
            pe.wait_ge(t_copied, i * 2 + (h + 1))
            pe.wait_ge(hot_ready, i * 2 + h + 1)
            for k in range(HALF * h, HALF * h + HALF):
                mm = pe.transpose(c.bank[:, h, (k % HALF) * P:(k % HALF + 1) * P], hot[:, k, :], c.ident[:])
            mm.then_inc(turned, 1)

        def spread_half(i, h):
            pe.wait_ge(t_copied, i * 2 + (h + 3))
            pe.wait_ge(kept, i * 2 + (h + 1))
            tiles = tiles_of_groups(c, mybir.EngineType.PE, e, i * BODY_GROUPS + h * half_groups, half_groups)
            for k in range(HALF):
                tile = tiles[k // per]
                mm = pe.matmul(c.bank[:, 2 + h % 2, k * 2 * NE1:(k + 1) * 2 * NE1], hot_t[:, HALF * (h % 2) + k, :],
                               c.edge_tab[:, ds(tile, 1), :].rearrange("p a w -> p (a w)"), start=True, stop=True)
            mm.then_inc(spread, 1)

        pe.wait_ge(tab_ready, 1)
        turn(0, 0)
        turn(0, 1)
        spread_half(0, 0)
        with pe.Fori(1, steps) as i:
            turn(i, 0)
            spread_half(i, -1)
            turn(i, 1)
            spread_half(i, 0)
        spread_half(steps, -1)
        pe.wait_ge(weighted, 1)
        with pe.Fori(0, steps) as i:
            for h in range(2):
                pe.wait_ge(hot2_ready, i * 2 + h + 1)
                pe.wait_ge(added, i * BODY_GROUPS + half_groups * (h + 1))
                for k in range(HALF * h, HALF * h + HALF):
                    mm = pe.matmul(c.bank[:, 4 + k // per, 0:ROW_G], hot[:, k, :],
                                   c.rows_g[:, ds(i * RING + k, 1), :].rearrange("p a w -> p (a w)"),
                                   start=k % per == 0, stop=k % per == per - 1)
                mm.then_inc(used, 1)
        meet(pe, met, met_n)

    @block.sync
    def _(sp):
        sp.dma_start(c.row_g[:, 0, :], a["b_gat"].partition_broadcast(P)).then_inc(c.row_g_in, 16)
        sp.dma_start(c.row_g[:, 1, :], a["ln_gamma"].partition_broadcast(P)).then_inc(c.row_g_in, 16)
        sp.dma_start(c.row_g[:, 2, :], a["ln_beta"].partition_broadcast(P)).then_inc(c.row_g_in, 16)
        meet(sp, met, met_n)

    @block.vector
    def _(dve):
        ch = Chain(dve, step)
        lift_b = c.lift[:]
        dve.sem_inc(added, BODY_GROUPS)

        def one_hots(i, h, free, ready):
            dve.wait_ge(free, i * 2 + h + 1)
            one_hots_of_half(dve, c, e, hot, i, h).then_inc(ready, 1)

        ch.then(dve.tensor_scalar(top[:], c.high[:], lift_b, None, ALU.subtract))
        ch.then(dve.tensor_tensor(top[:], top[:], far, ALU.add))
        ch.then(dve.scalar_tensor_tensor(et, top[:], 0.2, top[:], ALU.mult, ALU.max))
        dve.sem_inc(tab_ready, 1)
        ch.then(dve.tensor_tensor(own[:], src, far, ALU.add))
        ch.then(dve.scalar_tensor_tensor(own[:], own[:], 0.2, own[:], ALU.mult, ALU.max))
        dve.tensor_tensor(own[:], own[:], et, ALU.subtract).then_inc(z_ready, 1)
        with dve.Fori(0, steps) as i:
            for h in range(2):
                one_hots(i, h, turned, hot_ready)
        ch.then(dve.tensor_scalar(none[:], e.slot[:, :, 1], 0.0, NEG, ALU.is_lt, ALU.mult))
        dve.wait_ge(z_exped, 1)
        ch.then(dve.tensor_tensor(agg[:, :, 0:HID_G].rearrange("p t (h e) -> p t h e", e=NE1),
                                  c.tab[:, :, 0:HID_G].rearrange("p t (h e) -> p t h e", e=NE1),
                                  own[:].rearrange("p t (h o) -> p t h o", o=1).to_broadcast([P, T, NE1, NE1]),
                                  ALU.mult))
        ch.then(dve.tensor_copy(agg[:, :, HID_G:ROW_G], own[:]))
        dve.wait_ge(kept, 2 * steps + 2)
        ch.then(dve.tensor_tensor(z[:], c.rows_g[:, :, HID_G:ROW_G], at_slot[:, :, 0:NE1], ALU.add))
        ch.then(dve.scalar_tensor_tensor(z[:], z[:], 0.2, z[:], ALU.mult, ALU.max))
        ch.then(dve.tensor_tensor(z[:], z[:], at_slot[:, :, NE1:2 * NE1], ALU.subtract))
        dve.tensor_tensor(z[:], z[:], none[:].rearrange("p (t o) -> p t o", o=1).to_broadcast([P, e.tiles, NE1]),
                          ALU.add).then_inc(z_ready, 1)
        dve.wait_ge(z_exped, 2)
        for h in range(NE1):
            ch.then(dve.tensor_tensor(c.rows_g[:, :, h * NE1:(h + 1) * NE1], c.rows_g[:, :, h * NE1:(h + 1) * NE1],
                                      z[:, :, h:h + 1].to_broadcast([P, e.tiles, NE1]), ALU.mult))
        ch.then(dve.tensor_copy(c.rows_g[:, :, HID_G:ROW_G], z[:]))
        dve.sem_inc(weighted, 1)

        def add_half(i, h, tiles):
            dve.wait_ge(used, i * 2 + h + 3)
            for k, tile in enumerate(tiles):
                g = half_groups * h + k
                dve.wait_ge(added, i * BODY_GROUPS + (BODY_GROUPS + g))
                x = agg[:, ds(tile, 1), :].rearrange("p a d -> p (a d)")
                dve.tensor_tensor(x, c.bank[:, 4 + g % BODY_GROUPS, 0:ROW_G], x, ALU.add).then_inc(added, 1)

        tiles = lambda first, n: tiles_of_groups(c, mybir.EngineType.DVE, e, first, n)
        one_hots(0, 0, used, hot2_ready)
        one_hots(0, 1, used, hot2_ready)
        add_half(0, 0, tiles(0, half_groups))
        with dve.Fori(1, steps) as i:
            now = tiles(i * BODY_GROUPS - half_groups, 2 * half_groups)
            one_hots(i, 0, used, hot2_ready)
            add_half(i, -1, now[:half_groups])
            one_hots(i, 1, used, hot2_ready)
            add_half(i, 0, now[half_groups:])
        add_half(steps, -1, tiles(steps * BODY_GROUPS - half_groups, half_groups))
        dve.wait_ge(added, BODY_GROUPS * (steps + 1))
        ch.then(dve.tensor_scalar(own[:], agg[:, :, HID_G:ROW_G], 1e-16, None, ALU.add))
        ch.then(dve.reciprocal(own[:], own[:]))
        ch.then(dve.tensor_tensor(c.score16[:].rearrange("p t (h e) -> p t h e", e=NE1),
                                  agg[:, :, 0:HID_G].rearrange("p t (h e) -> p t h e", e=NE1),
                                  own[:].rearrange("p t (h o) -> p t h o", o=1).to_broadcast([P, T, NE1, NE1]),
                                  ALU.mult))
        meet(dve, met, met_n)


def gates1_stage(c, block, ctx, met_n):
    sq = c.sb(ctx, "score_square", [P, T, HID_G])
    m = c.sb(ctx, "score_mean", [P, T])
    v = c.sb(ctx, "score_var", [P, T])
    s4 = c.sb(ctx, "score4", [P, T, NE1])
    step, var_ready, rooted, to_exp, exped = (c.sem(ctx, f"gates1_{k}") for k in
                                              ("step", "var", "rooted", "shifted", "exped"))
    met = c.met
    shape = [P, T, HID_G]

    @block.scalar
    def _(act):
        act.wait_ge(var_ready, 1)
        act.activation(v[:], v[:], ACT.Sqrt).then_inc(rooted, 1)
        act.wait_ge(to_exp, 1)
        act.activation(c.gates1[:], c.gates1[:], ACT.Exp).then_inc(exped, 1)
        meet(act, met, met_n)

    @block.tensor
    def _(pe):
        meet(pe, met, met_n)

    @block.sync
    def _(sp):
        meet(sp, met, met_n)

    @block.vector
    def _(dve):
        ch = Chain(dve, step)
        s = c.score16[:]
        wide = lambda b: b[:].rearrange("p (t o) -> p t o", o=1).to_broadcast(shape)
        row = lambda i: c.row_g[:, i:i + 1, :].to_broadcast(shape)
        dve.wait_ge(c.row_g_in, 48)
        ch.then(dve.tensor_tensor(s, s, row(0), ALU.add))
        ch.then(dve.tensor_reduce(m[:], s, AX.X, ALU.add))
        ch.then(dve.tensor_scalar(m[:], m[:], 1.0 / HID_G, None, ALU.mult))
        ch.then(dve.tensor_tensor(s, s, wide(m), ALU.subtract))
        ch.then(dve.tensor_tensor(sq[:], s, s, ALU.mult))
        ch.then(dve.tensor_reduce(v[:], sq[:], AX.X, ALU.add))
        dve.tensor_scalar(v[:], v[:], 1.0 / HID_G, 1e-5, ALU.mult, ALU.add).then_inc(var_ready, 1)
        dve.wait_ge(rooted, 1)
        ch.then(dve.reciprocal(v[:], v[:]))
        ch.then(dve.tensor_tensor(s, s, wide(v), ALU.mult))
        ch.then(dve.tensor_tensor(s, s, row(1), ALU.mult))
        ch.then(dve.tensor_tensor(s, s, row(2), ALU.add))
        ch.then(dve.tensor_reduce(s4[:], s.rearrange("p t (h e) -> p t e h", e=NE1), AX.X, ALU.add))
        ch.then(dve.tensor_scalar(s4[:], s4[:], 1.0 / NE1, None, ALU.mult))
        top2_gates(c, dve, ch, ctx, "1", s4[:], NE1, c.gates1[:], to_exp, exped)
        meet(dve, met, met_n)




def build(nc, a, out, upto=4):
    c = Core(nc, a, out)
    c.upto = upto
    with ExitStack() as top:
        top.enter_context(nc.allow_non_contiguous_dma("small strided rows"))
        c.kept.append(top)
        stage_setup(c, top)
        c.support = nc.dram_tensor("support", [NP, D], F32, kind="Internal").ap()
        c.slot_x = nc.dram_tensor("slot_x", [SLOTS0 + CHOSEN * P, D], F32, kind="Internal").ap()
        c.slot_y = nc.dram_tensor("slot_y", [SLOTS0, D], F32, kind="Internal").ap()
        c.slots_cleared = c.sem(top, "slots_cleared")
        e1 = Edges(c, "gnn1", a["dst"], a["src"], a["edge_attr_2"], 125, top)
        eg = Edges(c, "router", a["router_dst"], a["router_src"], None, P, top)
        records = top.enter_context(ExitStack())
        e1.hold_records(c, records)
        eg.hold_records(c, records)
        with ExitStack() as l0:
            c.kept.append(l0)
            e0 = Edges(c, "gnn0", a["src"], a["dst"], a["edge_weight"], 125, l0)
            e0.hold_records(c, l0)
            with ExitStack() as s, nc.Block() as block:
                rank_stage(c, block, s, e0, 1)
            c.clear_spent()
            with ExitStack() as s, nc.Block() as block:
                scatter_records(c, block, s, e0)
                with ExitStack() as st:
                    norm_stage(c, block, st, "0", 2, True)
                with ExitStack() as st:
                    mix0_stage(c, block, st, 3)
                with ExitStack() as st:
                    rank_stage(c, block, st, e1, 4)
                with ExitStack() as st:
                    rank_stage(c, block, st, eg, 5)
            c.clear_spent()
            with ExitStack() as s, nc.Block() as block:
                clear_slots0(c, block, s)
                load_slots(c, block, s, e0)
                sum0_stage(c, block, s, e0)
            c.clear_spent()
        if c.upto >= 2:
            with ExitStack() as l1:
                c.kept.append(l1)
                m = 5
                with ExitStack() as s, nc.Block() as block:
                    c.group_expert = c.sb(s, "group_expert", [1, GROUPS0], I32)
                    c.XN = c.sb(s, "normed_rows", [P, T, D])
                    c.slot_from = c.sb(s, "slot_from", [P, T, CHOSEN], I32)
                    c.slot_to = c.sb(s, "slot_to", [P, T, CHOSEN], I32)
                    c.gate_of = c.sb(s, "gate_of", [P, T, CHOSEN])
                    c.routed = c.sem(s, "routed")
                    c.sent_all = c.sem(s, "all_nodes_sent")
                    c.outputs_stored = c.sem(s, "slot_out_all_stored")
                    send_nodes0(c, block, s)
                    scatter_records(c, block, s, e1)
                    fetch_outputs0(c, block, s)
                    for stage in (lambda st, m: norm_stage(c, block, st, "1", m, False, c.XN),
                                  lambda st, m: router0_stage(c, block, st, m),
                                  lambda st, m: experts_stage(
                                      c, block, st, "0", m, FF0, [(a["w1s"], a["w2s"])],
                                      a["b1_0"][:, EXPERTS0 * FF0 // P:], a["b2_0"][EXPERTS0 * D:], None),
                                  lambda st, m: private_experts_stage(c, block, st, m)):
                        m += 1
                        with ExitStack() as st:
                            stage(st, m)
                c.clear_spent()
                if c.upto >= 3:
                    c.table1 = nc.dram_tensor("table1", [NP, 2 * MSG], F32, kind="Internal").ap()
                    with ExitStack() as s, nc.Block() as block:
                        scatter_records(c, block, s, eg)
                        for stage in (lambda st, m: norm_stage(c, block, st, "2", m, False),
                                      lambda st, m: table1_stage(c, block, st, m),
                                      lambda st, m: mix1_stage(c, block, st, m)):
                            m += 1
                            with ExitStack() as st:
                                stage(st, m)
                    c.clear_spent()
                    records.close()
                    with ExitStack() as s:
                        c.msg = c.sb(s, "messages", [P, e1.tiles, MSG])
                        c.prob = c.sb(s, "edge_weight", [P, e1.tiles, HEADS1])
                        c.agg = c.XT[:].rearrange("p (t f) -> p t f", t=T)
                        with ExitStack() as s2:
                            e1.slot = c.sb(s, "slot_gnn1", [P, e1.tiles, 4])
                            with nc.Block() as block:
                                load_slots(c, block, s2, e1)
                                messages_stage(c, block, s2, e1)
                            c.clear_spent()
                        with ExitStack() as s2, nc.Block() as block:
                            m += 1
                            with ExitStack() as st:
                                softmax1_stage(c, block, st, e1, m)
                            c.softmax1_met = m
                            sum1_stage(c, block, s2, e1)
                        c.clear_spent()
                if c.upto >= 4:
                    c.table_g = nc.dram_tensor("table_g", [NP, ROW_G], F32, kind="Internal").ap()
                    c.tab = c.sb(l1, "tab_g", [P, T, ROW_G])
                    c.edge_tab = c.sb(l1, "edge_tab", [P, T, 2 * NE1])
                    c.high = c.sb(l1, "high", [P, T, NE1])
                    c.lift = c.sb(l1, "lift", [P, 1])
                    c.row_g = c.sb(l1, "row_g", [P, 3, HID_G])
                    c.row_g_in = c.sem(l1, "row_g_loaded")
                    c.score16 = c.sb(l1, "score16", [P, T, HID_G])
                    c.gates1 = c.sb(l1, "gates1", [P, T, NE1])
                    c.rows_g = c.sb(l1, "rows_g", [P, eg.tiles, ROW_G])
                    eg.slot = c.sb(l1, "slot_router", [P, eg.tiles, 4])
                    with nc.Block() as block:
                        for stage in (lambda st, m: norm_stage(c, block, st, "3", m, False),
                                      lambda st, m: table_g_stage(c, block, st, m)):
                            m += 1
                            with ExitStack() as st:
                                stage(st, m)
                    c.clear_spent()
                    with ExitStack() as s, nc.Block() as block:
                        load_slots(c, block, s, eg)
                        segment_max_stage(c, block, s, eg)
                    c.clear_spent()
                    with nc.Block() as block:
                        for stage in (lambda st, m: sum_g_stage(c, block, st, eg, m),
                                      lambda st, m: gates1_stage(c, block, st, m),
                                      lambda st, m: experts_stage(
                                          c, block, st, "1", m, 512,
                                          [(a["w1e"][i], a["w2e"][i]) for i in range(4)],
                                          a["b1_1"], a["b2_1"], c.gates1)):
                            m += 1
                            with ExitStack() as st:
                                stage(st, m)
                    c.clear_spent()
        stored = c.sem(top, "stored")
        with nc.Block() as block:
            @block.sync
            def _(sp):
                sp.dma_start(out[0:(T - 1) * P, :].rearrange("(t p) d -> p t d", p=P), c.X[:, 0:T - 1, :])\
                  .then_inc(stored, 16)
                sp.dma_start(out[(T - 1) * P:N, :], c.X[0:LAST, T - 1, :]).then_inc(stored, 16)
                sp.wait_ge(stored, 32)


        c.clear_spent()
def laid_out(x):
    import numpy as np
    n = {k: np.asarray(v) for k, v in x.items()}
    cols = lambda b: np.ascontiguousarray(b.reshape(-1, P).T)
    return {
        "x": n["x"], "src": n["src"], "dst": n["dst"], "edge_weight": n["edge_weight"],
        "gnn0_w": n["L0_gnn_weight"], "gnn0_b": n["L0_gnn_bias"], "qkv0_w": n["L0_mix_w_qkv"],
        "out0_w": n["L0_mix_w_out"], "b_out0": n["L0_mix_b_out"], "g_out0": n["L0_mix_g_out"],
        "g_pre0": cols(n["L0_mix_g_pre"]),
        "edge_attr_2": n["edge_attr_2"], "router0_w": n["L0_ffn_Wr"],
        "w1p": n["L0_ffn_W1p"], "w2p": n["L0_ffn_W2p"], "w1s": n["L0_ffn_W1s"], "w2s": n["L0_ffn_W2s"],
        "b1_0": cols(np.concatenate([n["L0_ffn_b1p"].reshape(-1), n["L0_ffn_b1s"]])),
        "b2_0": np.concatenate([n["L0_ffn_b2p"].reshape(-1), n["L0_ffn_b2s"]]),
        "wf": n["L1_gnn_W_forward"], "wr": n["L1_gnn_W_reverse"],
        "wf_t": np.ascontiguousarray(n["L1_gnn_W_forward"].T), "wr_t": np.ascontiguousarray(n["L1_gnn_W_reverse"].T),
        "att1_t": np.ascontiguousarray(n["L1_gnn_attn_forward"][0].T),
        "wkv1_t": np.ascontiguousarray(n["L1_mix_Wqkv"][INNER:].T), "wq1": n["L1_mix_Wqkv"][:INNER],
        "wout1_t": np.ascontiguousarray(n["L1_mix_Wout"].T), "bout1": n["L1_mix_bout"],
        "w_gat": n["L1_ffn_W_gat"], "att_src": n["L1_ffn_att_src"].reshape(-1),
        "att_dst": n["L1_ffn_att_dst"].reshape(-1), "b_gat": n["L1_ffn_b_gat"],
        "ln_gamma": n["L1_ffn_ln_gamma"], "ln_beta": n["L1_ffn_ln_beta"],
        "w1e": n["L1_ffn_W1"], "w2e": n["L1_ffn_W2"], "b1_1": cols(n["L1_ffn_b1"]), "b2_1": n["L1_ffn_b2"].reshape(-1),
        "router_src": np.ascontiguousarray(n["L1_ffn_edge_index"][0]),
        "router_dst": np.ascontiguousarray(n["L1_ffn_edge_index"][1]),
        "mem0": np.ascontiguousarray(n["L0_mix_mem_kv"].transpose(0, 3, 1, 2)).reshape(2, MEM, HID0),
    }


def kernel(**inputs):
    import numpy as np
    from concourse import bacc
    from concourse.bass_utils import run_bass_kernel_spmd

    nc = bacc.Bacc("TRN2", target_bir_lowering=False, num_devices=1)
    arrays = {f"in_{k}": v for k, v in laid_out(inputs).items()}
    aps = {k[3:]: nc.dram_tensor(k, v.shape, mybir.dt.from_np(v.dtype), kind="ExternalInput").ap()
           for k, v in arrays.items()}
    out = nc.dram_tensor("out", (N, D), F32, kind="ExternalOutput").ap()
    build(nc, aps, out)
    return run_bass_kernel_spmd(nc, [arrays], core_ids=[0]).results[0]["out"]
```

```python
from contextlib import ExitStack

import concourse.bass as bass
from concourse import mybir

F32 = mybir.dt.float32
I32 = mybir.dt.int32
BF16 = mybir.dt.bfloat16
ALU = mybir.AluOpType
ACT = mybir.ActivationFunctionType
AX = mybir.AxisListType
ds = bass.ds

P = 128
D = 256
N = 3125
T = -(-N // P)
LAST = N - (T - 1) * P
NP = T * P
KD = D // P
GROUP = 256
RING = 8
HALF = RING // 2
BODY_GROUPS = RING * P // GROUP
NEG = -1.0e30


def up(a, b):
    return -(-a // b) * b


def slot_tiles(edges, group):
    return up((edges + T * (group - 1)) // group * (group // P), RING)


class Chain:

    def __init__(self, eng, sem):
        self.eng, self.sem, self.n = eng, sem, 0

    def then(self, ins, extra=0):
        ins.then_inc(self.sem, 1)
        self.n += 1
        self.eng.wait_ge(self.sem, self.n + extra)


class Core:

    def __init__(self, nc, inputs, out):
        self.nc, self.a, self.out = nc, inputs, out
        self.kept = []
        self.spent = []

    def sb(self, ctx, name, shape, dt=F32):
        return ctx.enter_context(self.nc.sbuf_tensor(name, shape, dt))

    def sem(self, ctx, name):
        if any(ctx is k for k in self.kept):
            return ctx.enter_context(self.nc.semaphore(name))
        self.spent.append(self.nc.alloc_semaphore(name=name))
        return self.spent[-1]

    def clear_spent(self):
        self.nc.all_engine_barrier()
        self.nc.clear_and_free_semaphores(self.spent)
        self.nc.all_engine_barrier()
        self.spent = []


def meet(eng, met, n):
    eng.drain().then_inc(met, 1)
    eng.wait_ge(met, 4 * n)


def everyone_meets(block, met, n):
    block.sync(lambda e: meet(e, met, n))
    block.scalar(lambda e: meet(e, met, n))
    block.vector(lambda e: meet(e, met, n))
    block.tensor(lambda e: meet(e, met, n))




def stage_setup(c, ctx):
    nc = c.nc
    c.bank = ctx.enter_context(nc.psum_tensor("banks", [P, 8, 512], F32))
    c.met = c.sem(ctx, "met")
    c.row_norm = c.sb(ctx, "row_norm", [P, T])
    c.X = c.sb(ctx, "x", [P, T, D])
    c.XT = c.sb(ctx, "xT", [P, T * 260])
    c.xT = c.XT[:, 0:KD * NP].rearrange("p (k n) -> p k n", k=KD)
    c.ident = c.sb(ctx, "ident", [P, P])
    c.before = c.sb(ctx, "before", [P, P])
    c.ones = c.sb(ctx, "ones", [P, 512])
    c.iota_i = c.sb(ctx, "iota_i", [P, 512], I32)
    c.iota = c.sb(ctx, "iota", [P, 512])
    c.part_i = c.sb(ctx, "part_i", [P, 1], I32)
    c.part = c.sb(ctx, "part", [P, 1])
    c.head32 = c.sb(ctx, "head32", [P, P])
    c.head64 = c.sb(ctx, "head64", [P, P])
    load_sem = c.sem(ctx, "setup_loaded")
    const_sem = c.sem(ctx, "constants_made")
    zero_sem = c.sem(ctx, "tail_zeroed")
    with nc.Block() as block:
        @block.sync
        def _(sp):
            sp.dma_start(c.X[:, 0:T - 1, :], c.a["x"][0:(T - 1) * P, :].rearrange("(t p) d -> p t d", p=P))\
              .then_inc(load_sem, 16)
            sp.wait_ge(zero_sem, 1)
            sp.dma_start(c.X[0:LAST, T - 1, :], c.a["x"][(T - 1) * P:N, :]).then_inc(load_sem, 16)
            sp.wait_ge(load_sem, 32)

        @block.vector
        def _(dve):
            dve.memset(c.X[:, T - 1, :], 0.0).then_inc(zero_sem, 1)

        @block.gpsimd
        def _(pool):
            ch = Chain(pool, const_sem)
            ch.then(pool.memset(c.ones[:], 1.0))
            ch.then(pool.memset(c.ident[:], 0.0))
            ch.then(pool.affine_select(out=c.ident[:], in_=c.ident[:], compare_op=ALU.not_equal, fill=1.0,
                                       base=0, pattern=[[-1, P]], channel_multiplier=1))
            ch.then(pool.affine_select(out=c.before[:], in_=c.ones[:, 0:P], compare_op=ALU.is_gt, fill=0.0,
                                       base=0, pattern=[[1, P]], channel_multiplier=-1))
            ch.then(pool.iota(c.iota_i[:], pattern=[[1, 512]], base=0, channel_multiplier=0))
            ch.then(pool.tensor_copy(c.iota[:], c.iota_i[:]))
            ch.then(pool.iota(c.part_i[:], pattern=[[1, 1]], base=0, channel_multiplier=1))
            ch.then(pool.tensor_copy(c.part[:], c.part_i[:]))
            for mask, d in ((c.head32, DH0), (c.head64, FEAT)):
                heads = mask[:].rearrange("p (h d) -> p h d", d=d)
                ch.then(pool.affine_select(out=heads, in_=c.ones[:, 0:P].rearrange("p (h d) -> p h d", d=d),
                                           compare_op=ALU.is_ge, fill=0.0, base=0,
                                           pattern=[[-d, P // d], [0, d]], channel_multiplier=1))
                ch.then(pool.affine_select(out=heads, in_=heads, compare_op=ALU.is_ge, fill=0.0, base=d - 1,
                                           pattern=[[d, P // d], [0, d]], channel_multiplier=-1))




class Edges:

    def __init__(self, c, name, key, val, payload, parts, ctx, group=GROUP):
        self.name, self.key, self.val, self.payload = name, key, val, payload
        self.parts, self.slot = parts, None
        self.count = key.shape[0]
        self.per = self.count // parts
        assert self.per * parts == self.count and self.per % RING == 0
        self.group = group
        self.body_groups = RING * P // group
        self.tiles = slot_tiles(self.count, group)
        self.groups = self.tiles * P // group
        self.slots = c.nc.dram_tensor(f"slots_{name}", [P * self.tiles, 4], F32, kind="Internal").ap()
        self.group_tile = c.sb(ctx, f"group_tile_{name}", [1, self.groups], I32)
        self.filled = c.sem(ctx, f"slots_filled_{name}")
        self.ranked = c.sem(ctx, f"ranked_{name}")

    def hold_records(self, c, ctx):
        self.rows = c.sb(ctx, f"slot_row_{self.name}", [P, self.per], I32)
        self.rec = c.sb(ctx, f"rec_{self.name}", [P, self.per, 4])


def rank_stage(c, block, ctx, e, met_n):
    nc, J, n = c.nc, e.per, e.parts
    key = c.sb(ctx, f"key_{e.name}", [P, J], I32)
    val = c.sb(ctx, f"val_{e.name}", [P, J], I32)
    hi_i = c.sb(ctx, f"hi_i_{e.name}", [P, J], I32)
    hi = c.sb(ctx, f"hi_{e.name}", [P, J])
    words = 0 if e.payload is None else e.payload.shape[1] if len(e.payload.shape) == 2 else 1
    pay = c.sb(ctx, f"pay_{e.name}", [P, J * 2])
    one_hot = c.sb(ctx, f"in_tile_{e.name}", [P, 2, J])
    seen = c.sb(ctx, f"seen_{e.name}", [P, 2, J])
    pos = c.sb(ctx, f"pos_{e.name}", [P, J])
    posf = c.sb(ctx, f"posf_{e.name}", [P, J])
    cnt = c.sb(ctx, f"cnt_{e.name}", [P, T])
    num_i = c.sb(ctx, f"num_i_{e.name}", [P, T], I32)
    num = c.sb(ctx, f"num_{e.name}", [P, T])
    upto = c.sb(ctx, f"upto_{e.name}", [P, T])
    first = c.sb(ctx, f"first_{e.name}", [P, T])
    gt = c.sb(ctx, f"gt_{e.name}", [1, e.groups])
    fill = c.sb(ctx, f"fill_{e.name}", [P, e.tiles, 4])
    ps = c.bank[:, 0:2, :]
    key_in = c.sem(ctx, f"targets_loaded_{e.name}")
    loaded = c.sem(ctx, f"edges_loaded_{e.name}")
    step = c.sem(ctx, f"rank_step_{e.name}")
    counted = c.sem(ctx, f"counted_{e.name}")
    summed = c.sem(ctx, f"count_summed_{e.name}")
    empty = c.sem(ctx, f"empty_slots_{e.name}")
    met = c.met

    @block.sync
    def _(sp):
        sp.dma_start(key[0:n, :], e.key.rearrange("(p j) -> p j", p=n)).then_inc(key_in, 16)
        sp.dma_start(val[0:n, :], e.val.rearrange("(p j) -> p j", p=n)).then_inc(loaded, 16)
        if words == 2:
            sp.dma_start(pay[0:n, 0:J * 2], e.payload.rearrange("(p j) w -> p (j w)", p=n)).then_inc(loaded, 16)
        elif words == 1:
            sp.dma_start(pay[0:n, 0:J], e.payload.rearrange("(p j) -> p j", p=n)).then_inc(loaded, 16)
        sp.wait_ge(empty, 1)
        sp.dma_start(e.slots.rearrange("(p t) w -> p (t w)", p=P), fill[:].rearrange("p t w -> p (t w)"))\
          .then_inc(e.filled, 16)
        sp.wait_ge(e.filled, 16)
        meet(sp, met, met_n)

    @block.scalar
    def _(act):
        meet(act, met, met_n)

    @block.tensor
    def _(pe):
        pe.wait_ge(counted, 1)
        pe.matmul(ps[:, 0, 0:T], c.ones[0:n, 0:P], cnt[0:n, :], start=True, stop=True)
        pe.matmul(ps[0:n, 1, 0:T], c.before[0:n, 0:n], cnt[0:n, :], start=True, stop=True).then_inc(summed, 1)
        meet(pe, met, met_n)

    @block.vector
    def _(dve):
        ch = Chain(dve, step)
        ch.then(dve.memset(fill[:], 0.0))
        ch.then(dve.memset(fill[:, :, 1:2], -1.0))
        dve.sem_inc(empty, 1)
        dve.wait_ge(key_in, 16)
        ch.then(dve.tensor_scalar(hi_i[0:n, :], key[0:n, :], 7, None, ALU.logical_shift_right))
        ch.then(dve.tensor_copy(hi[0:n, :], hi_i[0:n, :]))
        ch.then(dve.tensor_scalar(hi_i[0:n, :], key[0:n, :], P - 1, None, ALU.bitwise_and))
        ch.then(dve.tensor_copy(e.rec[0:n, :, 1:2].rearrange("p j o -> p (j o)"), hi_i[0:n, :]))
        def count(b, place, order):
            dve.wait_ge(step, order)
            dve.tensor_scalar(one_hot[0:n, place, :], hi[0:n, :], c.iota[0:n, ds(b, 1)], 0.0, ALU.is_equal,
                              ALU.add, accum_out=cnt[0:n, ds(b, 1)]).then_inc(step, 1)

        with dve.Fori(0, T // 2) as i:
            for k in range(2):
                count(i * 2 + k, k, i * 2 + (ch.n + k - 1))
        count(T - 1, 0, ch.n + T - 2)
        ch.n += T
        dve.wait_ge(step, ch.n)
        dve.sem_inc(counted, 1)
        dve.wait_ge(loaded, 16 + (16 if words else 0))
        ch.then(dve.tensor_copy(e.rec[0:n, :, 0:1].bitcast(I32).rearrange("p j o -> p (j o)"), val[0:n, :]))
        if words < 2:
            ch.then(dve.memset(e.rec[0:n, :, 2:4], 0.0))
        if words:
            ch.then(dve.tensor_copy(e.rec[0:n, :, 2:2 + words],
                                    pay[0:n, 0:J * words].rearrange("p (j w) -> p j w", w=words)))
        dve.wait_ge(summed, 1)
        ch.then(dve.tensor_scalar(num_i[:], ps[:, 0, 0:T], float(e.group - 1), None, ALU.add))
        ch.then(dve.tensor_scalar(num_i[:], num_i[:], e.group.bit_length() - 1, None, ALU.logical_shift_right))
        ch.then(dve.tensor_copy(num[:], num_i[:]))
        ch.then(dve.tensor_tensor_scan(upto[:], c.ones[:, 0:T], num[:], 0.0, ALU.mult, ALU.add))
        ch.then(dve.tensor_tensor(first[:], upto[:], num[:], ALU.subtract))
        ch.then(dve.tensor_scalar(first[:], first[:], float(e.group), -1.0, ALU.mult, ALU.add))
        ch.then(dve.tensor_tensor(first[0:n, :], first[0:n, :], ps[0:n, 1, 0:T], ALU.add))
        ch.then(dve.memset(pos[0:n, :], 0.0))
        def find(b, places, done):
            w = len(places)
            for k in places:
                dve.wait_ge(step, done + (k - w - 1))
                dve.tensor_scalar(one_hot[0:n, k, :], hi[0:n, :], c.iota[0:n, ds(b + k, 1)], None,
                                  ALU.is_equal).then_inc(step, 1)
            for k in places:
                dve.wait_ge(step, done + (k + 1))
                dve.tensor_tensor_scan(seen[0:n, k, :], c.ones[0:n, 0:J], one_hot[0:n, k, :],
                                       first[0:n, ds(b + k, 1)], ALU.mult, ALU.add).then_inc(step, 1)
            for k in places:
                dve.wait_ge(step, done + (w + k + 1))
                dve.tensor_tensor(seen[0:n, k, :], seen[0:n, k, :], one_hot[0:n, k, :], ALU.mult).then_inc(step, 1)
            for k in places:
                dve.wait_ge(step, done + (2 * w + k + 1 if k == 0 else 3 * w + k))
                dve.tensor_tensor(pos[0:n, :], pos[0:n, :], seen[0:n, k, :], ALU.add).then_inc(step, 1)

        with dve.Fori(0, T // 2) as i:
            find(i * 2, (0, 1), i * 8 + ch.n)
        ch.n += 4 * (T - 1)
        dve.wait_ge(step, ch.n)
        find(T - 1, (0,), ch.n)
        ch.n += 4
        dve.wait_ge(step, ch.n)
        ch.then(dve.tensor_copy(e.rows[0:n, :], pos[0:n, :]))
        ch.then(dve.tensor_scalar(hi_i[0:n, :], e.rows[0:n, :], P - 1, None, ALU.bitwise_and))
        ch.then(dve.tensor_scalar(e.rows[0:n, :], e.rows[0:n, :], 7, None, ALU.logical_shift_right))
        ch.then(dve.tensor_copy(posf[0:n, :], e.rows[0:n, :]))
        ch.then(dve.scalar_tensor_tensor(e.rows[0:n, :], hi_i[0:n, :], float(e.tiles), posf[0:n, :],
                                         ALU.mult, ALU.add))
        dve.sem_inc(e.ranked, 1)
        ch.then(dve.memset(gt[:], 0.0))
        with dve.Fori(0, T) as b:
            ch.then(dve.scalar_tensor_tensor(gt[:], c.iota[0:1, 0:e.groups], upto[0:1, ds(b, 1)], gt[:],
                                             ALU.is_ge, ALU.add), b)
        ch.n += T - 1
        ch.then(dve.tensor_scalar(e.group_tile[:], gt[:], float(T - 1), None, ALU.min))
        meet(dve, met, met_n)


def scatter_records(c, block, ctx, e, begin=0, end=None):
    end = e.per // RING if end is None else end
    n = e.parts
    idx = c.sb(ctx, f"scatter_idx_{e.name}_{begin}", [P, RING], I32)
    rec = c.sb(ctx, f"scatter_rec_{e.name}_{begin}", [P, RING, 4])
    staged = c.sem(ctx, f"record_staged_{e.name}_{begin}")
    turns = c.sem(ctx, f"scatter_turns_{e.name}_{begin}")
    moved = [c.sem(ctx, f"records_moved_{e.name}_{begin}_{k}") for k in range(RING)]

    @block.gpsimd
    def _(pool):
        pool.wait_ge(e.ranked, 1)
        pool.wait_ge(e.filled, 16)

        def round_of(i, first):
            for h in range(2):
                if not first:
                    for k in range(HALF * h, HALF * h + HALF):
                        pool.wait_ge(moved[k], (i - begin) * 16)
                at = HALF * h
                pool.tensor_copy(idx[0:n, at:at + HALF], e.rows[0:n, ds(i * RING + at, HALF)]).then_inc(staged, 1)
                pool.tensor_copy(rec[0:n, at:at + HALF, :], e.rec[0:n, ds(i * RING + at, HALF), :])\
                    .then_inc(staged, 1)
                pool.wait_ge(staged, (i - begin) * 4 + 2 * h + 2)
                pool.sem_inc(turns, 1)
                for k in range(at, at + HALF):
                    pool.indirect_dma_start(e.slots, bass.IndirectOffsetOnAxis(idx[0:n, k:k + 1], 0),
                                            rec[0:n, k, :], None).then_inc(moved[k], 16)

        round_of(begin, True)
        with pool.Fori(begin + 1, end) as i:
            round_of(i, False)
        for k in range(RING):
            pool.wait_ge(moved[k], 16 * (end - begin))




def norm_stage(c, block, ctx, name, met_n, first, rows=None):
    X = c.X
    stats = c.sb(ctx, f"stats_{name}", [P, T, 6])
    mv = c.sb(ctx, f"mean_var_{name}", [P, T, 2])
    var = c.sb(ctx, f"var_{name}", [P, T])
    rstd = c.sb(ctx, f"rstd_{name}", [P, T])
    scale = c.sb(ctx, f"scale_{name}", [P, T])
    gain = c.sb(ctx, f"gain_{name}", [P, T])
    shift = c.sb(ctx, f"shift_{name}", [P, T])
    sd = c.sb(ctx, f"sd_{name}", [P, T])
    ring = 4
    xn = c.sb(ctx, f"xn_{name}", [P, ring, D])
    ps = [c.bank[:, k, 0:KD * P].rearrange("p (h n) -> p h n", h=KD) for k in range(ring)]
    step = c.sem(ctx, f"norm_step_{name}")
    var_ready = c.sem(ctx, f"var_ready_{name}")
    root_ready = c.sem(ctx, f"root_ready_{name}")
    normed = c.sem(ctx, f"normed_{name}")
    turned = c.sem(ctx, f"turned_{name}")
    copied = c.sem(ctx, f"turned_copied_{name}")
    kept = c.sem(ctx, f"residual_kept_{name}")
    met = c.met

    @block.vector
    def _(dve):
        ch = Chain(dve, step)
        for t in range(T):
            dve.bn_stats(stats[:, t, :], X[:, t, :]).then_inc(step, 1)
        ch.n += T
        dve.wait_ge(step, ch.n)
        for t in range(T):
            dve.bn_aggr(mv[:, t, :], stats[:, t, :]).then_inc(step, 1)
        ch.n += T
        dve.wait_ge(step, ch.n)
        ch.then(dve.tensor_scalar(var[:], mv[:, :, 1], 1e-5, None, ALU.add))
        dve.sem_inc(var_ready, 1)
        dve.wait_ge(root_ready, 1)
        ch.then(dve.reciprocal(rstd[:], sd[:]))
        if first:
            ch.then(dve.tensor_tensor(scale[:], rstd[:], rstd[:], ALU.mult))
            ch.then(dve.tensor_tensor(scale[:], scale[:], mv[:, :, 1], ALU.mult))
            ch.then(dve.tensor_scalar(var[:], scale[:], float(D), None, ALU.mult))
            dve.sem_inc(var_ready, 1)
            dve.wait_ge(root_ready, 2)
            ch.then(dve.tensor_scalar(sd[:], sd[:], 1e-12, 1.0 / D ** 0.5, ALU.max, ALU.mult))
            ch.then(dve.tensor_copy(c.row_norm[:], sd[:]))
            ch.then(dve.reciprocal(scale[:], sd[:]))
            ch.then(dve.tensor_tensor(scale[:], scale[:], rstd[:], ALU.mult))
            ch.then(dve.tensor_scalar(gain[:], rstd[:], 1.0, None, ALU.add))
            ch.then(dve.tensor_tensor(shift[:], rstd[:], mv[:, :, 0], ALU.mult))
        else:
            ch.then(dve.tensor_copy(scale[:], rstd[:]))

        def residual(t):
            dve.wait_ge(normed, t + 1)
            dve.tensor_scalar(X[:, t, :], X[:, t, :], gain[:, t:t + 1], shift[:, t:t + 1], ALU.mult, ALU.subtract)\
                .then_inc(kept, 1)

        for t in range(T):
            k = t % ring
            if t >= ring:
                dve.wait_ge(turned, t - ring + 1)
            dve.tensor_scalar(xn[:, k, :], X[:, t, :], mv[:, t, 0:1], scale[:, t:t + 1], ALU.subtract, ALU.mult)\
                .then_inc(normed, 1)
            if rows is not None:
                dve.tensor_scalar(rows[:, t, :], X[:, t, :], mv[:, t, 0:1], scale[:, t:t + 1], ALU.subtract, ALU.mult)
            if first:
                if t >= 1:
                    residual(t - 1)
        if first:
            residual(T - 1)
        meet(dve, met, met_n)

    @block.tensor
    def _(pe):
        for t in range(T):
            k = t % ring
            pe.wait_ge(normed, t + 1)
            if t >= ring:
                pe.wait_ge(copied, t - ring + 1)
            for h in range(KD):
                mm = pe.transpose(ps[k][:, h, :], xn[:, k, h * P:(h + 1) * P], c.ident[:])
            mm.then_inc(turned, 1)
        meet(pe, met, met_n)

    @block.scalar
    def _(act):
        act.wait_ge(var_ready, 1)
        act.activation(sd[:], var[:], ACT.Sqrt).then_inc(root_ready, 1)
        if first:
            act.wait_ge(var_ready, 2)
            act.activation(sd[:], var[:], ACT.Sqrt).then_inc(root_ready, 1)
        for t in range(T):
            act.wait_ge(turned, t + 1)
            act.copy(c.xT[:, :, t * P:(t + 1) * P], ps[t % ring][:, :, :]).then_inc(copied, 1)
        meet(act, met, met_n)

    @block.sync
    def _(sp):
        meet(sp, met, met_n)




HEADS0, DH0, MEM = 4, 32, 4
HID0 = HEADS0 * DH0


def mix0_stage(c, block, ctx, met_n):
    nc, a = c.nc, c.a
    TM = T + 1
    wg = c.sb(ctx, "w_gnn0", [P, KD, D])
    wq = c.sb(ctx, "w_qkv0", [P, KD, 3 * HID0])
    wo = c.sb(ctx, "w_out0", [P, D])
    g_pre = c.sb(ctx, "g_pre0", [P, KD])
    row = c.sb(ctx, "rows0", [P, 3, D])
    qkv = c.sb(ctx, "qkv0", [P, TM, 3 * HID0])
    sup = c.sb(ctx, "support_ring", [P, 2, D])
    y = c.sb(ctx, "y0", [P, T, D])
    scr = c.sb(ctx, "square0", [P, D])
    k_top = c.sb(ctx, "k_top", [P, HID0])
    k_max = c.sb(ctx, "k_max", [P, 1])
    k_diag = c.sb(ctx, "k_diag", [P, HID0])
    off = c.sb(ctx, "k_off", [P, 2])
    q_max = c.sb(ctx, "q_max", [P, T * HEADS0])
    q_sum = c.sb(ctx, "q_sum", [P, T * HEADS0])
    inv_k = c.sb(ctx, "inv_k", [P, 1])
    ctx_t = c.sb(ctx, "context_t", [P, HID0])
    mat = c.sb(ctx, "context_out", [P, D])
    q_t = c.sb(ctx, "q_t", [P, 2, P])
    ss = c.sb(ctx, "y_square", [P, T])
    rn = c.sb(ctx, "y_norm", [P, T])
    in_w = c.sem(ctx, "mix0_loaded")
    mem_zero = c.sem(ctx, "mem_zeroed")
    step = c.sem(ctx, "mix0_step")
    sup_ready = c.sem(ctx, "support_ready")
    sup_out = c.sem(ctx, "support_evacuated")
    sup_stored = [c.sem(ctx, f"support_stored_{k}") for k in range(2)]
    qkv_ready = c.sem(ctx, "qkv_ready")
    qkv_out = c.sem(ctx, "qkv_evacuated")
    scaled = c.sem(ctx, "g_pre_applied")
    top_ready, top_t, diag_ready, top_bc = (c.sem(ctx, f"k_top_{s}") for s in ("ready", "t", "diag", "bc"))
    k_shift, k_exp, q_shift, q_exp = (c.sem(ctx, s) for s in ("k_shifted", "k_exped", "q_shifted", "q_exped"))
    ctx_ready, ctx_out, mat_ready, mat_out = (c.sem(ctx, s) for s in ("ctx_ready", "ctx_out", "mat_ready", "mat_out"))
    q_ready, q_turned, q_copied, y_ready, y_out = \
        (c.sem(ctx, s) for s in ("q_ready", "q_turned", "q_copied", "y0_ready", "y0_out"))
    ss_ready, ss_root = c.sem(ctx, "ss_ready"), c.sem(ctx, "ss_root")
    met = c.met
    q, k, v = (qkv[:, :, i * HID0:(i + 1) * HID0] for i in range(3))

    @block.sync
    def _(sp):
        sp.dma_start(wg[:], a["gnn0_w"].rearrange("(k p) n -> p k n", p=P)).then_inc(in_w, 16)
        sp.dma_start(wq[:], a["qkv0_w"].rearrange("(k p) n -> p k n", p=P)).then_inc(in_w, 16)
        sp.dma_start(wo[:], a["out0_w"]).then_inc(in_w, 16)
        sp.dma_start(g_pre[:], a["g_pre0"]).then_inc(in_w, 16)
        for i, name in enumerate(("b_out0", "g_out0", "gnn0_b")):
            sp.dma_start(row[:, i, :], a[name].partition_broadcast(P)).then_inc(in_w, 16)
        sp.wait_ge(mem_zero, 1)
        for i in range(2):
            sp.dma_start(qkv[0:MEM, T, (1 + i) * HID0:(2 + i) * HID0], a["mem0"][i]).then_inc(in_w, 16)
        for t in range(T):
            sp.wait_ge(sup_out, t + 1)
            sp.dma_start(c.support[t * P:(t + 1) * P, :], sup[:, t % 2, :]).then_inc(sup_stored[t % 2], 16)
        sp.wait_ge(sup_stored[0], 16 * (-(-T // 2)))
        sp.wait_ge(sup_stored[1], 16 * (T // 2))
        meet(sp, met, met_n)

    @block.tensor
    def _(pe):
        pe.wait_ge(in_w, 16 * 9)
        pe.wait_ge(scaled, 1)
        for t in range(T):
            if t >= 2:
                pe.wait_ge(sup_out, t - 1)
                pe.wait_ge(qkv_out, t - 1)
            for kk in range(KD):
                mm = pe.matmul(c.bank[:, t % 2, 0:D], c.xT[:, kk, t * P:(t + 1) * P], wg[:, kk, :],
                               start=kk == 0, stop=kk == KD - 1)
            mm.then_inc(sup_ready, 1)
            for kk in range(KD):
                mm = pe.matmul(c.bank[:, 2 + t % 2, 0:3 * HID0], c.xT[:, kk, t * P:(t + 1) * P], wq[:, kk, :],
                               start=kk == 0, stop=kk == KD - 1)
            mm.then_inc(qkv_ready, 1)
        pe.wait_ge(top_ready, 1)
        pe.transpose(c.bank[:, 4, 0:P], k_top[:], c.ident[:]).then_inc(top_t, 1)
        pe.wait_ge(diag_ready, 1)
        pe.matmul(c.bank[:, 5, 0:HID0], c.ones[:, 0:P], k_diag[:], start=True, stop=True).then_inc(top_bc, 1)
        pe.wait_ge(k_exp, 1)
        for t in range(TM):
            pe.matmul(c.bank[:, 6, 0:HID0], v[:, t, :], k[:, t, :], start=t == 0, stop=t == TM - 1)
            mm = pe.matmul(c.bank[:, 7, 0:1], k[:, t, :], c.ones[:, 0:1], start=t == 0, stop=t == TM - 1)
        mm.then_inc(ctx_ready, 1)
        pe.wait_ge(ctx_out, 1)
        pe.matmul(c.bank[:, 4, 0:D], ctx_t[:], wo[:], start=True, stop=True).then_inc(mat_ready, 1)
        pe.wait_ge(q_ready, 1)
        pe.wait_ge(mat_out, 1)
        for t in range(T + 1):
            if t < T:
                if t >= 2:
                    pe.wait_ge(q_copied, t - 1)
                pe.transpose(c.bank[:, t % 2, 0:P], q[:, t, :], c.ident[:]).then_inc(q_turned, 1)
            if t >= 1:
                pe.wait_ge(q_copied, t)
                if t >= 3:
                    pe.wait_ge(y_out, t - 2)
                pe.matmul(c.bank[:, 2 + (t - 1) % 2, 0:D], q_t[:, (t - 1) % 2, :], mat[:],
                          start=True, stop=True).then_inc(y_ready, 1)
        meet(pe, met, met_n)

    @block.scalar
    def _(act):
        for t in range(T):
            act.wait_ge(qkv_ready, t + 1)
            act.copy(qkv[:, t, :], c.bank[:, 2 + t % 2, 0:3 * HID0]).then_inc(qkv_out, 1)
        act.wait_ge(k_shift, 1)
        act.activation(k, k, ACT.Exp).then_inc(k_exp, 1)
        act.wait_ge(q_shift, 1)
        act.activation(q[:, 0:T, :], q[:, 0:T, :], ACT.Exp).then_inc(q_exp, 1)
        for t in range(T):
            act.wait_ge(q_turned, t + 1)
            if t >= 2:
                act.wait_ge(y_ready, t - 1)
            act.copy(q_t[:, t % 2, :], c.bank[:, t % 2, 0:P]).then_inc(q_copied, 1)
        act.wait_ge(ss_ready, 1)
        act.activation(rn[:], ss[:], ACT.Sqrt).then_inc(ss_root, 1)
        meet(act, met, met_n)

    @block.vector
    def _(dve):
        ch = Chain(dve, step)
        dve.memset(qkv[:, T, :], 0.0).then_inc(mem_zero, 1)
        ch.then(dve.tensor_scalar(off[:, 0:1], c.part[:], float(LAST), NEG, ALU.is_ge, ALU.mult))
        ch.then(dve.tensor_scalar(off[:, 1:2], c.part[:], float(MEM), NEG, ALU.is_ge, ALU.mult))
        dve.wait_ge(in_w, 16 * 9)
        for kk in range(KD):
            ch.then(dve.tensor_scalar(wq[:, kk, :], wq[:, kk, :], g_pre[:, kk:kk + 1], None, ALU.mult))
        dve.sem_inc(scaled, 1)
        for t in range(T):
            dve.wait_ge(sup_ready, t + 1)
            if t >= 2:
                dve.wait_ge(sup_stored[t % 2], 16 * (t // 2))
            dve.tensor_scalar(sup[:, t % 2, :], c.bank[:, t % 2, 0:D], c.row_norm[:, t:t + 1], None, ALU.mult)\
                .then_inc(sup_out, 1)
        dve.wait_ge(qkv_out, T)
        ch.then(dve.tensor_scalar(k[:, T - 1, :], k[:, T - 1, :], off[:, 0:1], None, ALU.add))
        ch.then(dve.tensor_scalar(k[:, T, :], k[:, T, :], off[:, 1:2], None, ALU.add))
        dve.tensor_reduce(k_top[:], k.rearrange("p t c -> p c t"), AX.X, ALU.max).then_inc(top_ready, 1)
        dve.wait_ge(top_t, 1)
        ch.then(dve.tensor_reduce(k_max[:], c.bank[:, 4, 0:P], AX.X, ALU.max))
        dve.tensor_scalar(k_diag[:], c.ident[:], k_max[:], None, ALU.mult).then_inc(diag_ready, 1)
        dve.wait_ge(top_bc, 1)
        dve.tensor_tensor(k, k, c.bank[:, 5:6, 0:HID0].to_broadcast([P, TM, HID0]), ALU.subtract)\
            .then_inc(k_shift, 1)
        qh = q[:, 0:T, :].rearrange("p t (h d) -> p t h d", h=HEADS0)
        qs = [P, T, HEADS0, DH0]
        by_head = lambda b: b[:].rearrange("p (t h o) -> p t h o", h=HEADS0, o=1).to_broadcast(qs)
        ch.then(dve.tensor_reduce(q_max[:].rearrange("p (t h) -> p t h", h=HEADS0), qh, AX.X, ALU.max))
        dve.tensor_tensor(qh, qh, by_head(q_max), ALU.subtract).then_inc(q_shift, 1)
        dve.wait_ge(q_exp, 1)
        ch.then(dve.tensor_reduce(q_sum[:].rearrange("p (t h) -> p t h", h=HEADS0), qh, AX.X, ALU.add))
        ch.then(dve.reciprocal(q_sum[:], q_sum[:]))
        ch.then(dve.tensor_scalar(q_sum[:], q_sum[:], DH0 ** -0.5, None, ALU.mult))
        dve.tensor_tensor(qh, qh, by_head(q_sum), ALU.mult).then_inc(q_ready, 1)
        dve.wait_ge(ctx_ready, 1)
        ch.then(dve.reciprocal(inv_k[:], c.bank[:, 7, 0:1]))
        dve.tensor_tensor(ctx_t[:], c.bank[:, 6, 0:HID0], c.head32[:], ALU.mult).then_inc(ctx_out, 1)
        dve.wait_ge(mat_ready, 1)
        dve.tensor_scalar(mat[:], c.bank[:, 4, 0:D], inv_k[:], None, ALU.mult).then_inc(mat_out, 1)
        for t in range(T):
            dve.wait_ge(y_ready, t + 1)
            dve.tensor_tensor(y[:, t, :], c.bank[:, 2 + t % 2, 0:D], row[:, 0, :], ALU.add).then_inc(y_out, 1)
            dve.wait_ge(y_out, t + 1)
            ch.then(dve.scalar_tensor_tensor(scr[:], y[:, t, :], 1.0, y[:, t, :], ALU.mult, ALU.mult,
                                             accum_out=ss[:, t:t + 1]))
        dve.sem_inc(ss_ready, 1)
        dve.wait_ge(ss_root, 1)
        ch.then(dve.tensor_scalar(rn[:], rn[:], 1e-12, 1.0 / D ** 0.5, ALU.max, ALU.mult))
        ch.then(dve.reciprocal(rn[:], rn[:]))
        with dve.Fori(0, T) as t:
            flat = lambda b: b[:, ds(t, 1), :].rearrange("p a d -> p (a d)")
            ch.then(dve.scalar_tensor_tensor(flat(y), flat(y), rn[:, ds(t, 1)], row[:, 1, :],
                                             ALU.mult, ALU.mult), 3 * t)
            ch.then(dve.tensor_tensor(flat(y), flat(y), row[:, 2, :], ALU.add), 3 * t)
            ch.then(dve.tensor_tensor(flat(c.X), flat(c.X), flat(y), ALU.add), 3 * t)
        ch.n += 3 * (T - 1)
        meet(dve, met, met_n)




def load_slots(c, block, ctx, e):
    if e.slot is None:
        e.slot = c.sb(ctx, f"slot_{e.name}", [P, e.tiles, 4])
    e.slot_in = c.sem(ctx, f"slot_loaded_{e.name}")

    @block.sync
    def _(sp):
        sp.dma_start(e.slot[:].rearrange("p t w -> p (t w)"), e.slots.rearrange("(p t) w -> p (t w)", p=P))\
          .then_inc(e.slot_in, 16)


TURN = 3


def later_rounds(dve, c, e, steps, prepare, finish):
    half_groups = e.body_groups // 2

    def turn(first, n):
        tiles = tiles_of_groups(c, mybir.EngineType.DVE, e, (first - 1) * e.body_groups, n * e.body_groups)
        for u in range(n):
            for h in range(2):
                at = u * e.body_groups + half_groups * h
                prepare(first + u, h)
                finish(first + u, h, tiles[at:at + half_groups])

    turns = (steps - 1) // TURN
    with dve.Fori(0, turns) as i:
        turn(i * TURN + 1, TURN)
    if (steps - 1) % TURN:
        turn(turns * TURN + 1, (steps - 1) % TURN)
    tiles = tiles_of_groups(c, mybir.EngineType.DVE, e, (steps - 1) * e.body_groups, e.body_groups)
    for h in range(2):
        finish(steps, h, tiles[half_groups * h:half_groups * (h + 1)])


def in_turns(eng, begin, end, round_of):
    turns = (end - begin) // TURN
    with eng.Fori(0, turns) as i:
        for u in range(TURN):
            round_of(i * TURN + (begin + u))
    for i in range(begin + turns * TURN, end):
        round_of(i)


def tiles_of_groups(c, engine, e, first, n):
    return c.nc.values_load_multi_w_load_instructions(
        e.group_tile[0:1, ds(first, n)], engines=[engine], min_val=0, max_val=T - 1,
        skip_runtime_bounds_check_because="rank_stage clamps every entry to a tile's number")[1]


def one_hots_of_half(dve, c, e, hot, i, h):
    shape = [P, HALF, P]
    at = HALF * h
    return dve.tensor_tensor(hot[:, at:at + HALF, :], c.iota[:, 0:P].rearrange("p (o n) -> p o n", o=1).to_broadcast(shape),
                             e.slot[:, ds(i * RING + at, HALF), 1:2].to_broadcast(shape), ALU.is_equal)


def gather_rows(c, block, ctx, e, table, width, used):
    e.rows_in = c.sb(ctx, f"rows_{e.name}", [P, RING, width])
    idx = c.sb(ctx, f"gather_idx_{e.name}", [P, RING], I32)
    staged = c.sem(ctx, f"gather_idx_ready_{e.name}")
    turns = c.sem(ctx, f"gather_turns_{e.name}")
    e.gathered = [c.sem(ctx, f"gathered_{e.name}_{k}") for k in range(RING)]

    @block.gpsimd
    def _(pool):
        pool.wait_ge(e.slot_in, 16)
        with pool.Fori(0, e.tiles // RING) as i:
            for h in range(2):
                at = HALF * h
                pool.wait_ge(used, i * RING + at + HALF)
                pool.tensor_copy(idx[:, at:at + HALF],
                                 e.slot[:, ds(i * RING + at, HALF), 0:1].bitcast(I32).rearrange("p t o -> p (t o)"))\
                    .then_inc(staged, 1)
                pool.wait_ge(staged, i * 2 + h + 1)
                pool.sem_inc(turns, 1)
                for k in range(at, at + HALF):
                    pool.indirect_dma_start(e.rows_in[:, k, :], None, table, bass.IndirectOffsetOnAxis(idx[:, k:k + 1], 0))\
                        .then_inc(e.gathered[k], 16)


def sum0_stage(c, block, ctx, e):
    hot = c.sb(ctx, "one_hot0", [P, RING, P])
    used = c.sem(ctx, "rows_used0")
    hot_ready = c.sem(ctx, "one_hots_ready0")
    added = c.sem(ctx, "group_added0")
    gather_rows(c, block, ctx, e, c.support, D, used)
    steps = e.tiles // RING
    per = e.group // P
    half_groups = HALF // per

    @block.tensor
    def _(pe):
        pe.sem_inc(used, RING)
        with pe.Fori(0, steps) as i:
            for h in range(2):
                pe.wait_ge(hot_ready, i * 2 + h + 1)
                pe.wait_ge(added, i * e.body_groups + half_groups * (h + 1))
                for k in range(HALF * h, HALF * h + HALF):
                    pe.wait_ge(e.gathered[k], i * 16 + 16)
                    mm = pe.matmul(c.bank[:, k // per, 0:D], hot[:, k, :], e.rows_in[:, k, :], start=k % per == 0,
                                   stop=k % per == per - 1)
                mm.then_inc(used, HALF)

    @block.vector
    def _(dve):
        dve.sem_inc(added, e.body_groups)
        dve.wait_ge(e.slot_in, 16)

        def prepare(i, h):
            dve.wait_ge(used, i * RING + HALF * (h + 1))
            for k in range(HALF * h, HALF * h + HALF):
                col = lambda w: e.slot[:, ds(i * RING + k, 1), w:w + 1].rearrange("p t o -> p (t o)")
                ins = dve.tensor_scalar(hot[:, k, :], c.iota[:, 0:P], col(1), col(2), ALU.is_equal, ALU.mult)
            ins.then_inc(hot_ready, 1)

        def add_half(i, h, tiles):
            dve.wait_ge(used, i * RING + HALF * (h + 1))
            for k, tile in enumerate(tiles):
                g = half_groups * h + k
                dve.wait_ge(added, i * e.body_groups + g)
                x = c.X[:, ds(tile, 1), :].rearrange("p a d -> p (a d)")
                dve.tensor_tensor(x, c.bank[:, g, 0:D], x, ALU.add).then_inc(added, 1)

        prepare(0, 0)
        prepare(0, 1)
        later_rounds(dve, c, e, steps, prepare, add_half)




CHUNK_TILES = 5
CHUNK = CHUNK_TILES * P
HALF_CHUNK = CHUNK // 2
CHUNKS = T // CHUNK_TILES


def top2_gates(c, dve, ch, ctx, name, logits, n, gates, to_exp, exped):
    s = [P, T, n]
    buf = lambda k, shape: c.sb(ctx, f"{k}_{name}", shape)
    rank, rest, eq, pick, sel = (buf(k, s) for k in ("rank", "rest", "equal", "pick", "sel"))
    top, best = buf("top", [P, T]), buf("best", [P, T])
    wide = lambda b: b[:].rearrange("p (t o) -> p t o", o=1).to_broadcast(s)
    ch.then(dve.tensor_scalar(rank[:], c.iota[:, 0:n].rearrange("p (o e) -> p o e", o=1).to_broadcast(s),
                              -1.0, float(n), ALU.mult, ALU.add))
    ch.then(dve.tensor_copy(rest[:], logits))
    for turn in range(2):
        ch.then(dve.tensor_reduce(top[:], rest[:], AX.X, ALU.max))
        if turn == 0:
            ch.then(dve.tensor_tensor(gates, logits, wide(top), ALU.subtract))
            dve.sem_inc(to_exp, 1)
            dve.wait_ge(exped, 1)
        ch.then(dve.tensor_tensor(eq[:], rest[:], wide(top), ALU.is_equal))
        ch.then(dve.tensor_tensor(eq[:], eq[:], rank[:], ALU.mult))
        ch.then(dve.tensor_reduce(best[:], eq[:], AX.X, ALU.max))
        ch.then(dve.tensor_tensor(pick[:], eq[:], wide(best), ALU.is_equal))
        if turn == 0:
            ch.then(dve.tensor_copy(sel[:], pick[:]))
            ch.then(dve.scalar_tensor_tensor(rest[:].rearrange("p t e -> p (t e)"), pick[:].rearrange("p t e -> p (t e)"),
                                             3.0e38, rest[:].rearrange("p t e -> p (t e)"), ALU.mult, ALU.subtract))
            ch.then(dve.tensor_scalar(rest[:], rest[:], -1.0, None, ALU.mult))
        else:
            ch.then(dve.tensor_tensor(sel[:], sel[:], pick[:], ALU.add))
    ch.then(dve.tensor_tensor(gates, gates, sel[:], ALU.mult))
    ch.then(dve.tensor_reduce(top[:], gates, AX.X, ALU.add))
    ch.then(dve.reciprocal(top[:], top[:]))
    ch.then(dve.tensor_tensor(gates, gates, wide(top), ALU.mult))
    return sel, pick


EXPERTS0, FF0 = 8, 1024
CHOSEN = 2
PAIRS0 = CHOSEN * N
GROUPS0 = up((PAIRS0 + EXPERTS0 * (GROUP - 1)) // GROUP, 2)
SLOTS0 = GROUPS0 * GROUP


def clear_slots0(c, block, ctx):
    zero = c.sb(ctx, "zero_rows", [P, 2048])
    zeroed = c.sem(ctx, "zero_rows_ready")
    rows = c.slot_x[0:SLOTS0, :].rearrange("(p r) d -> p (r d)", p=P)
    width = SLOTS0 // P * D

    @block.scalar
    def _(act):
        act.wait_ge(zeroed, 1)
        for at in range(0, width, 2048):
            act.dma_start(rows[:, at:at + 2048], zero[:]).then_inc(c.slots_cleared, 16)
        act.wait_ge(c.slots_cleared, 16 * (width // 2048))

    @block.vector
    def _(dve):
        dve.memset(zero[:], 0.0).then_inc(zeroed, 1)


def router0_stage(c, block, ctx, met_n):
    n = EXPERTS0
    s3 = [P, T, n]
    wr = c.sb(ctx, "w_router", [P, KD, n])
    gates = c.sb(ctx, "gates0", s3)
    slot = c.sb(ctx, "slot_of", s3)
    upto = c.sb(ctx, "taken_upto", s3)
    num_i = c.sb(ctx, "expert_groups_i", [P, n], I32)
    num = c.sb(ctx, "expert_groups", [P, n])
    last = c.sb(ctx, "expert_last", [P, n])
    first = c.sb(ctx, "expert_first", [P, n])
    real = c.sb(ctx, "real", [P, 2])
    at = c.sb(ctx, "slot_at", [P, T, CHOSEN])
    of = c.sb(ctx, "expert_of", [1, GROUPS0])
    loaded, ready, to_exp, exped, step, picked, ranked = (
        c.sem(ctx, f"router_{k}") for k in ("loaded", "logits", "shifted", "exped", "step", "picked", "counted"))
    met = c.met
    mask = [None]

    @block.vector
    def _(dve):
        ch = Chain(dve, step)
        dve.wait_ge(ready, 1)
        sel, pick = top2_gates(c, dve, ch, ctx, "0", c.bank[:, 0, 0:T * n].rearrange("p (t e) -> p t e", e=n), n,
                               gates[:], to_exp, exped)
        mask[0] = sel
        ch.then(dve.tensor_scalar(real[:, 0:1], c.part[:], float(LAST), None, ALU.is_lt))
        ch.then(dve.tensor_scalar(sel[:, T - 1, :], sel[:, T - 1, :], real[:, 0:1], None, ALU.mult))
        dve.sem_inc(picked, 1)
        dve.wait_ge(ranked, 1)
        total = c.bank[:, 1, 0:T * n].rearrange("p (t e) -> p t e", e=n)
        for e in range(n):
            ch.then(dve.tensor_tensor_scan(upto[:, :, e], c.ones[:, 0:T], total[:, :, e], 0.0, ALU.mult, ALU.add))
        ch.then(dve.tensor_scalar(num_i[:], upto[:, T - 1, :], float(GROUP - 1), None, ALU.add))
        ch.then(dve.tensor_scalar(num_i[:], num_i[:], GROUP.bit_length() - 1, None, ALU.logical_shift_right))
        ch.then(dve.tensor_copy(num[:], num_i[:]))
        ch.then(dve.tensor_tensor_scan(last[:], c.ones[:, 0:n], num[:], 0.0, ALU.mult, ALU.add))
        ch.then(dve.tensor_tensor(first[:], last[:], num[:], ALU.subtract))
        ch.then(dve.tensor_scalar(first[:], first[:], float(GROUP), None, ALU.mult))
        ch.then(dve.tensor_tensor(slot[:], upto[:], total, ALU.subtract))
        ch.then(dve.tensor_tensor(slot[:], slot[:], c.bank[:, 2, 0:T * n].rearrange("p (t e) -> p t e", e=n), ALU.add))
        ch.then(dve.tensor_tensor(slot[:], slot[:],
                                  first[:].rearrange("p (o e) -> p o e", o=1).to_broadcast(s3), ALU.add))
        ch.then(dve.memset(of[:], 0.0))
        for e in range(n):
            ch.then(dve.scalar_tensor_tensor(of[:], c.iota[0:1, 0:GROUPS0], last[0:1, e:e + 1], of[:],
                                             ALU.is_ge, ALU.add))
        ch.then(dve.tensor_scalar(c.group_expert[:], of[:], float(n - 1), None, ALU.min))
        ch.then(dve.tensor_scalar(pick[:, T - 1, :], pick[:, T - 1, :], real[:, 0:1], None, ALU.mult))
        for k in (1, 0):
            if k == 0:
                ch.then(dve.tensor_tensor(pick[:], sel[:], pick[:], ALU.subtract))
            ch.then(dve.tensor_tensor(upto[:], slot[:], pick[:], ALU.mult))
            ch.then(dve.tensor_reduce(at[:, :, k], upto[:], AX.X, ALU.add))
            ch.then(dve.tensor_tensor(upto[:], gates[:], pick[:], ALU.mult))
            ch.then(dve.tensor_reduce(c.gate_of[:, :, k], upto[:], AX.X, ALU.add))
        ch.then(dve.tensor_copy(c.slot_from[:], at[:]))
        ch.then(dve.tensor_scalar(real[:, 0:1], real[:, 0:1], -1.0, 1.0, ALU.mult, ALU.add))
        for k in range(CHOSEN):
            ch.then(dve.tensor_scalar(real[:, 1:2], c.part[:], float(SLOTS0 + k * P), real[:, 0:1], ALU.add, ALU.mult))
            ch.then(dve.tensor_scalar(at[:, T - 1, k:k + 1], at[:, T - 1, k:k + 1], real[:, 1:2], None, ALU.add))
        ch.then(dve.tensor_copy(c.slot_to[:], at[:]))
        dve.sem_inc(c.routed, 1)
        meet(dve, met, met_n)

    @block.sync
    def _(sp):
        sp.dma_start(wr[:], c.a["router0_w"].rearrange("(k p) n -> p k n", p=P)).then_inc(loaded, 16)
        meet(sp, met, met_n)

    @block.tensor
    def _(pe):
        pe.wait_ge(loaded, 16)
        for t in range(T):
            for k in range(KD):
                mm = pe.matmul(c.bank[:, 0, t * n:(t + 1) * n], c.xT[:, k, t * P:(t + 1) * P], wr[:, k, :],
                               start=k == 0, stop=k == KD - 1)
        mm.then_inc(ready, 1)
        pe.wait_ge(picked, 1)
        sel = mask[0][:].rearrange("p t e -> p (t e)")
        pe.matmul(c.bank[:, 1, 0:T * n], c.ones[:, 0:P], sel, start=True, stop=True)
        pe.matmul(c.bank[:, 2, 0:T * n], c.before[:], sel, start=True, stop=True).then_inc(ranked, 1)
        meet(pe, met, met_n)

    @block.scalar
    def _(act):
        act.wait_ge(to_exp, 1)
        act.activation(gates[:], gates[:], ACT.Exp).then_inc(exped, 1)
        meet(act, met, met_n)


EARLY = 11


def send_nodes0(c, block, ctx):
    sent = c.sem(ctx, "nodes_sent")

    @block.gpsimd
    def _(pool):
        pool.wait_ge(c.routed, 1)
        pool.wait_ge(c.slots_cleared, 16 * (SLOTS0 // P * D // 2048))
        for t in range(T):
            for k in range(CHOSEN):
                pool.indirect_dma_start(c.slot_x, bass.IndirectOffsetOnAxis(c.slot_to[:, t, k:k + 1], 0),
                                        c.XN[:, t, :], None).then_inc(sent, 16)
        pool.wait_ge(sent, 16 * T * CHOSEN)
        pool.sem_inc(c.sent_all, 1)


def fetch_outputs0(c, block, ctx):
    c.out_ring = c.sb(ctx, "expert_row_ring", [P, RING, D])
    c.ring_in = [c.sem(ctx, f"expert_row_in_{k}") for k in range(RING)]
    c.ring_used = c.sem(ctx, "expert_row_used")

    @block.gpsimd
    def _(pool):
        pool.wait_ge(c.outputs_stored, 1)
        for j in range(T * CHOSEN):
            if j >= RING:
                pool.wait_ge(c.ring_used, j - RING + 1)
            pool.indirect_dma_start(c.out_ring[:, j % RING, :], None, c.slot_y,
                                    bass.IndirectOffsetOnAxis(c.slot_from[:, j // CHOSEN, j % CHOSEN:j % CHOSEN + 1], 0))\
                .then_inc(c.ring_in[j % RING], 16)


def private_experts_stage(c, block, ctx, met_n):
    a, met, FC, SUB = c.a, c.met, FF0 // P, GROUP // P
    w1 = c.sb(ctx, "w1_private", [P, 2, KD, FF0])
    w2 = c.sb(ctx, "w2_private", [P, 2, FC, D])
    b1 = c.sb(ctx, "b1_private", [P, 2, FC])
    b2 = c.sb(ctx, "b2_private", [P, 2, D])
    rows = c.sb(ctx, "slot_rows", [P, 2, SUB, D])
    xT = c.sb(ctx, "slot_xT", [P, 2, KD, GROUP])
    hid = c.sb(ctx, "hidden_private", [P, FC, GROUP])
    y = c.sb(ctx, "slot_out", [P, 2, SUB, D])
    weights_in = [c.sem(ctx, f"weights_in_{k}") for k in range(2)]
    rows_in = [c.sem(ctx, f"slot_rows_in_{k}") for k in range(2)]
    stored = [c.sem(ctx, f"slot_out_stored_{k}") for k in range(2)]
    turned = c.sem(ctx, "slot_rows_turned")
    x_ready = c.sem(ctx, "slot_xT_ready")
    h_ready = c.sem(ctx, "hidden_ready_private")
    h_done = c.sem(ctx, "hidden_gelu_private")
    y_ready = c.sem(ctx, "out_ready_private")
    y_done = c.sem(ctx, "out_biased_private")
    pairs = GROUPS0 // 2

    @block.sync
    def _(sp):
        def load_rows(g, b):
            sp.dma_start(rows[:, b, :, :], c.slot_x[ds(g * GROUP, GROUP), :].rearrange("(j p) d -> p j d", p=P))\
                .then_inc(rows_in[b], 16)

        def load_weights(g, b):
            e = sp.value_load(c.group_expert[0:1, ds(g, 1)], min_val=0, max_val=EXPERTS0 - 1)
            sp.dma_start(w1[:, b, :, :], a["w1p"][ds(e, 1), :, :].rearrange("e (k p) f -> p (e k) f", p=P))\
                .then_inc(weights_in[b], 16)
            sp.dma_start(b1[:, b, :], a["b1_0"][:, ds(e * FC, FC)]).then_inc(weights_in[b], 16)
            sp.dma_start(b2[:, b, :], a["b2_0"][ds(e * D, D)].partition_broadcast(P)).then_inc(weights_in[b], 16)
            sp.dma_start(w2[:, b, :, :], a["w2p"][ds(e, 1), :, :].rearrange("e (f p) d -> p (e f) d", p=P))\
                .then_inc(weights_in[b], 16)

        def step(i, b, tail):
            g = i * 2 + b
            if not (tail and b == 1):
                sp.wait_ge(y_done, i * (2 * SUB) + (b * SUB + 2))
                load_weights(g + 1, 1 - b)
            if not tail:
                sp.wait_ge(turned, g + 1)
                load_rows(g + 2, b)
            sp.wait_ge(y_done, i * (2 * SUB) + (b + 1) * SUB + 2)
            sp.dma_start(c.slot_y[ds(g * GROUP, GROUP), :].rearrange("(j p) d -> p j d", p=P), y[:, b, :, :])\
                .then_inc(stored[b], 16)

        load_weights(0, 0)
        sp.wait_ge(c.sent_all, 1)
        load_rows(0, 0)
        load_rows(1, 1)
        with sp.Fori(0, pairs - 1) as i:
            step(i, 0, False)
            step(i, 1, False)
        step(pairs - 1, 0, True)
        step(pairs - 1, 1, True)
        for b in range(2):
            sp.wait_ge(stored[b], 16 * pairs + 16)
        sp.sem_inc(c.outputs_stored, 1)
        meet(sp, met, met_n)

    @block.tensor
    def _(pe):
        def turn(i, b):
            pe.wait_ge(rows_in[b], i * 16 + 16)
            pe.wait_ge(x_ready, i * 2 + b + 1)
            for j in range(SUB):
                for k in range(KD):
                    mm = pe.transpose(c.bank[:, 4 + b, k * GROUP + j * P:k * GROUP + (j + 1) * P],
                                      rows[:, b, j, k * P:(k + 1) * P], c.ident[:])
            mm.then_inc(turned, 1)

        def group(i, b, tail):
            pe.wait_ge(x_ready, i * 2 + b + 3)
            pe.wait_ge(weights_in[b], i * 64 + 64)
            for f in range(FC):
                pe.wait_ge(h_done, i * (2 * FC) + (b * FC + f + 1))
                for k in range(KD):
                    mm = pe.matmul(c.bank[:, f % 4, 0:GROUP], w1[:, b, k, f * P:(f + 1) * P], xT[:, b, k, :],
                                   start=k == 0, stop=k == KD - 1)
                mm.then_inc(h_ready, 1)
            if not (tail and b == 1):
                turn(i + b, 1 - b)
            for j in range(SUB):
                pe.wait_ge(y_done, i * (2 * SUB) + (b * SUB + j + 1))
                for f in range(FC):
                    if j == 0:
                        pe.wait_ge(h_done, i * (2 * FC) + (b * FC + f + 1 + 4))
                    mm = pe.matmul(c.bank[:, 6 + j, 0:D], hid[:, f, j * P:(j + 1) * P], w2[:, b, f, :],
                                   start=f == 0, stop=f == FC - 1)
                mm.then_inc(y_ready, 1)

        turn(0, 0)
        with pe.Fori(0, pairs - 1) as i:
            group(i, 0, False)
            group(i, 1, False)
        group(pairs - 1, 0, True)
        group(pairs - 1, 1, True)
        meet(pe, met, met_n)

    @block.scalar
    def _(act):
        act.sem_inc(h_done, 4)
        act.sem_inc(y_ready, 1)
        with act.Fori(0, pairs) as i:
            for b in range(2):
                act.wait_ge(weights_in[b], i * 64 + 64)
                act.wait_ge(y_ready, i * (2 * SUB) + (b * SUB + 1))
                for f in range(FC):
                    act.wait_ge(h_ready, i * (2 * FC) + (b * FC + f + 1))
                    act.activation(hid[:, f, :], c.bank[:, f % 4, 0:GROUP], ACT.Gelu, bias=b1[:, b, f:f + 1])\
                       .then_inc(h_done, 1)
        meet(act, met, met_n)

    @block.vector
    def _(dve):
        dve.sem_inc(x_ready, 2)
        dve.sem_inc(y_done, 2)
        dve.sem_inc(stored[0], 16)
        dve.sem_inc(stored[1], 16)

        def copy_xT(i, b):
            dve.wait_ge(turned, i * 2 + b + 1)
            dve.tensor_copy(xT[:, b, :, :].rearrange("p k n -> p (k n)"), c.bank[:, 4 + b, :]).then_inc(x_ready, 1)

        def group(i, b, tail):
            if not (tail and b == 1):
                copy_xT(i + b, 1 - b)
            dve.wait_ge(stored[b], i * 16 + 16)
            for j in range(SUB):
                dve.wait_ge(y_ready, i * (2 * SUB) + (b * SUB + j + 1 + 1))
                dve.tensor_tensor(y[:, b, j, :], c.bank[:, 6 + j, 0:D], b2[:, b, :], ALU.add).then_inc(y_done, 1)

        copy_xT(0, 0)
        with dve.Fori(0, pairs - 1) as i:
            group(i, 0, False)
            group(i, 1, False)
        group(pairs - 1, 0, True)
        group(pairs - 1, 1, True)
        for j in range(T * CHOSEN):
            dve.wait_ge(c.ring_in[j % RING], 16 * (j // RING + 1))
            if j >= 1:
                dve.wait_ge(c.ring_used, j)
            x = c.X[:, j // CHOSEN, :]
            dve.scalar_tensor_tensor(x, c.out_ring[:, j % RING, :], c.gate_of[:, j // CHOSEN, j % CHOSEN:j % CHOSEN + 1],
                                     x, ALU.mult, ALU.add).then_inc(c.ring_used, 1)
        meet(dve, met, met_n)


def experts_stage(c, block, ctx, name, met_n, F, experts, b1_rows, b2_rows, gates):
    E, FC = len(experts), F // P
    w1 = c.sb(ctx, f"w1_{name}", [P, 2, KD, F])
    w2 = c.sb(ctx, f"w2_{name}", [P, 2, FC, D])
    b1 = c.sb(ctx, f"b1_{name}", [P, E * FC])
    b2 = c.sb(ctx, f"b2_{name}", [P, E, D])
    hid = c.sb(ctx, f"hidden_{name}", [P, FC, 2, HALF_CHUNK])
    part = c.sb(ctx, f"expert_out_{name}", [P, 2, D])
    biases = c.sem(ctx, f"biases_loaded_{name}")
    loaded = [c.sem(ctx, f"expert_loaded_{name}_{k}") for k in range(2)]
    h_ready = c.sem(ctx, f"hidden_ready_{name}")
    h_done = c.sem(ctx, f"hidden_gelu_{name}")
    y_ready = c.sem(ctx, f"out_ready_{name}")
    y_done = c.sem(ctx, f"out_added_{name}")
    biased = c.sem(ctx, f"out_biased_{name}")
    met = c.met
    since = {0: 1, 4: 4}

    @block.sync
    def _(sp):
        sp.dma_start(b1[:], b1_rows).then_inc(biases, 16)
        sp.dma_start(b2[:].rearrange("p e d -> p (e d)"), b2_rows.partition_broadcast(P)).then_inc(biases, 16)
        for e, (W1, W2) in enumerate(experts):
            if e >= 2:
                sp.wait_ge(y_ready, (e - 1) * T)
            sp.dma_start(w1[:, e % 2, :, :], W1.rearrange("(k p) f -> p k f", p=P)).then_inc(loaded[e % 2], 16)
            sp.dma_start(w2[:, e % 2, :, :], W2.rearrange("(f p) d -> p f d", p=P)).then_inc(loaded[e % 2], 16)
        meet(sp, met, met_n)

    @block.tensor
    def _(pe):
        for e in range(E):
            pe.wait_ge(loaded[e % 2], 32 * (e // 2 + 1))
            with pe.Fori(0, CHUNKS) as i:
                for f in range(FC):
                    pe.wait_ge(h_done, i * FC + (e * CHUNKS * FC + f + 1))
                    for half in range(2):
                        for k in range(KD):
                            mm = pe.matmul(c.bank[:, 2 * (f % 2) + half, 0:HALF_CHUNK],
                                           w1[:, e % 2, k, f * P:(f + 1) * P],
                                           c.xT[:, k, ds(i * CHUNK + half * HALF_CHUNK, HALF_CHUNK)],
                                           start=k == 0, stop=k == KD - 1)
                    mm.then_inc(h_ready, 1)
                for t in range(CHUNK_TILES):
                    pe.wait_ge(y_done, i * CHUNK_TILES + (e * T + t + 1 + CHUNK_TILES - since.get(t, 5)))
                    for f in range(FC):
                        if t == 0:
                            pe.wait_ge(h_done, i * FC + (e * CHUNKS * FC + f + 1 + 2))
                        mm = pe.matmul(c.bank[:, 4 + t % 4, 0:D],
                                       hid[:, f, :, :].rearrange("p a n -> p (a n)")[:, t * P:(t + 1) * P],
                                       w2[:, e % 2, f, :], start=f == 0, stop=f == FC - 1)
                    mm.then_inc(y_ready, 1)
        meet(pe, met, met_n)

    @block.scalar
    def _(act):
        act.wait_ge(biases, 32)
        act.sem_inc(h_done, 2)
        for e in range(E):
            with act.Fori(0, CHUNKS) as i:
                act.wait_ge(y_ready, i * CHUNK_TILES + e * T)
                for f in range(FC):
                    act.wait_ge(h_ready, i * FC + (e * CHUNKS * FC + f + 1))
                    act.activation(hid[:, f, :, :], c.bank[:, 2 * (f % 2):2 * (f % 2) + 2, 0:HALF_CHUNK],
                                   ACT.Gelu, bias=b1[:, e * FC + f:e * FC + f + 1]).then_inc(h_done, 1)
        meet(act, met, met_n)

    @block.vector
    def _(dve):
        dve.wait_ge(biases, 32)
        dve.sem_inc(y_done, CHUNK_TILES)
        for e in range(E):
            with dve.Fori(0, CHUNKS) as i:
                for t in range(CHUNK_TILES):
                    tile = i * CHUNK_TILES + t
                    x = c.X[:, ds(tile, 1), :].rearrange("p a d -> p (a d)")
                    gate = 1.0 if gates is None else gates[:, ds(tile, 1), e:e + 1].rearrange("p a b -> p (a b)")
                    dve.wait_ge(y_ready, tile + (e * T + 1))
                    dve.wait_ge(y_done, tile + (e * T + CHUNK_TILES))
                    dve.tensor_tensor(part[:, 0, :], c.bank[:, 4 + t % 4, 0:D], b2[:, e, :], ALU.add)\
                        .then_inc(biased, 1)
                    dve.wait_ge(biased, tile + (e * T + 1))
                    dve.scalar_tensor_tensor(x, part[:, 0, :], gate, x, ALU.mult, ALU.add).then_inc(y_done, 1)
        meet(dve, met, met_n)




HEADS1, FEAT = 4, 64
MSG = FEAT + HEADS1
AGG = HEADS1 * (FEAT + 1)
INNER = 512
KV_GROUPS = 2 * INNER // FEAT


def table1_stage(c, block, ctx, met_n):
    a = c.a
    w_all = c.sb(ctx, "w_all", [P, KD, 2 * MSG])
    w_nat = c.sb(ctx, "w_nat", [FEAT, 2, D])
    att = c.sb(ctx, "att1", [FEAT, HEADS1])
    rows = c.sb(ctx, "table1_rows", [P, T, 2 * MSG])
    loaded, folded, copied, ready, out, stored = (c.sem(ctx, f"table1_{k}") for k in
                                                  ("loaded", "folded", "copied", "ready", "evacuated", "stored"))
    met = c.met

    @block.sync
    def _(sp):
        for i, d in enumerate(("wf", "wr")):
            sp.dma_start(w_all[:, :, i * MSG:i * MSG + FEAT], a[d + "_t"].rearrange("(k p) n -> p k n", p=P))\
              .then_inc(loaded, 16)
            sp.dma_start(w_nat[:, i, :], a[d]).then_inc(loaded, 16)
        sp.dma_start(att[:], a["att1_t"]).then_inc(loaded, 16)
        sp.wait_ge(out, T)
        sp.dma_start(c.table1.rearrange("(t p) w -> p t w", p=P), rows[:]).then_inc(stored, 16)
        sp.wait_ge(stored, 16)
        meet(sp, met, met_n)

    @block.tensor
    def _(pe):
        pe.wait_ge(loaded, 16 * 5)
        for i in range(2):
            for k in range(KD):
                mm = pe.matmul(c.bank[:, 7, (2 * i + k) * HEADS1:(2 * i + k + 1) * HEADS1],
                               w_nat[:, i, k * P:(k + 1) * P], att[:], start=True, stop=True)
        mm.then_inc(folded, 1)
        pe.wait_ge(copied, 1)
        for t in range(T):
            if t >= 4:
                pe.wait_ge(out, t - 3)
            for k in range(KD):
                mm = pe.matmul(c.bank[:, t % 4, 0:2 * MSG], c.xT[:, k, t * P:(t + 1) * P], w_all[:, k, :],
                               start=k == 0, stop=k == KD - 1)
            mm.then_inc(ready, 1)
        meet(pe, met, met_n)

    @block.scalar
    def _(act):
        for t in range(T):
            act.wait_ge(ready, t + 1)
            act.copy(rows[:, t, :], c.bank[:, t % 4, 0:2 * MSG]).then_inc(out, 1)
        meet(act, met, met_n)

    @block.vector
    def _(dve):
        dve.wait_ge(folded, 1)
        dve.wait_ge(loaded, 16 * 5)
        dve.tensor_copy(w_all[:].rearrange("p k (i m) -> p i k m", i=2)[:, :, :, FEAT:MSG],
                        c.bank[:, 7, 0:4 * HEADS1].rearrange("p (i k h) -> p i k h", i=2, k=KD)).then_inc(copied, 1)
        meet(dve, met, met_n)


def mix1_stage(c, block, ctx, met_n):
    a = c.a
    heads = INNER // FEAT
    pairs = INNER // P
    wkv = c.sb(ctx, "w_kv1", [P, KD, 2 * INNER])
    wq = c.sb(ctx, "w_q1", [P, pairs, D])
    wo = c.sb(ctx, "w_out1", [P, pairs, D])
    bo = c.sb(ctx, "b_out1", [P, D])
    kv = c.sb(ctx, "kv1", [P, 3, KV_GROUPS, FEAT])
    sq = c.sb(ctx, "kv_square", [P, 2, KV_GROUPS, FEAT])
    mean = c.sb(ctx, "weight_mean", [P, KD * KV_GROUPS])
    var = c.sb(ctx, "kv_var", [P, 2, KV_GROUPS])
    dots = c.sb(ctx, "dots", [P, pairs, P])
    mat = c.sb(ctx, "mat1", [P, pairs, D])
    mat2 = c.sb(ctx, "mat2", [P, KD, D])
    loaded, centred, kv_ready, squared, var_ready, rooted, normed, step = \
        (c.sem(ctx, f"mix1_{k}") for k in ("loaded", "centred", "kv_ready", "squared", "var", "rooted", "normed", "step"))
    kv_used, dots_ready, dots_out, mat_ready, mat_out, mat2_ready, mat2_out, y_ready, y_out = \
        (c.sem(ctx, f"mix1_{k}") for k in ("kv_used", "dots_ready", "dots_out", "mat_ready", "mat_out", "mat2_ready",
                                           "mat2_out", "y_ready", "y_out"))
    met = c.met
    raw_of = lambda t: c.bank[:, 2 * (t % 2):2 * (t % 2) + 2, :].rearrange("p a (g f) -> p (a g) f", f=FEAT)

    @block.sync
    def _(sp):
        sp.dma_start(wkv[:], a["wkv1_t"].rearrange("(k p) n -> p k n", p=P)).then_inc(loaded, 16)
        sp.dma_start(wq[:], a["wq1"].rearrange("(j p) n -> p j n", p=P)).then_inc(loaded, 16)
        sp.dma_start(wo[:], a["wout1_t"].rearrange("(j p) n -> p j n", p=P)).then_inc(loaded, 16)
        sp.dma_start(bo[:], a["bout1"].partition_broadcast(P)).then_inc(loaded, 16)
        meet(sp, met, met_n)

    @block.tensor
    def _(pe):
        pe.wait_ge(loaded, 64)
        pe.wait_ge(centred, 1)
        for t in range(T + 2):
            if t < T:
                b = 2 * (t % 2)
                if t >= 2:
                    pe.wait_ge(normed, t - 1)
                for half in range(2):
                    for k in range(KD):
                        mm = pe.matmul(c.bank[:, b + half, :], c.xT[:, k, t * P:(t + 1) * P],
                                       wkv[:, k, half * INNER:(half + 1) * INNER], start=k == 0, stop=k == KD - 1)
                mm.then_inc(kv_ready, 1)
            if t >= 2:
                u = t - 2
                n = P if u < T - 1 else LAST
                pe.wait_ge(normed, u + 1)
                row = kv[0:n, u % 3, :, :].rearrange("p g f -> p (g f)")
                for j in range(pairs):
                    mm = pe.matmul(c.bank[:, 4 + j, 0:P], row[:, INNER + j * P:INNER + (j + 1) * P],
                                   row[:, j * P:(j + 1) * P], start=u == 0, stop=u == T - 1)
                mm.then_inc(kv_used, 1)
        pe.wait_ge(dots_out, pairs)
        for j in range(pairs):
            pe.matmul(c.bank[:, j, 0:D], dots[:, j, :], wo[:, j, :], start=True, stop=True)\
              .then_inc(mat_ready, 1)
        pe.wait_ge(mat_out, pairs)
        for k in range(KD):
            for j in range(pairs):
                mm = pe.matmul(c.bank[:, 4 + k, 0:D], wq[:, j, k * P:(k + 1) * P], mat[:, j, :],
                               start=j == 0, stop=j == pairs - 1)
        mm.then_inc(mat2_ready, 1)
        pe.wait_ge(mat2_out, 1)
        for t in range(T):
            if t >= 4:
                pe.wait_ge(y_out, t - 3)
            for k in range(KD):
                mm = pe.matmul(c.bank[:, t % 4, 0:D], c.xT[:, k, t * P:(t + 1) * P], mat2[:, k, :],
                               start=k == 0, stop=k == KD - 1)
            mm.then_inc(y_ready, 1)
        meet(pe, met, met_n)

    @block.scalar
    def _(act):
        for t in range(T + 1):
            if t >= 1:
                r = (t - 1) % 2
                act.wait_ge(var_ready, t)
                act.activation(var[:, r, :], var[:, r, :], ACT.Sqrt).then_inc(rooted, 1)
            if t < T:
                act.wait_ge(kv_ready, t + 1)
                act.activation(sq[:, t % 2, :, :], raw_of(t), ACT.Square).then_inc(squared, 1)
        meet(act, met, met_n)

    @block.vector
    def _(dve):
        ch = Chain(dve, step)
        dve.wait_ge(loaded, 64)
        rows = wkv[:].rearrange("p k (g f) -> p (k g) f", f=FEAT)
        ch.then(dve.tensor_reduce(mean[:], rows, AX.X, ALU.add))
        ch.then(dve.tensor_scalar(mean[:], mean[:], 1.0 / FEAT, None, ALU.mult))
        dve.tensor_tensor(rows, rows, mean[:].rearrange("p (g o) -> p g o", o=1)
                          .to_broadcast([P, KD * KV_GROUPS, FEAT]), ALU.subtract).then_inc(centred, 1)
        for t in range(T + 1):
            if t >= 1:
                u, r = t - 1, (t - 1) % 2
                dve.wait_ge(rooted, t)
                ch.then(dve.reciprocal(var[:, r, :], var[:, r, :]))
                if u >= 3:
                    dve.wait_ge(kv_used, u - 2)
                dve.tensor_tensor(kv[:, u % 3, :, :], raw_of(u), var[:, r, :].rearrange("p (g o) -> p g o", o=1)
                                  .to_broadcast([P, KV_GROUPS, FEAT]), ALU.mult).then_inc(normed, 1)
            if t < T:
                r = t % 2
                dve.wait_ge(squared, t + 1)
                if t >= 2:
                    dve.wait_ge(normed, t - 1)
                ch.then(dve.tensor_reduce(var[:, r, :], sq[:, r, :, :], AX.X, ALU.add))
                dve.tensor_scalar(var[:, r, :], var[:, r, :], 1.0 / FEAT, 1e-5, ALU.mult, ALU.add)\
                    .then_inc(var_ready, 1)
        ch.then(dve.tensor_tensor(c.X[:], c.X[:], bo[:].rearrange("p (o d) -> p o d", o=1).to_broadcast([P, T, D]),
                                  ALU.add))
        dve.wait_ge(kv_used, T)
        for j in range(pairs):
            dve.tensor_tensor(dots[:, j, :], c.bank[:, 4 + j, 0:P], c.head64[:], ALU.mult).then_inc(dots_out, 1)
        for j in range(pairs):
            dve.wait_ge(mat_ready, j + 1)
            dve.tensor_copy(mat[:, j, :], c.bank[:, j, 0:D]).then_inc(mat_out, 1)
        dve.wait_ge(mat2_ready, 1)
        dve.tensor_scalar(mat2[:], c.bank[:, 4:4 + KD, 0:D], 1.0 / N, None, ALU.mult).then_inc(mat2_out, 1)
        for t in range(T):
            dve.wait_ge(y_ready, t + 1)
            dve.tensor_tensor(c.X[:, t, :], c.X[:, t, :], c.bank[:, t % 4, 0:D], ALU.add).then_inc(y_out, 1)
        meet(dve, met, met_n)




def messages_stage(c, block, ctx, e):
    tmp = c.sb(ctx, "reverse_part", [P, 2, MSG])
    used = c.sem(ctx, "rows_used1")
    half_way = c.sem(ctx, "reverse_part_ready")
    gather_rows(c, block, ctx, e, c.table1, 2 * MSG, used)

    @block.vector
    def _(dve):
        dve.sem_inc(used, RING)
        dve.wait_ge(e.slot_in, 16)
        with dve.Fori(0, e.tiles // RING) as i:
            for k in range(RING + 1):
                if k < RING:
                    dve.wait_ge(e.gathered[k], i * 16 + 16)
                    col = e.slot[:, ds(i * RING + k, 1), 3:4].rearrange("p t o -> p (t o)")
                    if k >= 2:
                        dve.wait_ge(used, i * RING + (RING + k - 1))
                    dve.tensor_scalar(tmp[:, k % 2, :], e.rows_in[:, k, MSG:2 * MSG], col, None, ALU.mult)\
                        .then_inc(half_way, 1)
                if k >= 1:
                    j = k - 1
                    dve.wait_ge(half_way, i * RING + (j + 1))
                    col = e.slot[:, ds(i * RING + j, 1), 2:3].rearrange("p t o -> p (t o)")
                    dve.scalar_tensor_tensor(c.msg[:, ds(i * RING + j, 1), :].rearrange("p a m -> p (a m)"),
                                             e.rows_in[:, j, 0:MSG], col, tmp[:, j % 2, :], ALU.mult, ALU.add)\
                        .then_inc(used, 1)
            dve.wait_ge(used, i * RING + 2 * RING)


def softmax1_stage(c, block, ctx, e, met_n):
    none = c.sb(ctx, "no_edge", [P, e.tiles])
    top = c.sb(ctx, "score_top", [P, HEADS1])
    top4 = c.sb(ctx, "score_max", [HEADS1, 1])
    diag = c.sb(ctx, "score_diag", [HEADS1, HEADS1])
    step, top_ready, turned, diag_ready, spread, shifted, exped = \
        (c.sem(ctx, f"softmax1_{k}") for k in ("step", "top", "turned", "diag", "spread", "shifted", "exped"))
    met = c.met

    @block.tensor
    def _(pe):
        pe.wait_ge(top_ready, 1)
        pe.transpose(c.bank[0:HEADS1, 0, 0:P], top[:], c.ident[:]).then_inc(turned, 1)
        pe.wait_ge(diag_ready, 1)
        pe.matmul(c.bank[:, 1, 0:HEADS1], c.ones[0:HEADS1, 0:P], diag[:], start=True, stop=True).then_inc(spread, 1)
        meet(pe, met, met_n)

    @block.scalar
    def _(act):
        act.wait_ge(shifted, 1)
        act.activation(c.prob[:], c.prob[:], ACT.Exp).then_inc(exped, 1)
        act.wait_ge(exped, 1)
        meet(act, met, met_n)

    @block.sync
    def _(sp):
        meet(sp, met, met_n)

    @block.vector
    def _(dve):
        ch = Chain(dve, step)
        s = c.msg[:, :, FEAT:MSG]
        ch.then(dve.tensor_scalar(none[:], e.slot[:, :, 1], 0.0, NEG, ALU.is_lt, ALU.mult))
        ch.then(dve.scalar_tensor_tensor(c.prob[:], s, 0.2, s, ALU.mult, ALU.max))
        ch.then(dve.tensor_tensor(c.prob[:], c.prob[:],
                                  none[:].rearrange("p (t o) -> p t o", o=1).to_broadcast([P, e.tiles, HEADS1]),
                                  ALU.add))
        ch.then(dve.memset(c.msg[:, :, FEAT:FEAT + 1], 1.0))
        dve.tensor_reduce(top[:], c.prob[:].rearrange("p t h -> p h t"), AX.X, ALU.max).then_inc(top_ready, 1)
        dve.wait_ge(turned, 1)
        ch.then(dve.tensor_reduce(top4[:], c.bank[0:HEADS1, 0, 0:P], AX.X, ALU.max))
        dve.tensor_scalar(diag[:], c.ident[0:HEADS1, 0:HEADS1], top4[:], None, ALU.mult).then_inc(diag_ready, 1)
        dve.wait_ge(spread, 1)
        dve.tensor_tensor(c.prob[:], c.prob[:],
                          c.bank[:, 1:2, 0:HEADS1].to_broadcast([P, e.tiles, HEADS1]), ALU.subtract)\
            .then_inc(shifted, 1)
        ch.then(dve.memset(c.agg[:], 0.0))
        meet(dve, met, met_n)


def sum1_stage(c, block, ctx, e):
    hot = c.sb(ctx, "one_hot1", [P, RING, P])
    val = c.sb(ctx, "weighted1", [P, RING, HEADS1, FEAT + 1])
    den = c.sb(ctx, "weight_sum", [P, T * HEADS1])
    used = c.sem(ctx, "halves_summed1")
    hot_ready = c.sem(ctx, "one_hots_ready1")
    val_dve, val_pool = c.sem(ctx, "weighted_dve"), c.sem(ctx, "weighted_pool")
    added = c.sem(ctx, "group_added1")
    step = c.sem(ctx, "mean1_step")
    per = GROUP // P
    steps = e.tiles // RING
    half_groups = HALF // per
    own = 1

    def weigh(eng, i, at, n, sem):
        shape = [P, n, HEADS1, FEAT + 1]
        m = c.msg[:, ds(i * RING + at, n), 0:FEAT + 1].rearrange("p t (o f) -> p t o f", o=1).to_broadcast(shape)
        w = c.prob[:, ds(i * RING + at, n), :].rearrange("p t (h o) -> p t h o", o=1).to_broadcast(shape)
        eng.tensor_tensor(val[:, at:at + n, :, :], m, w, ALU.mult).then_inc(sem, 1)

    @block.gpsimd
    def _(pool):
        pool.wait_ge(c.met, 4 * c.softmax1_met)

        def round_of(i):
            for h in range(2):
                pool.wait_ge(used, i * 2 + h + 1)
                weigh(pool, i, HALF * h + own, HALF - own, val_pool)

        in_turns(pool, 0, steps, round_of)

    @block.tensor
    def _(pe):
        pe.sem_inc(used, 2)
        with pe.Fori(0, steps) as i:
            for h in range(2):
                pe.wait_ge(hot_ready, i * 2 + h + 1)
                pe.wait_ge(val_dve, i * 2 + h + 1)
                pe.wait_ge(val_pool, i * 2 + h + 1)
                pe.wait_ge(added, i * BODY_GROUPS + half_groups * (h + 1))
                for k in range(HALF * h, HALF * h + HALF):
                    mm = pe.matmul(c.bank[:, k // per, 0:AGG], hot[:, k, :], val[:, k, :, :].rearrange("p h f -> p (h f)"),
                                   start=k % per == 0, stop=k % per == per - 1)
                mm.then_inc(used, 1)

    @block.vector
    def _(dve):
        ch = Chain(dve, step)
        dve.sem_inc(added, BODY_GROUPS)

        def prepare(i, h):
            dve.wait_ge(used, i * 2 + h + 1)
            one_hots_of_half(dve, c, e, hot, i, h).then_inc(hot_ready, 1)
            weigh(dve, i, HALF * h, own, val_dve)

        def add_half(i, h, tiles):
            dve.wait_ge(used, i * 2 + h + 1)
            for k, tile in enumerate(tiles):
                g = half_groups * h + k
                dve.wait_ge(added, i * BODY_GROUPS + g)
                x = c.agg[:, ds(tile, 1), :].rearrange("p a d -> p (a d)")
                dve.tensor_tensor(x, c.bank[:, g, 0:AGG], x, ALU.add).then_inc(added, 1)

        prepare(0, 0)
        prepare(0, 1)
        later_rounds(dve, c, e, steps, prepare, add_half)
        dve.wait_ge(added, BODY_GROUPS * (steps + 1))
        agg = c.agg[:].rearrange("p t (h f) -> p (t h) f", f=FEAT + 1)
        ch.then(dve.tensor_scalar(den[:], agg[:, :, FEAT], 1e-10, None, ALU.add))
        ch.then(dve.reciprocal(den[:], den[:]))
        ch.then(dve.tensor_tensor(agg[:, :, 0:FEAT], agg[:, :, 0:FEAT],
                                  den[:].rearrange("p (g o) -> p g o", o=1).to_broadcast([P, T * HEADS1, FEAT]),
                                  ALU.mult))
        x = c.X[:].rearrange("p t (h f) -> p (t h) f", f=FEAT)
        ch.then(dve.tensor_tensor(x, x, agg[:, :, 0:FEAT], ALU.add))




NE1 = 4
HID_G = NE1 * NE1
ROW_G = HID_G + NE1
FAR = NE1


def table_g_stage(c, block, ctx, met_n):
    a = c.a
    w = c.sb(ctx, "w_gat", [P, KD, HID_G])
    att = c.sb(ctx, "att_gat", [P, 2, HID_G])
    prod = c.sb(ctx, "att_prod", [P, T, HID_G])
    low = c.sb(ctx, "low", [P, 1])
    lowd = c.sb(ctx, "low_diag", [P, P])
    loaded, ready, step, stored, out, low_ready, low_back = \
        (c.sem(ctx, f"table_g_{k}") for k in ("loaded", "ready", "step", "stored", "out", "low", "low_back"))
    met = c.met
    h = c.tab[:, :, 0:HID_G]
    a_src = c.tab[:, :, HID_G:ROW_G]

    @block.sync
    def _(sp):
        sp.dma_start(w[:], a["w_gat"].rearrange("(k p) n -> p k n", p=P)).then_inc(loaded, 16)
        sp.dma_start(att[:, 0, :], a["att_src"].partition_broadcast(P)).then_inc(loaded, 16)
        sp.dma_start(att[:, 1, :], a["att_dst"].partition_broadcast(P)).then_inc(loaded, 16)
        sp.wait_ge(out, 1)
        sp.dma_start(c.table_g.rearrange("(t p) w -> p t w", p=P), c.tab[:]).then_inc(stored, 16)
        sp.wait_ge(stored, 16)
        meet(sp, met, met_n)

    @block.scalar
    def _(act):
        meet(act, met, met_n)

    @block.tensor
    def _(pe):
        pe.wait_ge(loaded, 48)
        for t in range(T):
            for k in range(KD):
                mm = pe.matmul(c.bank[:, 0, t * HID_G:(t + 1) * HID_G], c.xT[:, k, t * P:(t + 1) * P], w[:, k, :],
                               start=k == 0, stop=k == KD - 1)
        mm.then_inc(ready, 1)
        pe.wait_ge(low_ready, 1)
        pe.transpose(c.bank[0:1, 1, 0:P], low[:], c.ident[:]).then_inc(low_back, 1)
        pe.wait_ge(low_ready, 2)
        pe.matmul(c.bank[:, 2, 0:1], c.ones[0:1, 0:P], lowd[0:1, 0:1], start=True, stop=True).then_inc(low_back, 1)
        meet(pe, met, met_n)

    @block.vector
    def _(dve):
        ch = Chain(dve, step)
        shape = [P, T, HID_G]
        dve.wait_ge(ready, 1)
        ch.then(dve.tensor_copy(h, c.bank[:, 0, 0:T * HID_G].rearrange("p (t n) -> p t n", n=HID_G)))
        for i, to in ((0, a_src), (1, c.edge_tab[:, :, 0:NE1])):
            ch.then(dve.tensor_tensor(prod[:], h, att[:, i:i + 1, :].to_broadcast(shape), ALU.mult))
            ch.then(dve.tensor_reduce(to, prod[:].rearrange("p t (h e) -> p t h e", e=NE1), AX.X, ALU.add))
        dve.sem_inc(out, 1)
        dve.tensor_reduce(low[:], a_src, AX.XY, ALU.min).then_inc(low_ready, 1)
        dve.wait_ge(low_back, 1)
        dve.tensor_reduce(lowd[0:1, 0:1], c.bank[0:1, 1, 0:P], AX.X, ALU.min).then_inc(low_ready, 1)
        dve.wait_ge(low_back, 2)
        ch.then(dve.tensor_scalar(c.lift[:], c.bank[:, 2, 0:1], -1.0, 1.0, ALU.mult, ALU.add))
        ch.then(dve.tensor_scalar(c.high[:], a_src, c.lift[:], None, ALU.add))
        meet(dve, met, met_n)


def segment_max_stage(c, block, ctx, e):
    per = GROUP // P
    hot = c.sb(ctx, "one_hot_m", [P, RING, P])
    lifted = c.sb(ctx, "lifted", [P, RING, NE1])
    diag = c.sb(ctx, "score_diags", [P, RING, NE1, P])
    mx = c.sb(ctx, "group_max", [P, BODY_GROUPS, NE1])
    used = c.sem(ctx, "rows_used_g")
    lift_ready = c.sem(ctx, "lifted_ready")
    hot_ready = c.sem(ctx, "one_hot_ready_m")
    diag_ready = c.sem(ctx, "diag_ready")
    spread = c.sem(ctx, "scores_spread")
    taken = c.sem(ctx, "spread_taken")
    mx_step = c.sem(ctx, "group_max_taken_in")
    steps = e.tiles // RING
    half_groups = HALF // per
    own = 1
    gather_rows(c, block, ctx, e, c.table_g, ROW_G, used)

    @block.scalar
    def _(act):
        with act.Fori(0, steps) as i:
            for half in range(2):
                at = half * HALF
                for k in range(at, at + HALF):
                    act.wait_ge(e.gathered[k], i * 16 + 16)
                act.wait_ge(spread, i * 2 + half + 1)
                act.activation(lifted[:, at:at + HALF, :], e.rows_in[:, at:at + HALF, HID_G:ROW_G], ACT.Identity,
                               bias=c.lift[:]).then_inc(lift_ready, 1)
                act.copy(c.rows_g[:, ds(i * RING + at, HALF), :], e.rows_in[:, at:at + HALF, :])\
                    .then_inc(used, HALF)
                act.wait_ge(lift_ready, i * 2 + half + 1)
                for k in range(HALF * half + own, HALF * half + HALF):
                    for h in range(NE1):
                        op = act.activation(diag[:, k, h, :], c.ident[:], ACT.Copy, scale=lifted[:, k, h:h + 1])
                op.then_inc(diag_ready, 1)

    @block.tensor
    def _(pe):
        pe.sem_inc(spread, 2)
        with pe.Fori(0, steps) as i:
            for half in range(2):
                pe.wait_ge(taken, i * BODY_GROUPS + half_groups * (half + 1))
                pe.wait_ge(hot_ready, i * 2 + half + 1)
                pe.wait_ge(diag_ready, i * 2 + half + 1)
                for k in range(HALF * half, HALF * half + HALF):
                    mm = pe.matmul(c.bank[:, k, :], hot[:, k, :], diag[:, k, :, :].rearrange("p h n -> p (h n)"),
                                   start=True, stop=True)
                mm.then_inc(spread, 1)

    @block.vector
    def _(dve):
        dve.sem_inc(used, RING)
        dve.sem_inc(taken, BODY_GROUPS)
        dve.sem_inc(mx_step, 1)
        dve.wait_ge(e.slot_in, 16)

        def prepare(i, half):
            at = half * HALF
            dve.wait_ge(spread, i * 2 + half + 1)
            dve.wait_ge(lift_ready, i * 2 + half + 1)
            shape = [P, NE1, P]
            for k in range(at, at + own):
                dve.tensor_tensor(diag[:, k, :, :], c.ident[:].rearrange("p (o n) -> p o n", o=1).to_broadcast(shape),
                                  lifted[:, k, :].rearrange("p (h o) -> p h o", o=1).to_broadcast(shape), ALU.mult)
            one_hots_of_half(dve, c, e, hot, i, half).then_inc(hot_ready, 1)

        def take_max(i, half, tiles):
            dve.wait_ge(spread, i * 2 + half + 1)
            for k in range(half_groups):
                b = half_groups * half + k
                dve.tensor_reduce(mx[:, b, :], c.bank[:, per * b:per * b + per, :].rearrange("p a (h n) -> p h a n", h=NE1),
                                  AX.XY, ALU.max).then_inc(taken, 1)
            for k, tile in enumerate(tiles):
                g = half_groups * half + k
                high = c.high[:, ds(tile, 1), :].rearrange("p a h -> p (a h)")
                dve.wait_ge(taken, i * BODY_GROUPS + (g + 1))
                dve.wait_ge(mx_step, i * BODY_GROUPS + (g + 1 - BODY_GROUPS))
                dve.tensor_tensor(high, high, mx[:, g, :], ALU.max).then_inc(mx_step, 1)

        prepare(0, 0)
        prepare(0, 1)
        later_rounds(dve, c, e, steps, prepare, take_max)


PARTS = 3


def sum_g_stage(c, block, ctx, e, met_n):
    a = c.a
    top = c.sb(ctx, "edge_max", [P, T, NE1])
    none = c.sb(ctx, "no_edge_g", [P, e.tiles])
    hot = c.sb(ctx, "one_hot_g", [P, RING, P])
    hot16 = c.sb(ctx, "one_hot16", [P, RING, P], BF16)
    hot_t = c.sb(ctx, "one_hot_t", [P, RING, P], BF16)
    ident16 = c.sb(ctx, "ident16", [P, P], BF16)
    tab16 = c.sb(ctx, "target_parts", [P, T, PARTS, 2 * NE1], BF16)
    rest = c.sb(ctx, "target_rest", [P, T, 2 * NE1])
    at_parts = c.sb(ctx, "target_parts_at_slot", [P, e.tiles, PARTS, 2 * NE1])
    at_slot = c.sb(ctx, "target_at_slot", [P, e.tiles, 2 * NE1])
    z = c.sb(ctx, "edge_score", [P, e.tiles, NE1])
    agg = c.sb(ctx, "agg_g", [P, T, ROW_G])
    own = c.sb(ctx, "own_weight", [P, T, NE1])
    step, z_ready, z_exped = (c.sem(ctx, f"sum_g_{k}") for k in ("step", "shifted", "exped"))
    tab_ready = c.sem(ctx, "targets_table_ready")
    hot_ready = c.sem(ctx, "one_hot_ready_g")
    turned = c.sem(ctx, "one_hot_turned_g")
    t_copied = c.sem(ctx, "one_hot_t_copied")
    spread = c.sem(ctx, "targets_spread")
    kept = c.sem(ctx, "targets_kept")
    hot2_ready = c.sem(ctx, "one_hot_ready_g2")
    used = c.sem(ctx, "halves_summed_g")
    added = c.sem(ctx, "group_added_g")
    weighted = c.sem(ctx, "weighted_g")
    met = c.met
    per = GROUP // P
    steps = e.tiles // RING
    src = c.tab[:, :, HID_G:ROW_G]
    far = c.edge_tab[:, :, 0:NE1]
    et = c.edge_tab[:, :, NE1:2 * NE1]
    half_groups = HALF // per
    width = PARTS * 2 * NE1
    turned_bank = lambda h: c.bank[:, h, 0:HALF * P // 2].bitcast(BF16)

    @block.scalar
    def _(act):
        act.wait_ge(z_ready, 1)
        act.activation(own[:], own[:], ACT.Exp).then_inc(z_exped, 1)
        act.sem_inc(t_copied, 2)
        act.sem_inc(kept, 2)

        def copy_t(i, h):
            act.wait_ge(turned, i * 2 + (h + 3))
            act.copy(hot_t[:, HALF * h:HALF * h + HALF, :], turned_bank(h).rearrange("p (a n) -> p a n", n=P))\
               .then_inc(t_copied, 1)

        def keep(i, h):
            act.wait_ge(spread, i * 2 + (h + 1))
            act.copy(at_parts[:, ds(i * RING + h * HALF, HALF), :, :].rearrange("p k q w -> p (k q w)"),
                     c.bank[:, 2 + h % 2, 0:HALF * width])\
               .then_inc(kept, 1)

        copy_t(0, 0)
        copy_t(0, 1)
        keep(0, 0)

        def round_of(i):
            copy_t(i, 0)
            keep(i, -1)
            copy_t(i, 1)
            keep(i, 0)

        in_turns(act, 1, steps, round_of)
        keep(steps, -1)
        act.wait_ge(z_ready, 2)
        act.activation(z[:], z[:], ACT.Exp).then_inc(z_exped, 1)
        meet(act, met, met_n)

    @block.tensor
    def _(pe):
        pe.sem_inc(turned, 2)
        pe.sem_inc(used, 2)

        def turn(i, h):
            pe.wait_ge(t_copied, i * 2 + (h + 1))
            pe.wait_ge(hot_ready, i * 2 + h + 1)
            for k in range(HALF * h, HALF * h + HALF):
                mm = pe.transpose(turned_bank(h)[:, (k % HALF) * P:(k % HALF + 1) * P], hot16[:, k, :], ident16[:])
            mm.then_inc(turned, 1)

        def spread_half(i, h):
            pe.wait_ge(t_copied, i * 2 + (h + 3))
            pe.wait_ge(kept, i * 2 + (h + 1))
            tiles = tiles_of_groups(c, mybir.EngineType.PE, e, i * BODY_GROUPS + h * half_groups, half_groups)
            for k in range(HALF):
                tile = tiles[k // per]
                mm = pe.matmul(c.bank[:, 2 + h % 2, k * width:(k + 1) * width], hot_t[:, HALF * (h % 2) + k, :],
                               tab16[:, ds(tile, 1), :, :].rearrange("p a q w -> p (a q w)"), start=True, stop=True)
            mm.then_inc(spread, 1)

        pe.wait_ge(tab_ready, 1)
        turn(0, 0)
        turn(0, 1)
        spread_half(0, 0)

        def spread_round(i):
            turn(i, 0)
            spread_half(i, -1)
            turn(i, 1)
            spread_half(i, 0)

        in_turns(pe, 1, steps, spread_round)
        spread_half(steps, -1)
        pe.wait_ge(weighted, 1)

        def sum_round(i):
            for h in range(2):
                pe.wait_ge(hot2_ready, i * 2 + h + 1)
                pe.wait_ge(added, i * BODY_GROUPS + half_groups * (h + 1))
                for k in range(HALF * h, HALF * h + HALF):
                    mm = pe.matmul(c.bank[:, 4 + k // per, 0:ROW_G], hot[:, k, :],
                                   c.rows_g[:, ds(i * RING + k, 1), :].rearrange("p a w -> p (a w)"),
                                   start=k % per == 0, stop=k % per == per - 1)
                mm.then_inc(used, 1)

        in_turns(pe, 0, steps, sum_round)
        meet(pe, met, met_n)

    @block.sync
    def _(sp):
        sp.dma_start(c.row_g[:, 0, :], a["b_gat"].partition_broadcast(P)).then_inc(c.row_g_in, 16)
        sp.dma_start(c.row_g[:, 1, :], a["ln_gamma"].partition_broadcast(P)).then_inc(c.row_g_in, 16)
        sp.dma_start(c.row_g[:, 2, :], a["ln_beta"].partition_broadcast(P)).then_inc(c.row_g_in, 16)
        meet(sp, met, met_n)

    @block.vector
    def _(dve):
        ch = Chain(dve, step)
        lift_b = c.lift[:]
        dve.sem_inc(added, BODY_GROUPS)

        def one_hots(i, h, free, ready, hot=hot):
            dve.wait_ge(free, i * 2 + h + 1)
            one_hots_of_half(dve, c, e, hot, i, h).then_inc(ready, 1)

        ch.then(dve.tensor_scalar(top[:], c.high[:], lift_b, None, ALU.subtract))
        ch.then(dve.tensor_tensor(top[:], top[:], far, ALU.add))
        ch.then(dve.scalar_tensor_tensor(et, top[:], 0.2, top[:], ALU.mult, ALU.max))
        ch.then(dve.tensor_copy(ident16[:], c.ident[:]))
        ch.then(dve.tensor_copy(rest[:], c.edge_tab[:]))
        for q in range(PARTS):
            ch.then(dve.tensor_copy(tab16[:, :, q, :], rest[:]))
            if q < PARTS - 1:
                ch.then(dve.tensor_tensor(rest[:], rest[:], tab16[:, :, q, :], ALU.subtract))
        dve.sem_inc(tab_ready, 1)
        ch.then(dve.tensor_tensor(own[:], src, far, ALU.add))
        ch.then(dve.scalar_tensor_tensor(own[:], own[:], 0.2, own[:], ALU.mult, ALU.max))
        dve.tensor_tensor(own[:], own[:], et, ALU.subtract).then_inc(z_ready, 1)

        def hot_round(i):
            for h in range(2):
                one_hots(i, h, turned, hot_ready, hot16)

        in_turns(dve, 0, steps, hot_round)
        ch.then(dve.tensor_scalar(none[:], e.slot[:, :, 1], 0.0, NEG, ALU.is_lt, ALU.mult))
        dve.wait_ge(z_exped, 1)
        ch.then(dve.tensor_tensor(agg[:, :, 0:HID_G].rearrange("p t (h e) -> p t h e", e=NE1),
                                  c.tab[:, :, 0:HID_G].rearrange("p t (h e) -> p t h e", e=NE1),
                                  own[:].rearrange("p t (h o) -> p t h o", o=1).to_broadcast([P, T, NE1, NE1]),
                                  ALU.mult))
        ch.then(dve.tensor_copy(agg[:, :, HID_G:ROW_G], own[:]))
        dve.wait_ge(kept, 2 * steps + 2)
        ch.then(dve.tensor_tensor(at_slot[:], at_parts[:, :, 2, :], at_parts[:, :, 1, :], ALU.add))
        ch.then(dve.tensor_tensor(at_slot[:], at_slot[:], at_parts[:, :, 0, :], ALU.add))
        ch.then(dve.tensor_tensor(z[:], c.rows_g[:, :, HID_G:ROW_G], at_slot[:, :, 0:NE1], ALU.add))
        ch.then(dve.scalar_tensor_tensor(z[:], z[:], 0.2, z[:], ALU.mult, ALU.max))
        ch.then(dve.tensor_tensor(z[:], z[:], at_slot[:, :, NE1:2 * NE1], ALU.subtract))
        dve.tensor_tensor(z[:], z[:], none[:].rearrange("p (t o) -> p t o", o=1).to_broadcast([P, e.tiles, NE1]),
                          ALU.add).then_inc(z_ready, 1)
        dve.wait_ge(z_exped, 2)
        for h in range(NE1):
            ch.then(dve.tensor_tensor(c.rows_g[:, :, h * NE1:(h + 1) * NE1], c.rows_g[:, :, h * NE1:(h + 1) * NE1],
                                      z[:, :, h:h + 1].to_broadcast([P, e.tiles, NE1]), ALU.mult))
        ch.then(dve.tensor_copy(c.rows_g[:, :, HID_G:ROW_G], z[:]))
        dve.sem_inc(weighted, 1)

        def add_half(i, h, tiles):
            dve.wait_ge(used, i * 2 + h + 1)
            for k, tile in enumerate(tiles):
                g = half_groups * h + k
                dve.wait_ge(added, i * BODY_GROUPS + g)
                x = agg[:, ds(tile, 1), :].rearrange("p a d -> p (a d)")
                dve.tensor_tensor(x, c.bank[:, 4 + g, 0:ROW_G], x, ALU.add).then_inc(added, 1)

        one_hots(0, 0, used, hot2_ready)
        one_hots(0, 1, used, hot2_ready)
        later_rounds(dve, c, e, steps, lambda i, h: one_hots(i, h, used, hot2_ready), add_half)
        dve.wait_ge(added, BODY_GROUPS * (steps + 1))
        ch.then(dve.tensor_scalar(own[:], agg[:, :, HID_G:ROW_G], 1e-16, None, ALU.add))
        ch.then(dve.reciprocal(own[:], own[:]))
        ch.then(dve.tensor_tensor(c.score16[:].rearrange("p t (h e) -> p t h e", e=NE1),
                                  agg[:, :, 0:HID_G].rearrange("p t (h e) -> p t h e", e=NE1),
                                  own[:].rearrange("p t (h o) -> p t h o", o=1).to_broadcast([P, T, NE1, NE1]),
                                  ALU.mult))
        meet(dve, met, met_n)


def gates1_stage(c, block, ctx, met_n):
    sq = c.sb(ctx, "score_square", [P, T, HID_G])
    m = c.sb(ctx, "score_mean", [P, T])
    v = c.sb(ctx, "score_var", [P, T])
    s4 = c.sb(ctx, "score4", [P, T, NE1])
    step, var_ready, rooted, to_exp, exped = (c.sem(ctx, f"gates1_{k}") for k in
                                              ("step", "var", "rooted", "shifted", "exped"))
    met = c.met
    shape = [P, T, HID_G]

    @block.scalar
    def _(act):
        act.wait_ge(var_ready, 1)
        act.activation(v[:], v[:], ACT.Sqrt).then_inc(rooted, 1)
        act.wait_ge(to_exp, 1)
        act.activation(c.gates1[:], c.gates1[:], ACT.Exp).then_inc(exped, 1)
        meet(act, met, met_n)

    @block.tensor
    def _(pe):
        meet(pe, met, met_n)

    @block.sync
    def _(sp):
        meet(sp, met, met_n)

    @block.vector
    def _(dve):
        ch = Chain(dve, step)
        s = c.score16[:]
        wide = lambda b: b[:].rearrange("p (t o) -> p t o", o=1).to_broadcast(shape)
        row = lambda i: c.row_g[:, i:i + 1, :].to_broadcast(shape)
        dve.wait_ge(c.row_g_in, 48)
        ch.then(dve.tensor_tensor(s, s, row(0), ALU.add))
        ch.then(dve.tensor_reduce(m[:], s, AX.X, ALU.add))
        ch.then(dve.tensor_scalar(m[:], m[:], 1.0 / HID_G, None, ALU.mult))
        ch.then(dve.tensor_tensor(s, s, wide(m), ALU.subtract))
        ch.then(dve.tensor_tensor(sq[:], s, s, ALU.mult))
        ch.then(dve.tensor_reduce(v[:], sq[:], AX.X, ALU.add))
        dve.tensor_scalar(v[:], v[:], 1.0 / HID_G, 1e-5, ALU.mult, ALU.add).then_inc(var_ready, 1)
        dve.wait_ge(rooted, 1)
        ch.then(dve.reciprocal(v[:], v[:]))
        ch.then(dve.tensor_tensor(s, s, wide(v), ALU.mult))
        ch.then(dve.tensor_tensor(s, s, row(1), ALU.mult))
        ch.then(dve.tensor_tensor(s, s, row(2), ALU.add))
        ch.then(dve.tensor_reduce(s4[:], s.rearrange("p t (h e) -> p t e h", e=NE1), AX.X, ALU.add))
        ch.then(dve.tensor_scalar(s4[:], s4[:], 1.0 / NE1, None, ALU.mult))
        top2_gates(c, dve, ch, ctx, "1", s4[:], NE1, c.gates1[:], to_exp, exped)
        meet(dve, met, met_n)




def build(nc, a, out, upto=4):
    c = Core(nc, a, out)
    c.upto = upto
    with ExitStack() as top:
        top.enter_context(nc.allow_non_contiguous_dma("small strided rows"))
        c.kept.append(top)
        stage_setup(c, top)
        c.support = nc.dram_tensor("support", [NP, D], F32, kind="Internal").ap()
        c.slot_x = nc.dram_tensor("slot_x", [SLOTS0 + CHOSEN * P, D], F32, kind="Internal").ap()
        c.slot_y = nc.dram_tensor("slot_y", [SLOTS0, D], F32, kind="Internal").ap()
        c.slots_cleared = c.sem(top, "slots_cleared")
        e1 = Edges(c, "gnn1", a["dst"], a["src"], a["edge_attr_2"], 125, top)
        eg = Edges(c, "router", a["router_dst"], a["router_src"], None, P, top)
        records = top.enter_context(ExitStack())
        e1.hold_records(c, records)
        eg.hold_records(c, records)
        with ExitStack() as l0:
            c.kept.append(l0)
            e0 = Edges(c, "gnn0", a["src"], a["dst"], a["edge_weight"], 125, l0, group=P)
            e0.hold_records(c, l0)
            with ExitStack() as s, nc.Block() as block:
                scatter_records(c, block, s, e0)
                with ExitStack() as st:
                    rank_stage(c, block, st, e0, 1)
                with ExitStack() as st:
                    norm_stage(c, block, st, "0", 2, True)
                with ExitStack() as st:
                    mix0_stage(c, block, st, 3)
                with ExitStack() as st:
                    rank_stage(c, block, st, e1, 4)
                with ExitStack() as st:
                    rank_stage(c, block, st, eg, 5)
            c.clear_spent()
            with ExitStack() as s, nc.Block() as block:
                clear_slots0(c, block, s)
                load_slots(c, block, s, e0)
                sum0_stage(c, block, s, e0)
            c.clear_spent()
        if c.upto >= 2:
            with ExitStack() as l1:
                c.kept.append(l1)
                m = 5
                with ExitStack() as s, nc.Block() as block:
                    c.group_expert = c.sb(s, "group_expert", [1, GROUPS0], I32)
                    c.XN = c.sb(s, "normed_rows", [P, T, D])
                    c.slot_from = c.sb(s, "slot_from", [P, T, CHOSEN], I32)
                    c.slot_to = c.sb(s, "slot_to", [P, T, CHOSEN], I32)
                    c.gate_of = c.sb(s, "gate_of", [P, T, CHOSEN])
                    c.routed = c.sem(s, "routed")
                    c.sent_all = c.sem(s, "all_nodes_sent")
                    c.outputs_stored = c.sem(s, "slot_out_all_stored")
                    send_nodes0(c, block, s)
                    scatter_records(c, block, s, e1)
                    scatter_records(c, block, s, eg, 0, EARLY)
                    fetch_outputs0(c, block, s)
                    for stage in (lambda st, m: norm_stage(c, block, st, "1", m, False, c.XN),
                                  lambda st, m: router0_stage(c, block, st, m),
                                  lambda st, m: experts_stage(
                                      c, block, st, "0", m, FF0, [(a["w1s"], a["w2s"])],
                                      a["b1_0"][:, EXPERTS0 * FF0 // P:], a["b2_0"][EXPERTS0 * D:], None),
                                  lambda st, m: private_experts_stage(c, block, st, m)):
                        m += 1
                        with ExitStack() as st:
                            stage(st, m)
                c.clear_spent()
                if c.upto >= 3:
                    c.table1 = nc.dram_tensor("table1", [NP, 2 * MSG], F32, kind="Internal").ap()
                    with ExitStack() as s, nc.Block() as block:
                        scatter_records(c, block, s, eg, EARLY)
                        for stage in (lambda st, m: norm_stage(c, block, st, "2", m, False),
                                      lambda st, m: table1_stage(c, block, st, m),
                                      lambda st, m: mix1_stage(c, block, st, m)):
                            m += 1
                            with ExitStack() as st:
                                stage(st, m)
                    c.clear_spent()
                    records.close()
                    with ExitStack() as s:
                        c.msg = c.sb(s, "messages", [P, e1.tiles, MSG])
                        c.prob = c.sb(s, "edge_weight", [P, e1.tiles, HEADS1])
                        c.agg = c.XT[:].rearrange("p (t f) -> p t f", t=T)
                        with ExitStack() as s2:
                            e1.slot = c.sb(s, "slot_gnn1", [P, e1.tiles, 4])
                            with nc.Block() as block:
                                load_slots(c, block, s2, e1)
                                messages_stage(c, block, s2, e1)
                            c.clear_spent()
                        with ExitStack() as s2, nc.Block() as block:
                            m += 1
                            with ExitStack() as st:
                                softmax1_stage(c, block, st, e1, m)
                            c.softmax1_met = m
                            sum1_stage(c, block, s2, e1)
                        c.clear_spent()
                if c.upto >= 4:
                    c.table_g = nc.dram_tensor("table_g", [NP, ROW_G], F32, kind="Internal").ap()
                    c.tab = c.sb(l1, "tab_g", [P, T, ROW_G])
                    c.edge_tab = c.sb(l1, "edge_tab", [P, T, 2 * NE1])
                    c.high = c.sb(l1, "high", [P, T, NE1])
                    c.lift = c.sb(l1, "lift", [P, 1])
                    c.row_g = c.sb(l1, "row_g", [P, 3, HID_G])
                    c.row_g_in = c.sem(l1, "row_g_loaded")
                    c.score16 = c.sb(l1, "score16", [P, T, HID_G])
                    c.gates1 = c.sb(l1, "gates1", [P, T, NE1])
                    c.rows_g = c.sb(l1, "rows_g", [P, eg.tiles, ROW_G])
                    eg.slot = c.sb(l1, "slot_router", [P, eg.tiles, 4])
                    with nc.Block() as block:
                        for stage in (lambda st, m: norm_stage(c, block, st, "3", m, False),
                                      lambda st, m: table_g_stage(c, block, st, m)):
                            m += 1
                            with ExitStack() as st:
                                stage(st, m)
                    c.clear_spent()
                    with ExitStack() as s, nc.Block() as block:
                        load_slots(c, block, s, eg)
                        segment_max_stage(c, block, s, eg)
                    c.clear_spent()
                    with nc.Block() as block:
                        for stage in (lambda st, m: sum_g_stage(c, block, st, eg, m),
                                      lambda st, m: gates1_stage(c, block, st, m),
                                      lambda st, m: experts_stage(
                                          c, block, st, "1", m, 512,
                                          [(a["w1e"][i], a["w2e"][i]) for i in range(4)],
                                          a["b1_1"], a["b2_1"], c.gates1)):
                            m += 1
                            with ExitStack() as st:
                                stage(st, m)
                    c.clear_spent()
        stored = c.sem(top, "stored")
        with nc.Block() as block:
            @block.sync
            def _(sp):
                sp.dma_start(out[0:(T - 1) * P, :].rearrange("(t p) d -> p t d", p=P), c.X[:, 0:T - 1, :])\
                  .then_inc(stored, 16)
                sp.dma_start(out[(T - 1) * P:N, :], c.X[0:LAST, T - 1, :]).then_inc(stored, 16)
                sp.wait_ge(stored, 32)


def laid_out(x):
    import numpy as np
    n = {k: np.asarray(v) for k, v in x.items()}
    cols = lambda b: np.ascontiguousarray(b.reshape(-1, P).T)
    return {
        "x": n["x"], "src": n["src"], "dst": n["dst"], "edge_weight": n["edge_weight"],
        "gnn0_w": n["L0_gnn_weight"], "gnn0_b": n["L0_gnn_bias"], "qkv0_w": n["L0_mix_w_qkv"],
        "out0_w": n["L0_mix_w_out"], "b_out0": n["L0_mix_b_out"], "g_out0": n["L0_mix_g_out"],
        "g_pre0": cols(n["L0_mix_g_pre"]),
        "edge_attr_2": n["edge_attr_2"], "router0_w": n["L0_ffn_Wr"],
        "w1p": n["L0_ffn_W1p"], "w2p": n["L0_ffn_W2p"], "w1s": n["L0_ffn_W1s"], "w2s": n["L0_ffn_W2s"],
        "b1_0": cols(np.concatenate([n["L0_ffn_b1p"].reshape(-1), n["L0_ffn_b1s"]])),
        "b2_0": np.concatenate([n["L0_ffn_b2p"].reshape(-1), n["L0_ffn_b2s"]]),
        "wf": n["L1_gnn_W_forward"], "wr": n["L1_gnn_W_reverse"],
        "wf_t": np.ascontiguousarray(n["L1_gnn_W_forward"].T), "wr_t": np.ascontiguousarray(n["L1_gnn_W_reverse"].T),
        "att1_t": np.ascontiguousarray(n["L1_gnn_attn_forward"][0].T),
        "wkv1_t": np.ascontiguousarray(n["L1_mix_Wqkv"][INNER:].T), "wq1": n["L1_mix_Wqkv"][:INNER],
        "wout1_t": np.ascontiguousarray(n["L1_mix_Wout"].T), "bout1": n["L1_mix_bout"],
        "w_gat": n["L1_ffn_W_gat"], "att_src": n["L1_ffn_att_src"].reshape(-1),
        "att_dst": n["L1_ffn_att_dst"].reshape(-1), "b_gat": n["L1_ffn_b_gat"],
        "ln_gamma": n["L1_ffn_ln_gamma"], "ln_beta": n["L1_ffn_ln_beta"],
        "w1e": n["L1_ffn_W1"], "w2e": n["L1_ffn_W2"], "b1_1": cols(n["L1_ffn_b1"]), "b2_1": n["L1_ffn_b2"].reshape(-1),
        "router_src": np.ascontiguousarray(n["L1_ffn_edge_index"][0]),
        "router_dst": np.ascontiguousarray(n["L1_ffn_edge_index"][1]),
        "mem0": np.ascontiguousarray(n["L0_mix_mem_kv"].transpose(0, 3, 1, 2)).reshape(2, MEM, HID0),
    }


def kernel(**inputs):
    import numpy as np
    from concourse import bacc
    from concourse.bass_utils import run_bass_kernel_spmd

    nc = bacc.Bacc("TRN2", target_bir_lowering=False, num_devices=1)
    arrays = {f"in_{k}": v for k, v in laid_out(inputs).items()}
    aps = {k[3:]: nc.dram_tensor(k, v.shape, mybir.dt.from_np(v.dtype), kind="ExternalInput").ap()
           for k, v in arrays.items()}
    out = nc.dram_tensor("out", (N, D), F32, kind="ExternalOutput").ap()
    build(nc, aps, out)
    return run_bass_kernel_spmd(nc, [arrays], core_ids=[0]).results[0]["out"]
```
